# Optimizing a Trainium2 kernel written in Bass

```python
import numpy as np
import jax
import jax.numpy as jnp

def _softmax(x, axis=-1):
    return jax.nn.softmax(x, axis=axis)

def _gelu(x):
    return jax.nn.gelu(x, approximate=True)

def _silu(x):
    return jax.nn.silu(x)

def _sigmoid(x):
    return jax.nn.sigmoid(x)

def _layernorm(x, axis=-1, eps=1e-05):
    m = jnp.mean(x, axis=axis, keepdims=True)
    v = jnp.var(x, axis=axis, keepdims=True)
    return (x - m) / jnp.sqrt(v + eps)

def _scatter_add(tgt, idx, src, axis=0):
    return tgt.at[idx].add(src)

def _segment_sum(src, seg, n):
    return jax.ops.segment_sum(src, seg, n)
kernel_name = 'mk_seq_postln_d1_jaxref_r8_d1e1ea'

def setup_inputs(seed: int=0):
    np.random.seed(seed)
    _w = jnp.asarray

    def _L0_attn_setup():
        import jax, jax.numpy as jnp
        import numpy as np
        B, T, C = (2, 256, 256)
        NH = 16
        G = 4
        NKV = NH // G
        HD = C // NH
        BASE = 10000.0

        def _rope(x):
            b, h, t, d = x.shape
            half = d // 2
            theta = 1.0 / BASE ** (jnp.arange(0, half, dtype=jnp.float32) * 2.0 / d)
            ang = jnp.arange(h, dtype=jnp.float32)[:, None] * theta[None, :]
            cos = jnp.cos(ang)[None, :, None, :]
            sin = jnp.sin(ang)[None, :, None, :]
            xs = x.reshape(b, h, t, half, 2)
            x0, x1 = (xs[..., 0], xs[..., 1])
            out = jnp.stack([x0 * cos - x1 * sin, x1 * cos + x0 * sin], axis=-1)
            return out.reshape(b, h, t, d)
        key = jax.random.key(seed)
        ks = jax.random.split(key, 9)
        s = 0.02
        return {'x': jax.random.normal(ks[0], (B, T, C), jnp.float32), 'wq_w': jax.random.normal(ks[1], (C, C), jnp.float32) * s, 'wq_b': jax.random.normal(ks[2], (C,), jnp.float32) * s, 'wk_w': jax.random.normal(ks[3], (C // G, C), jnp.float32) * s, 'wk_b': jax.random.normal(ks[4], (C // G,), jnp.float32) * s, 'wv_w': jax.random.normal(ks[5], (C // G, C), jnp.float32) * s, 'wv_b': jax.random.normal(ks[6], (C // G,), jnp.float32) * s, 'cp_w': jax.random.normal(ks[7], (C, C), jnp.float32) * s, 'cp_b': jax.random.normal(ks[8], (C,), jnp.float32) * s}
    _L0_attn_in = _L0_attn_setup()

    def _L0_ffn_setup():
        import jax, jax.numpy as jnp
        import numpy as np
        TOP_K = 4
        key = jax.random.key(seed)
        ks = jax.random.split(key, 9)
        B, T, D, H, NE = (2, 128, 256, 176, 16)
        s = 0.02
        return {'x': jax.random.normal(ks[0], (B, T, D), jnp.float32), 'gate_w': jax.random.normal(ks[1], (NE, D), jnp.float32) * s, 'gate_b': jax.random.normal(ks[2], (NE,), jnp.float32) * s, 'w1_shared': jax.random.normal(ks[3], (D, H), jnp.float32) * s, 'w2_shared': jax.random.normal(ks[4], (H, D), jnp.float32) * s, 'w3_shared': jax.random.normal(ks[5], (D, H), jnp.float32) * s, 'w1_routed': jax.random.normal(ks[6], (NE, D, H), jnp.float32) * s, 'w2_routed': jax.random.normal(ks[7], (NE, H, D), jnp.float32) * s, 'w3_routed': jax.random.normal(ks[8], (NE, D, H), jnp.float32) * s}
    _L0_ffn_in = _L0_ffn_setup()
    _d = {'L0_attn_x': _L0_attn_in['x'], 'L0_attn_wq_w': _L0_attn_in['wq_w'], 'L0_attn_wq_b': _L0_attn_in['wq_b'], 'L0_attn_wk_w': _L0_attn_in['wk_w'], 'L0_attn_wk_b': _L0_attn_in['wk_b'], 'L0_attn_wv_w': _L0_attn_in['wv_w'], 'L0_attn_wv_b': _L0_attn_in['wv_b'], 'L0_attn_cp_w': _L0_attn_in['cp_w'], 'L0_attn_cp_b': _L0_attn_in['cp_b'], 'L0_ffn_gate_w': _L0_ffn_in['gate_w'], 'L0_ffn_gate_b': _L0_ffn_in['gate_b'], 'L0_ffn_w1_shared': _L0_ffn_in['w1_shared'], 'L0_ffn_w2_shared': _L0_ffn_in['w2_shared'], 'L0_ffn_w3_shared': _L0_ffn_in['w3_shared'], 'L0_ffn_w1_routed': _L0_ffn_in['w1_routed'], 'L0_ffn_w2_routed': _L0_ffn_in['w2_routed'], 'L0_ffn_w3_routed': _L0_ffn_in['w3_routed']}
    _x0 = _d['L0_attn_x']
    _d['L0_attn_x'] = jax.random.normal(jax.random.fold_in(jax.random.key(seed), 1), (2, 1024, 256), dtype=_x0.dtype)
    del _x0
    return _d

def reference(L0_attn_x, L0_attn_wq_w, L0_attn_wq_b, L0_attn_wk_w, L0_attn_wk_b, L0_attn_wv_w, L0_attn_wv_b, L0_attn_cp_w, L0_attn_cp_b, L0_ffn_gate_w, L0_ffn_gate_b, L0_ffn_w1_shared, L0_ffn_w2_shared, L0_ffn_w3_shared, L0_ffn_w1_routed, L0_ffn_w2_routed, L0_ffn_w3_routed):

    def _L0_attn_ref(x, wq_w, wq_b, wk_w, wk_b, wv_w, wv_b, cp_w, cp_b):
        import jax, jax.numpy as jnp
        import numpy as np
        B, T, C = (2, 256, 256)
        NH = 16
        G = 4
        NKV = NH // G
        HD = C // NH
        BASE = 10000.0

        def _rope(x):
            b, h, t, d = x.shape
            half = d // 2
            theta = 1.0 / BASE ** (jnp.arange(0, half, dtype=jnp.float32) * 2.0 / d)
            ang = jnp.arange(h, dtype=jnp.float32)[:, None] * theta[None, :]
            cos = jnp.cos(ang)[None, :, None, :]
            sin = jnp.sin(ang)[None, :, None, :]
            xs = x.reshape(b, h, t, half, 2)
            x0, x1 = (xs[..., 0], xs[..., 1])
            out = jnp.stack([x0 * cos - x1 * sin, x1 * cos + x0 * sin], axis=-1)
            return out.reshape(b, h, t, d)
        b, t, c = x.shape
        q = x @ wq_w.T + wq_b
        k = x @ wk_w.T + wk_b
        v = x @ wv_w.T + wv_b
        q = q.reshape(b, t, NH, HD).transpose(0, 2, 1, 3)
        k = k.reshape(b, t, NKV, HD).transpose(0, 2, 1, 3)
        v = v.reshape(b, t, NKV, HD).transpose(0, 2, 1, 3)
        q = _rope(q)
        k = _rope(k)
        k = jnp.repeat(k, G, axis=1)
        v = jnp.repeat(v, G, axis=1)
        att = jnp.einsum('bhqd,bhkd->bhqk', q, k) / HD ** 0.5
        mask = jnp.tril(jnp.ones((t, t), dtype=bool))
        att = jnp.where(mask[None, None], att, -jnp.inf)
        att = jax.nn.softmax(att, axis=-1)
        y = jnp.einsum('bhqk,bhkd->bhqd', att, v)
        y = y.transpose(0, 2, 1, 3).reshape(b, t, c)
        return y @ cp_w.T + cp_b

    def _L0_ffn_ref(x, gate_w, gate_b, w1_shared, w2_shared, w3_shared, w1_routed, w2_routed, w3_routed):
        import jax, jax.numpy as jnp
        import numpy as np
        TOP_K = 4
        n_experts = w1_routed.shape[0]
        logits = jnp.einsum('ed,btd->bte', gate_w, x)
        scores = jax.nn.sigmoid(logits) + gate_b
        weights, indices = jax.lax.top_k(scores, TOP_K)
        weights = weights / weights.sum(-1, keepdims=True)
        shared_out = jax.nn.silu(x @ w1_shared) * (x @ w3_shared) @ w2_shared
        one_hot = jax.nn.one_hot(indices, n_experts, dtype=x.dtype)
        router_probs = (weights[..., None] * one_hot).sum(-2)
        h1 = jnp.einsum('btd,edc->btec', x, w1_routed)
        h2 = jnp.einsum('btd,edc->btec', x, w3_routed)
        h3 = jax.nn.silu(h1 * h2)
        experts_out = jnp.einsum('btec,ecd->bted', h3, w2_routed)
        routed_out = jnp.einsum('bted,bte->btd', experts_out, router_probs)
        return shared_out + routed_out
    x = L0_attn_x
    x = _layernorm(x + _L0_attn_ref(x, L0_attn_wq_w, L0_attn_wq_b, L0_attn_wk_w, L0_attn_wk_b, L0_attn_wv_w, L0_attn_wv_b, L0_attn_cp_w, L0_attn_cp_b), axis=-1)
    x = _layernorm(x + _L0_ffn_ref(x, L0_ffn_gate_w, L0_ffn_gate_b, L0_ffn_w1_shared, L0_ffn_w2_shared, L0_ffn_w3_shared, L0_ffn_w1_routed, L0_ffn_w2_routed, L0_ffn_w3_routed), axis=-1)
    return x

_drawn_inputs = setup_inputs


def setup_inputs(seed=0):
    import zlib

    import numpy as np

    out = dict(_drawn_inputs(seed))
    spreads = {}
    factors = {'L0_attn_wq_w': 8.0,
     'L0_attn_wq_b': 8.0,
     'L0_attn_wk_w': 8.0,
     'L0_attn_wk_b': 8.0,
     'L0_attn_wv_w': 6.62,
     'L0_attn_wv_b': 7.534,
     'L0_attn_cp_w': 5.026,
     'L0_attn_cp_b': 2.935,
     'L0_ffn_gate_w': 8.0,
     'L0_ffn_gate_b': 8.0,
     'L0_ffn_w1_shared': 4.098,
     'L0_ffn_w2_shared': 4.049,
     'L0_ffn_w3_shared': 4.041,
     'L0_ffn_w1_routed': 8.0,
     'L0_ffn_w2_routed': 8.0,
     'L0_ffn_w3_routed': 8.0}
    for name, (base, spread) in spreads.items():
        noise = np.random.default_rng([zlib.crc32(name.encode()), seed]).standard_normal(out[name].shape)
        drawn = base * np.exp(spread * noise) if base else spread * noise
        out[name] = jnp.asarray(drawn.astype(out[name].dtype))
    for name, factor in factors.items():
        out[name] = (out[name] * factor).astype(out[name].dtype)
    return out
```

```python
from contextlib import ExitStack

import concourse.bass as bass
import numpy as np
from concourse import mybir

F32 = mybir.dt.float32
F32R = mybir.dt.float32r
BF16 = mybir.dt.bfloat16
U16 = mybir.dt.uint16
U32 = mybir.dt.uint32
ALU = mybir.AluOpType
ACT = mybir.ActivationFunctionType
AX_X = mybir.AxisListType.X

P = 128
B, T, C = 2, 1024, 256
NH, G = 16, 4
NKV = NH // G
HD = C // NH
KVW = NKV * HD
KC = C // P
TT = T // P
HALF = 512
NHALF = T // HALF
NE, HID, TOPK = 16, 176, 4
HALL = (NE + 1) * HID
NCH = -(-HALL // P)
NCR = NE * HID // P
LAST = HALL - (NCH - 1) * P
EPS = 1e-5
NEG = -1e30
ROWS = 3 * HD
QROWS = ROWS + 2
GROUPS = B * T // HALF
NSL = 3
DLAG = 2
PROBROWS = 3 * NE


def at(loop, per, n):
    return loop * per + n


def max_units():
    units = [(0, (0, 1, 2, 3), P, P), (1, (0, 1, 2, 3), 2 * P, 2 * P)]
    for i in (2, 3):
        units += [(i, (0, 1), (i + 1) * P, HALF), (i, (2, 3), (i + 1) * P, HALF)]
    for i in range(4, TT):
        units += [(i, (h,), (i + 1) * P, 2 * HALF) for h in range(G)]
    return units


def exp_steps():
    return [(q, j, max(0, P * j - HALF * q), j >= 4 * q) for q in range(NHALF) for j in range(4 * (q + 1))]


UNITS = max_units()
STEPS = exp_steps()
NU, NST = len(UNITS), len(STEPS)
DIAGS = sum(s[3] for s in STEPS)


def spread():
    cost = [HALF - s[2] for s in STEPS]
    whole, out, done, run = 0.87 * sum(cost), [], 0, 0
    for c in cost:
        run += c
        due = min(NU + 1, -(-int((NU + 1) * run) // int(whole)))
        out.append(due - done)
        done = due
    assert done == NU + 1
    return out


SPREAD = spread()
PROLOG = 4
S_PER = PROLOG + NKV * (NU + 1) + 3 * TT
T_PER = 4 + NKV * NST * G + 2 * TT + 1
T_OF, S_OF = {}, {}
for _s in range(TT + 5):
    for _d, _ring, _lag, _name in ((T_OF, "T", 1, "y"), (T_OF, "T", 4, "x1"), (S_OF, "S", 0, "norm"),
                                   (S_OF, "S", 2, "proj"), (S_OF, "S", 5, "gate")):
        if 0 <= _s - _lag < TT:
            _start = 4 + NKV * NST * G if _ring == "T" else PROLOG + NKV * (NU + 1)
            _d[(_name, _s - _lag)] = _start + len(_d)
t_of, s_of = T_OF, S_OF
assert S_PER % 2 == 0 and T_PER % 3 == 0


def attention_moe(nc, x, wq_w, wq_b, wk_w, wk_b, wv_w, wv_b, cp_w, cp_b, gate_w, gate_b,
                  w1_shared, w2_shared, w3_shared, w1_routed, w2_routed, w3_routed,
                  rot_q, rot_k, expert_of, iota_e, out):
    x1_dram = nc.dram_tensor("x1_scratch", (C, B * T), F32, kind="Internal").ap()
    prob_dram = nc.dram_tensor("prob_scratch", (PROBROWS, B * T), BF16, kind="Internal").ap()

    ctx = ExitStack()
    with ctx:
        def sem(name):
            return ctx.enter_context(nc.semaphore(name))

        def sb(name, shape, dt=F32, stack=ctx):
            return stack.enter_context(nc.sbuf_tensor(name, shape, dt))

        def pb(name, shape, dt=F32, stack=ctx):
            return stack.enter_context(nc.psum_tensor(name, shape, dt))

        ident = sb("ident", [P, P])
        ident_b = sb("ident_b", [P, P], BF16)
        eps_pow = sb("eps_pow", [P, 1])

        att = ExitStack()
        mask_b = sb("mask_b", [P, P], BF16, att)
        wq_n = sb("wq_n", [P, KC, C], F32, att)
        wk_n = sb("wk_n", [KVW, C], F32, att)
        wv_n = sb("wv_n", [KVW, C], F32, att)
        cp_n = sb("cp_n", [P, KC, C], F32, att)
        gw_n = sb("gw_n", [NE, C], F32, att)
        rq = sb("rq", [P, KC, P], F32, att)
        rk = sb("rk", [KVW, KVW], F32, att)
        bq_n = sb("bq_n", [P, KC], F32, att)
        bk_n = sb("bk_n", [KVW, 1], F32, att)
        bv_b = sb("bv_b", [P, KVW], F32, att)
        cpb_b = sb("cpb_b", [P, C], F32, att)
        gb_b = sb("gb_b", [P, NE], F32, att)
        iota_b = sb("iota_b", [P, NE], F32, att)
        wqT = sb("wqT", [P, KC, C], F32, att)
        wkT = sb("wkT", [P, KC, KVW], F32, att)
        wvT = sb("wvT", [P, KC, KVW], F32, att)
        cpT = sb("cpT", [P, KC, C], F32, att)
        gwT = sb("gwT", [P, KC, NE], F32, att)
        bq = sb("bq", [P, KC], F32, att)
        bk = sb("bk", [KVW, 1], F32, att)
        xn = sb("xn", [P, TT, C], F32, att)
        xT = sb("xT", [P, KC, T], F32, att)
        qh = sb("qh", [P, KC, T], F32R, att)
        ql = sb("ql", [P, KC, T], F32R, att)
        kh = sb("kh", [KVW, T], F32R, att)
        kl = sb("kl", [KVW, T], F32R, att)
        QS = sb("QS", [QROWS, NH, T], F32R, att)
        KS = sb("KS", [QROWS, NKV, T], F32R, att)
        V = sb("V", [P, TT, NKV, 2 * HD], F32, att)
        prob = sb("prob", [P, 2, G, HALF], F32, att)
        MX = sb("MX", [P, G, TT], F32, att)
        M2 = sb("M2", [P, 2, G * TT], F32R, att)
        MT = sb("MT", [2 * G * TT, P], F32, att)
        O = sb("O", [P, NKV, T], F32, att)
        rc = sb("rc", [P, 2, NH], F32, att)
        y = sb("y", [P, 2, C], F32, att)
        yT = sb("yT", [P, 2, KC, P], F32, att)
        r = sb("r", [P, 2, C], F32, att)
        st1 = sb("st1", [P, 2, 6], F32, att)
        mv1 = sb("mv1", [P, 2, 2], F32, att)
        ve1 = sb("ve1", [P, 2, 1], F32, att)
        rs1 = sb("rs1", [P, 2, 1], F32, att)
        x1 = sb("x1", [P, 2, C], F32, att)
        x1Tb = sb("x1Tb", [P, KC, T], F32, att)
        lg = sb("lg", [P, TT, NE], F32, att)
        th = sb("th", [P, TT, NE], F32, att)
        sc = sb("sc", [P, TT, NE], F32, att)
        top = sb("top", [P, TT, 8], F32, att)
        idx = sb("idx", [P, TT, 8], U32, att)
        idf = sb("idf", [P, TT, 8], F32, att)
        hit = sb("hit", [P, TT, NE, TOPK], F32, att)
        pick = sb("pick", [P, TT, NE], F32, att)
        tsum = sb("tsum", [P, TT, 1], F32, att)
        trec = sb("trec", [P, TT, 1], F32, att)
        prt = sb("prt", [P, TT, NE], F32, att)
        pr3 = sb("pr3", [P, TT, PROBROWS], BF16, att)
        pT = sb("pT", [PROBROWS, T], BF16, att)
        psS = pb("psS", [P, 2, 2 * HALF], F32, att)
        psT = pb("psT", [P, 3, HALF], F32, att)
        psO = pb("psO", [P, HALF], F32, att)
        att.close()

        ffn = ExitStack()
        sel = sb("sel", [PROBROWS, NCR, P], BF16, ffn)
        w1h = sb("w1h", [P, KC, HALL], F32R, ffn)
        w1l = sb("w1l", [P, KC, HALL], F32R, ffn)
        w3h = sb("w3h", [P, KC, HALL], F32R, ffn)
        w3l = sb("w3l", [P, KC, HALL], F32R, ffn)
        w2h = sb("w2h", [P, NCH, C], F32R, ffn)
        w2l = sb("w2l", [P, NCH, C], F32R, ffn)
        x1f = sb("x1f", [P, 2, KC, HALF], F32, ffn)
        xh = sb("xh", [P, 2, KC, HALF], F32R, ffn)
        xl = sb("xl", [P, 2, KC, HALF], F32R, ffn)
        pg = sb("pg", [PROBROWS, 2, HALF], BF16, ffn)
        za = sb("za", [P, 2 * NSL, HALF], F32, ffn)
        gh = sb("gh", [P, NSL, HALF], F32R, ffn)
        gl = sb("gl", [P, NSL, HALF], F32R, ffn)
        yo = sb("yo", [P, 2, C], F32, ffn)
        st2 = sb("st2", [P, 2, 6], F32, ffn)
        mv2 = sb("mv2", [P, 2, 2], F32, ffn)
        ve2 = sb("ve2", [P, 2, 1], F32, ffn)
        rs2 = sb("rs2", [P, 2, 1], F32, ffn)
        psH = pb("psH", [P, 2, 2, HALF], F32, ffn)
        psB = pb("psB", [P, 2, HALF], F32, ffn)
        psY = pb("psY", [P, KC, HALF], F32, ffn)
        ffn.close()

        s_wload = sem("s_wload")
        s_const = sem("s_const")
        s_wt = sem("s_wt")
        s_wtc = sem("s_wtc")
        s_x = sem("s_x")
        s_m2 = sem("s_m2")
        s_S = sem("s_S")
        s_Sfree = sem("s_Sfree")
        s_T = sem("s_T")
        s_Tfree = sem("s_Tfree")
        s_stack = sem("s_stack")
        s_mrow = sem("s_mrow")
        s_res = sem("s_res")
        s_sel = sem("s_sel")
        s_pfree = sem("s_pfree")
        s_O = sem("s_O")
        s_Ofree = sem("s_Ofree")
        s_var = sem("s_var")
        s_rstd = sem("s_rstd")
        s_x1 = sem("s_x1")
        s_th = sem("s_th")
        s_pr3 = sem("s_pr3")
        s_x1st = sem("s_x1st")
        s_pst = sem("s_pst")
        s_attdone = sem("s_attdone")
        s_dve = sem("s_dve")
        s_stage = [sem(f"s_stage{i}") for i in range(2 * NSL)]
        s_hi = sem("s_hi")
        s_lo = sem("s_lo")
        s_selw = sem("s_selw")
        s_x1f = [sem(f"s_x1f{i}") for i in range(2)]
        s_x1free = sem("s_x1free")
        s_xh = sem("s_xh")
        s_xl = sem("s_xl")
        s_h = sem("s_h")
        s_b = sem("s_b")
        s_ln = sem("s_ln")
        s_copy = sem("s_copy")
        s_z = sem("s_z")
        s_tanh = sem("s_tanh")
        s_w = sem("s_w")
        s_g = sem("s_g")
        s_gh = sem("s_gh")
        s_gl = sem("s_gl")
        s_gfree = sem("s_gfree")
        s_yfree = sem("s_yfree")
        s_var2 = sem("s_var2")
        s_rstd2 = sem("s_rstd2")
        s_yo = sem("s_yo")
        s_out = [sem(f"s_out{i}") for i in range(2)]
        s_gate = sem("s_gate")

        block = ctx.enter_context(nc.Block())

        WLOADS = 15
        pieces = []
        for hi, lo, rt, shd in ((w1h, w1l, w1_routed, w1_shared), (w3h, w3l, w3_routed, w3_shared)):
            for k in range(KC):
                for e0 in range(0, NE, 2):
                    pieces.append((hi[:, k, e0 * HID:(e0 + 2) * HID], lo[:, k, e0 * HID:(e0 + 2) * HID],
                                   rt[e0:e0 + 2, k * P:(k + 1) * P, :].rearrange("e p h -> p e h"), P, 2, HID))
                pieces.append((hi[:, k, NE * HID:HALL], lo[:, k, NE * HID:HALL], shd[k * P:(k + 1) * P, :]
                               .rearrange("p (a h) -> p a h", a=1), P, 1, HID))
        w2_flat = w2_routed.rearrange("e h d -> (e h) d")
        for c0 in range(0, NCR, 2):
            pieces.append((w2h[:, c0:c0 + 2, :], w2l[:, c0:c0 + 2, :],
                           w2_flat[c0 * P:(c0 + 2) * P, :].rearrange("(q p) d -> p q d", p=P), P, 2, C))
        pieces.append((w2h[:, NCR, :], w2l[:, NCR, :], w2_shared[0:P, :].rearrange("p (a d) -> p a d", a=1), P, 1, C))
        pieces.append((w2h[0:LAST, NCH - 1, :], w2l[0:LAST, NCH - 1, :],
                       w2_shared[P:HID, :].rearrange("p (a d) -> p a d", a=1), LAST, 1, C))
        NPC = len(pieces)
        NSTG = 2 * NSL

        def stage(n):
            _, _, _, rows, a, w = pieces[n]
            return za[0:rows, n % NSTG, 0:a * w]

        @block.sync
        def _(sp):
            sp.dma_start(wq_n[:, :, :], wq_w.rearrange("(m p) c -> p m c", p=P)).then_inc(s_wload, 16)
            sp.dma_start(rq[:, :, :], rot_q.rearrange("(m p) c -> p m c", p=P)).then_inc(s_wload, 16)
            sp.dma_start(wk_n[:, :], wk_w).then_inc(s_wload, 16)
            sp.dma_start(rk[:, :], rot_k).then_inc(s_wload, 16)
            sp.dma_start(wv_n[:, :], wv_w).then_inc(s_wload, 16)
            sp.dma_start(cp_n[:, :, :], cp_w.rearrange("(m p) c -> p m c", p=P)).then_inc(s_wload, 16)
            sp.dma_start(gw_n[:, :], gate_w).then_inc(s_wload, 16)
            for m in range(KC):
                sp.dma_start(bq_n[:, m:m + 1], wq_b[m * P:(m + 1) * P].rearrange("(p a) -> p a", a=1)).then_inc(s_wload, 16)
            sp.dma_start(bk_n[:, :], wk_b.rearrange("(p a) -> p a", a=1)).then_inc(s_wload, 16)
            sp.dma_start(bv_b[:, :], wv_b.partition_broadcast(P)).then_inc(s_wload, 16)
            sp.dma_start(cpb_b[:, :], cp_b.partition_broadcast(P)).then_inc(s_wload, 16)
            sp.dma_start(gb_b[:, :], gate_b.partition_broadcast(P)).then_inc(s_wload, 16)
            sp.dma_start(iota_b[:, :], iota_e.partition_broadcast(P)).then_inc(s_wload, 16)
            for i in range(2):
                sp.sem_inc(s_out[i], 16)
            sp.sem_inc(s_x1st, 16)
            sp.sem_inc(s_pst, 16)
            with sp.Fori(0, B) as b:
                sp.wait_ge(s_Sfree, at(b, S_PER, 2))
                sp.sem_inc(s_gate, 1)
                sp.dma_start(xn[:, :, :], x[bass.ds(b * T, T), :].rearrange("(i p) c -> p i c", p=P)).then_inc(s_x, 16)
                sp.wait_ge(s_Sfree, at(b, S_PER, 3))
                for src, row in ((kh, 0), (kl, 1), (kh, 2)):
                    sp.dma_start(KS[row * HD:(row + 1) * HD, :, :].bitcast(F32), src[:, :].bitcast(F32)).then_inc(s_stack, 16)
                for m in range(KC):
                    sp.wait_ge(s_Sfree, at(b, S_PER, 4 + m))
                    for src, row in ((qh, 0), (qh, 1), (ql, 2)):
                        sp.dma_start(QS[row * HD:(row + 1) * HD, m * 8:(m + 1) * 8, :].bitcast(F32),
                                     src[:, m, :].bitcast(F32)).then_inc(s_stack, 16)
                for g in range(NKV):
                    sp.wait_ge(s_Sfree, at(b, S_PER, 2 + PROLOG + (g + 1) * (NU + 1)))
                    for s in range(2):
                        sp.dma_start(QS[ROWS + s:ROWS + s + 1, g * G:(g + 1) * G, :].bitcast(F32)
                                     .rearrange("p h (i t) -> p (h i) t", t=P),
                                     MT[s * G * TT:(s + 1) * G * TT, :]).then_inc(s_mrow, 16)
                sp.wait_ge(s_Tfree, at(b, T_PER, 3 + T_PER))
                sp.sem_inc(s_gate, 1)
                sp.dma_start(x1_dram[:, bass.ds(b * T, T)].rearrange("(k p) t -> p k t", p=P), x1Tb[:, :, :]).then_inc(s_x1st, 16)
                sp.dma_start(prob_dram[:, bass.ds(b * T, T)], pT[:, :]).then_inc(s_pst, 16)
            sp.wait_ge(s_x1st, 16 * (B + 1))
            sp.wait_ge(s_pst, 16 * (B + 1))
            sp.sem_inc(s_attdone, 1)

            sp.wait_ge(s_attdone, 5)
            sp.dma_start(sel[:, :, :].bitcast(U16), expert_of.rearrange("k (q p) -> k q p", p=P)).then_inc(s_selw, 16)
            for n in range(NPC):
                _, _, src, rows, a, w = pieces[n]
                if n >= NSTG:
                    sp.wait_ge(s_lo, n - NSTG + 1)
                sp.dma_start(stage(n).rearrange("p (a w) -> p a w", a=a), src).then_inc(s_stage[n % NSTG], 16)
            with sp.Fori(0, GROUPS // 2) as gg:
                for par in range(2):
                    sp.wait_ge(s_x1free, at(gg, 2, par + 1))
                    sp.sem_inc(s_gate, 1)
                    tok = bass.ds(gg * (2 * HALF) + par * HALF, HALF)
                    sp.dma_start(x1f[:, par, :, :], x1_dram[:, tok].rearrange("(k p) t -> p k t", p=P)).then_inc(s_x1f[par], 16)
                    sp.dma_start(pg[:, par, :], prob_dram[:, tok]).then_inc(s_x1f[par], 16)
                for par in range(2):
                    for i in range(4):
                        sp.wait_ge(s_yo, at(gg, 8, 4 + par * 4 + i + 1))
                        sp.sem_inc(s_gate, 1)
                        sp.dma_start(out[bass.ds(gg * (2 * HALF) + (par * 4 + i) * P, P), :], yo[:, i % 2, :]).then_inc(s_out[i % 2], 16)
            for i in range(2):
                sp.wait_ge(s_out[i], 16 * (2 * GROUPS + 1))

        @block.gpsimd
        def _(pool):
            nc.gpsimd.memset(ident[:, :], 0.0).then_inc(s_const, 1)
            nc.gpsimd.memset(ident_b[:, :], 0.0).then_inc(s_const, 1)
            nc.gpsimd.memset(mask_b[:, :], 0.0).then_inc(s_const, 1)
            nc.gpsimd.memset(eps_pow[:, :], -0.5).then_inc(s_const, 1)
            nc.gpsimd.memset(KS[:, :, :].bitcast(F32), 1.0).then_inc(s_const, 1)
            nc.gpsimd.memset(V[:, :, :, :], 1.0).then_inc(s_const, 1)
            pool.wait_ge(s_const, 6)
            for m in (ident, ident_b):
                nc.gpsimd.affine_select(out=m[:, :], in_=m[:, :], compare_op=ALU.not_equal, fill=1.0, base=0,
                                        pattern=[[-1, P]], channel_multiplier=1).then_inc(s_const, 1)
            nc.gpsimd.affine_select(out=mask_b[:, :], in_=mask_b[:, :], compare_op=ALU.is_ge, fill=NEG, base=0,
                                    pattern=[[-1, P]], channel_multiplier=1).then_inc(s_const, 1)
            pool.wait_ge(s_wload, 16 * (WLOADS - 1))
            with pool.Fori(0, B) as b:
                pool.wait_ge(s_T, at(b, T_PER, 4))
                pool.sem_inc(s_gate, 1)
                nc.gpsimd.tensor_tensor(xn[:, :, :], xn[:, :, :], cpb_b[:, :].unsqueeze(1).to_broadcast([P, TT, C]),
                                        ALU.add).then_inc(s_res, 1)
                for g in range(NKV):
                    nd = 0
                    for n, (q, j, c0, diag) in enumerate(STEPS):
                        if not diag:
                            continue
                        pool.wait_ge(s_Tfree, at(b, T_PER, 3 + 4 + (g * NST + n + 1) * G))
                        pool.sem_inc(s_gate, 1)
                        blk = prob[:, (g * NST + n) % 2, :, 0:P]
                        nc.gpsimd.affine_select(out=blk, in_=blk, compare_op=ALU.is_ge, fill=0.0, base=0,
                                                pattern=[[0, G], [1, P]], channel_multiplier=-1).then_inc(s_sel, 1)
                        nd += 1
                for i in range(TT):
                    pool.wait_ge(s_var, at(b, TT, i + 1))
                    nc.gpsimd.tensor_tensor(rs1[:, i % 2, :], ve1[:, i % 2, :], eps_pow[:, :], ALU.pow).then_inc(s_rstd, 1)
            pool.drain().then_inc(s_attdone, 1)

            pool.sem_inc(s_gl, NSL)
            with pool.Fori(0, GROUPS // 2) as gg:
                for par in range(2):
                    for q in range(NCH):
                        rows = LAST if q == NCH - 1 else P
                        n = par * NCH + q
                        pool.wait_ge(s_gh, at(gg, 2 * NCH, n + 1))
                        nc.gpsimd.tensor_tensor(gl[0:rows, q % NSL, :], za[0:rows, 2 * (q % NSL), :],
                                                gh[0:rows, q % NSL, :].bitcast(F32), ALU.subtract).then_inc(s_gl, 1)
                    for i in range(4):
                        pool.wait_ge(s_var2, at(gg, 8, par * 4 + i + 1))
                        nc.gpsimd.tensor_tensor(rs2[:, i % 2, :], ve2[:, i % 2, :], eps_pow[:, :], ALU.pow).then_inc(s_rstd2, 1)

        @block.scalar
        def _(act):
            act.sem_inc(s_Tfree, 3)
            act.sem_inc(s_Ofree, 1)
            act.wait_ge(s_wt, 1)
            nc.scalar.copy(wqT[:, :, :], psT[:, 0, :].rearrange("p (k o) -> p k o", k=KC)).then_inc(s_wtc, 1)
            nc.scalar.copy(cpT[:, :, :], psT[:, 1, :].rearrange("p (k o) -> p k o", k=KC)).then_inc(s_wtc, 1)
            kv = psT[:, 2, 0:2 * KC * KVW].rearrange("p (w k o) -> p w k o", w=2, k=KC)
            nc.scalar.copy(wkT[:, :, :], kv[:, 0, :, :]).then_inc(s_wtc, 1)
            nc.scalar.copy(wvT[:, :, :], kv[:, 1, :, :]).then_inc(s_wtc, 1)
            o = 2 * KC * KVW
            nc.scalar.copy(gwT[:, :, :], psT[:, 2, o:o + KC * NE].rearrange("p (k o) -> p k o", k=KC)).then_inc(s_wtc, 1)
            nc.scalar.copy(bq[:, :], psT[:, 2, o + 32:o + 34]).then_inc(s_wtc, 1)
            nc.scalar.copy(bk[:, :], psT[0:KVW, 2, o + 34:o + 35]).then_inc(s_wtc, 1)
            with act.Fori(0, B) as b:
                t = 0
                for u in range(4):
                    act.wait_ge(s_T, at(b, T_PER, t + 1))
                    nc.scalar.copy(xT[:, u // 2, (u % 2) * HALF:(u % 2 + 1) * HALF], psT[:, t % 3, :]).then_inc(s_Tfree, 1)
                    t += 1
                done = None
                for g in range(NKV):
                    for n, (q, j, c0, diag) in enumerate(STEPS):
                        step = g * NST + n
                        act.wait_ge(s_pfree, at(b, NKV * NST, step + 1))
                        for h in range(G):
                            act.wait_ge(s_T, at(b, T_PER, t + 1))
                            nc.scalar.activation(prob[:, step % 2, h, 0:HALF - c0], psT[:, t % 3, 0:HALF - c0],
                                                 ACT.Exp).then_inc(s_Tfree, 1)
                            t += 1
                        if done is not None:
                            dg, dq, cnt = done
                            act.wait_ge(s_O, at(b, NKV * NHALF, cnt + 1))
                            nc.scalar.copy(O[:, dg, dq * HALF:(dq + 1) * HALF], psO[:, :]).then_inc(s_Ofree, 1)
                            done = None
                        if j == 4 * (q + 1) - 1:
                            done = (g, q, g * NHALF + q)
                dg, dq, cnt = done
                act.wait_ge(s_O, at(b, NKV * NHALF, cnt + 1))
                nc.scalar.copy(O[:, dg, dq * HALF:(dq + 1) * HALF], psO[:, :]).then_inc(s_Ofree, 1)
                act.wait_ge(s_x1st, at(b, 16, 16))
                act.wait_ge(s_pst, at(b, 16, 16))
                for s in range(TT + 5):
                    if 0 <= s - 1 < TT:
                        i = s - 1
                        act.wait_ge(s_T, at(b, T_PER, t + 1))
                        nc.scalar.copy(yT[:, i % 2, :, :], psT[:, t % 3, 0:C].rearrange("p (k t) -> p k t", k=KC)).then_inc(s_Tfree, 1)
                        t += 1
                    if 0 <= s - 4 < TT:
                        i = s - 4
                        act.wait_ge(s_T, at(b, T_PER, t + 1))
                        nc.scalar.copy(x1Tb[:, :, i * P:(i + 1) * P], psT[:, t % 3, 0:C].rearrange("p (k t) -> p k t", k=KC)).then_inc(s_Tfree, 1)
                        t += 1
                act.wait_ge(s_Sfree, at(b, S_PER, 2 + S_PER))
                nc.scalar.activation(th[:, :, :], lg[:, :, :], ACT.Tanh, scale=0.5).then_inc(s_th, 1)
                act.wait_ge(s_T, at(b, T_PER, t + 1))
                nc.scalar.copy(pT[:, :], psT[0:PROBROWS, t % 3, :].bitcast(BF16)).then_inc(s_Tfree, 1)
                t += 1
                assert t == T_PER
            act.drain().then_inc(s_attdone, 1)

            for n in range(NPC):
                hi, _, _, rows, a, w = pieces[n]
                act.wait_ge(s_stage[n % NSTG], 16 * (n // NSTG + 1))
                src = stage(n) if len(hi.shape) == 2 else stage(n).rearrange("p (a w) -> p a w", a=a)
                nc.scalar.copy(hi, src).then_inc(s_hi, 1)
            with act.Fori(0, GROUPS // 2) as gg:
                for par in range(2):
                    act.wait_ge(s_x1f[par], at(gg, 32, 32))
                    nc.scalar.copy(xh[:, par, :, :], x1f[:, par, :, :]).then_inc(s_xh, 1)
                    for q in range(NCH + 1):
                        n = par * NCH + q
                        if q < NCH:
                            rows = LAST if q == NCH - 1 else P
                            a, tn = za[0:rows, 2 * (q % NSL), :], za[0:rows, 2 * (q % NSL) + 1, :]
                            act.wait_ge(s_h, at(gg, 2 * NCH, n + 1))
                            act.wait_ge(s_gl, at(gg, 2 * NCH, n + 1))
                            nc.scalar.copy(a, psH[0:rows, q % 2, 0, :]).then_inc(s_copy, 1)
                        if q > 0:
                            p = q - 1
                            prow = LAST if p == NCH - 1 else P
                            act.wait_ge(s_g, at(gg, 2 * NCH, 2 + n))
                            act.wait_ge(s_gfree, at(gg, 2 * NCH, n))
                            nc.scalar.copy(gh[0:prow, p % NSL, :], za[0:prow, 2 * (p % NSL), :]).then_inc(s_gh, 1)
                        if q < NCH:
                            if q < NCR:
                                act.wait_ge(s_z, at(gg, 2 * NCR, par * NCR + q + 1))
                            else:
                                act.wait_ge(s_copy, at(gg, 2 * NCH, n + 1))
                            nc.scalar.activation(tn, a, ACT.Tanh, scale=0.5).then_inc(s_tanh, 1)

        @block.vector
        def _(dve):
            chain = [0]

            def link(loop, per, ins):
                chain[0] += 1
                ins.then_inc(s_dve, 1)
                dve.wait_ge(s_dve, at(loop, per, chain[0]))

            dve.sem_inc(s_Sfree, 2)
            dve.sem_inc(s_g, 2)
            dve.sem_inc(s_yfree, 2)
            dve.sem_inc(s_yo, 4)
            dve.wait_ge(s_wload, 16 * (WLOADS - 1))
            dve.wait_ge(s_wtc, 7)
            dve.wait_ge(s_const, 9)
            link(0, 0, nc.vector.tensor_scalar(gb_b[:, :], gb_b[:, :], 0.5, None, ALU.add))
            base0 = chain[0]
            PER = 3 + NKV + TT * 3 + 14
            with dve.Fori(0, B) as b:
                u = 0

                def unit():
                    dve.wait_ge(s_S, at(b, S_PER, u + 1))
                    return psS[:, u % 2, :]

                for hi, lo, bias, rows in ((kh[:, :], kl[:, :], bk[:, 0:1], KVW),
                                           (qh[:, 0, :], ql[:, 0, :], bq[:, 0:1], P),
                                           (qh[:, 1, :], ql[:, 1, :], bq[:, 1:2], P)):
                    ps = unit()[0:rows, :]
                    link(b, PER, nc.vector.tensor_scalar(hi, ps, bias, None, ALU.add))
                    nc.vector.scalar_tensor_tensor(out=lo, in0=ps, scalar=bias, in1=hi.bitcast(F32),
                                                   op0=ALU.add, op1=ALU.subtract).then_inc(s_Sfree, 1)
                    u += 1
                ps = unit()[:, 0:HALF].rearrange("p (i v d) -> p i v d", i=TT, v=NKV)
                nc.vector.tensor_tensor(V[:, :, :, 0:HD], ps, bv_b[:, :].rearrange("p (v d) -> p v d", v=NKV)
                                        .unsqueeze(1).to_broadcast([P, TT, NKV, HD]), ALU.add).then_inc(s_Sfree, 1)
                u += 1
                for g in range(NKV):
                    for i, heads, n, dist in UNITS:
                        ps = unit()
                        src = ps[:, 0:len(heads) * dist].rearrange("p (h n) -> p h n", h=len(heads))[:, :, 0:n]
                        nc.vector.tensor_reduce(out=MX[:, heads[0]:heads[-1] + 1, i], in_=src, op=ALU.max,
                                                axis=AX_X).then_inc(s_Sfree, 1)
                        u += 1
                    dve.wait_ge(s_Sfree, at(b, S_PER, 2 + u))
                    mx = MX[:, :, :].rearrange("p h i -> p (h i)")
                    link(b, PER, nc.vector.tensor_scalar(M2[:, 0, :], mx, -1.0, None, ALU.mult))
                    nc.vector.scalar_tensor_tensor(out=M2[:, 1, :], in0=mx, scalar=-1.0, in1=M2[:, 0, :].bitcast(F32),
                                                   op0=ALU.mult, op1=ALU.subtract).then_inc(s_m2, 1)
                    ps = unit()
                    if g:
                        dve.wait_ge(s_mrow, at(b, 32 * NKV, 32 * g))
                    nc.vector.tensor_copy(MT[:, :], ps[0:2 * G * TT, 0:P]).then_inc(s_Sfree, 1)
                    u += 1
                dve.wait_ge(s_res, at(b, 1, 1))
                for s in range(TT + 5):
                    if s < TT:
                        i = s
                        if i >= 2:
                            dve.wait_ge(s_T, at(b, T_PER, t_of[("y", i - 2)] + 1))
                        ps = unit()[:, 0:HALF].rearrange("p (h w) -> p h w", h=NH)
                        link(b, PER, nc.vector.reciprocal(rc[:, i % 2, :].unsqueeze(2), ps[:, :, HD:HD + 1]))
                        nc.vector.tensor_tensor(y[:, i % 2, :].rearrange("p (h d) -> p h d", h=NH), ps[:, :, 0:HD],
                                                rc[:, i % 2, :].unsqueeze(2).to_broadcast([P, NH, HD]),
                                                ALU.mult).then_inc(s_Sfree, 1)
                        u += 1
                    if 0 <= s - 2 < TT:
                        i = s - 2
                        if i >= 2:
                            dve.wait_ge(s_x1, at(b, TT, i - 1))
                        ps = unit()
                        nc.vector.tensor_tensor(r[:, i % 2, :], ps[:, 0:C], xn[:, i, :], ALU.add).then_inc(s_Sfree, 1)
                        u += 1
                        dve.wait_ge(s_Sfree, at(b, S_PER, 2 + u))
                        link(b, PER, nc.vector.bn_stats(st1[:, i % 2, :], r[:, i % 2, :]))
                        dve.sem_inc(s_gate, 1)
                        link(b, PER, nc.vector.bn_aggr(mv1[:, i % 2, :], st1[:, i % 2, :]))
                        nc.vector.tensor_scalar(ve1[:, i % 2, :], mv1[:, i % 2, 1:2], EPS, None, ALU.add).then_inc(s_var, 1)
                    if 0 <= s - 3 < TT:
                        i = s - 3
                        dve.wait_ge(s_rstd, at(b, TT, i + 1))
                        if i >= 2:
                            dve.wait_ge(s_T, at(b, T_PER, t_of[("x1", i - 2)] + 1))
                        nc.vector.tensor_scalar(x1[:, i % 2, :], r[:, i % 2, :], mv1[:, i % 2, 0:1], rs1[:, i % 2, 0:1],
                                                ALU.subtract, ALU.mult).then_inc(s_x1, 1)
                    if 0 <= s - 5 < TT:
                        i = s - 5
                        ps = unit()
                        nc.vector.tensor_copy(lg[:, i, :], ps[:, 0:NE]).then_inc(s_Sfree, 1)
                        u += 1
                assert u == S_PER
                dve.wait_ge(s_th, at(b, 1, 1))
                link(b, PER, nc.vector.scalar_tensor_tensor(
                    out=sc[:, :, :], in0=th[:, :, :], scalar=0.5,
                    in1=gb_b[:, :].unsqueeze(1).to_broadcast([P, TT, NE]), op0=ALU.mult, op1=ALU.add))
                dve.sem_inc(s_gate, 1)
                for i in range(TT):
                    last = nc.vector.max(out=top[:, i, :], in_=sc[:, i, :])
                link(b, PER, last)
                dve.sem_inc(s_gate, 1)
                for i in range(TT):
                    last = nc.vector.max_index(out=idx[:, i, :], in_max=top[:, i, :], in_values=sc[:, i, :])
                link(b, PER, last)
                link(b, PER, nc.vector.tensor_copy(idf[:, :, :], idx[:, :, :]))
                link(b, PER, nc.vector.tensor_tensor(
                    hit[:, :, :, :], iota_b[:, :].unsqueeze(1).unsqueeze(3).to_broadcast([P, TT, NE, TOPK]),
                    idf[:, :, 0:TOPK].unsqueeze(2).to_broadcast([P, TT, NE, TOPK]), ALU.is_equal))
                link(b, PER, nc.vector.tensor_reduce(out=pick[:, :, :], in_=hit[:, :, :, :], op=ALU.add, axis=AX_X))
                link(b, PER, nc.vector.tensor_reduce(out=tsum[:, :, 0], in_=top[:, :, 0:TOPK], op=ALU.add, axis=AX_X))
                link(b, PER, nc.vector.reciprocal(trec[:, :, :], tsum[:, :, :]))
                link(b, PER, nc.vector.tensor_tensor(prt[:, :, :], pick[:, :, :], sc[:, :, :], ALU.mult))
                link(b, PER, nc.vector.scalar_tensor_tensor(out=prt[:, :, :], in0=prt[:, :, :], scalar=0.5,
                                                            in1=trec[:, :, :].to_broadcast([P, TT, NE]),
                                                            op0=ALU.mult, op1=ALU.mult))
                for k in range(3):
                    part = pr3[:, :, k * NE:(k + 1) * NE]
                    cp = nc.vector.tensor_copy(part, prt[:, :, :])
                    if k == 2:
                        cp.then_inc(s_pr3, 1)
                        break
                    link(b, PER, cp)
                    link(b, PER, nc.vector.tensor_tensor(prt[:, :, :], prt[:, :, :], part, ALU.subtract))
                CH = chain[0] - base0
                assert CH == PER, (CH, PER)
            dve.drain().then_inc(s_attdone, 1)

            for n in range(NPC):
                hi, lo, _, rows, a, w = pieces[n]
                dve.wait_ge(s_hi, n + 1)
                src = stage(n) if len(hi.shape) == 2 else stage(n).rearrange("p (a w) -> p a w", a=a)
                nc.vector.tensor_tensor(lo, src, hi.bitcast(F32), ALU.subtract).then_inc(s_lo, 1)
            with dve.Fori(0, GROUPS // 2) as gg:
                for par in range(2):
                    dve.wait_ge(s_xh, at(gg, 2, par + 1))
                    nc.vector.tensor_tensor(xl[:, par, :, :], x1f[:, par, :, :], xh[:, par, :, :].bitcast(F32),
                                            ALU.subtract).then_inc(s_xl, 1)
                    for q in range(NCH):
                        n = par * NCH + q
                        rows = LAST if q == NCH - 1 else P
                        a, tn = za[0:rows, 2 * (q % NSL), :], za[0:rows, 2 * (q % NSL) + 1, :]
                        h2 = psH[0:rows, q % 2, 1, :]
                        if q < NCR:
                            dve.wait_ge(s_copy, at(gg, 2 * NCH, n + 1))
                            nc.vector.tensor_tensor(a, a, h2, ALU.mult).then_inc(s_z, 1)
                            dve.wait_ge(s_tanh, at(gg, 2 * NCH, n + 1))
                            nc.vector.scalar_tensor_tensor(out=tn, in0=tn, scalar=1.0, in1=a,
                                                           op0=ALU.add, op1=ALU.mult).then_inc(s_w, 1)
                            dve.wait_ge(s_w, at(gg, 2 * NCH, n + 1))
                            dve.wait_ge(s_b, at(gg, 2 * (NCR + 2), par * (NCR + 2) + q + 1))
                            nc.vector.tensor_tensor(a, tn, psB[:, q % 2, :], ALU.mult).then_inc(s_g, 1)
                        else:
                            dve.wait_ge(s_tanh, at(gg, 2 * NCH, n + 1))
                            nc.vector.scalar_tensor_tensor(out=tn, in0=tn, scalar=1.0, in1=a,
                                                           op0=ALU.add, op1=ALU.mult).then_inc(s_w, 1)
                            dve.wait_ge(s_w, at(gg, 2 * NCH, n + 1))
                            nc.vector.scalar_tensor_tensor(out=a, in0=h2, scalar=0.5, in1=tn,
                                                           op0=ALU.mult, op1=ALU.mult).then_inc(s_g, 1)
                    for k in range(KC):
                        dve.wait_ge(s_gfree, at(gg, 2 * NCH, NSL + (par + 1) * NCH))
                        nc.vector.tensor_tensor(x1f[:, par, k, :], psY[:, k, :], x1f[:, par, k, :], ALU.add).then_inc(s_yfree, 1)
                    for i in range(4):
                        dve.wait_ge(s_b, at(gg, 2 * (NCR + 2), par * (NCR + 2) + NCR + i // 2 + 1))
                        ps = psB[:, (i // 2) % 2, (i % 2) * C:(i % 2 + 1) * C]
                        k2 = i % 2
                        nc.vector.bn_stats(st2[:, k2, :], ps).then_inc(s_ln, 1)
                        dve.wait_ge(s_ln, at(gg, 16, par * 8 + 2 * i + 1))
                        dve.sem_inc(s_gate, 1)
                        nc.vector.bn_aggr(mv2[:, k2, :], st2[:, k2, :]).then_inc(s_ln, 1)
                        dve.wait_ge(s_ln, at(gg, 16, par * 8 + 2 * i + 2))
                        nc.vector.tensor_scalar(ve2[:, k2, :], mv2[:, k2, 1:2], EPS, None, ALU.add).then_inc(s_var2, 1)
                        dve.wait_ge(s_rstd2, at(gg, 8, par * 4 + i + 1))
                        dve.wait_ge(s_out[k2], at(gg, 64, 16 * (par * 2 + i // 2 + 1)))
                        nc.vector.tensor_scalar(yo[:, k2, :], ps, mv2[:, k2, 0:1], rs2[:, k2, 0:1],
                                                ALU.subtract, ALU.mult).then_inc(s_yo, 1)

        @block.tensor
        def _(pe):
            mm = nc.tensor.matmul

            pe.sem_inc(s_pfree, 2)
            pe.sem_inc(s_x1free, 2)
            pe.sem_inc(s_gfree, NSL)
            pe.wait_ge(s_wload, 16 * (WLOADS - 1))
            pe.wait_ge(s_const, 9)
            for k in range(KC):
                for m in range(KC):
                    c = k * C + m * P
                    mm(psT[:, 0, c:c + P], wq_n[:, m, k * P:(k + 1) * P], rq[:, m, :], start=True, stop=True)
                    mm(psT[:, 1, c:c + P], cp_n[:, m, k * P:(k + 1) * P], ident[:, :], start=True, stop=True)
                c = k * KVW
                mm(psT[:, 2, c:c + KVW], wk_n[:, k * P:(k + 1) * P], rk[:, :], start=True, stop=True)
                c = (KC + k) * KVW
                mm(psT[:, 2, c:c + KVW], wv_n[:, k * P:(k + 1) * P], ident[0:KVW, 0:KVW], start=True, stop=True)
                c = 2 * KC * KVW + k * NE
                mm(psT[:, 2, c:c + NE], gw_n[:, k * P:(k + 1) * P], ident[0:NE, 0:NE], start=True, stop=True)
            c = 2 * KC * KVW + 32
            for m in range(KC):
                mm(psT[:, 2, c + m:c + m + 1], rq[:, m, :], bq_n[:, m:m + 1], start=True, stop=True)
            mm(psT[0:KVW, 2, c + 2:c + 3], rk[:, :], bk_n[:, :], start=True, stop=True).then_inc(s_wt, 1)
            pe.wait_ge(s_wtc, 7)

            with pe.Fori(0, B) as b:
                u, t = 0, 0

                def s_slot():
                    pe.wait_ge(s_Sfree, at(b, S_PER, u + 1))
                    return psS[:, u % 2, :]

                def t_slot():
                    pe.wait_ge(s_Tfree, at(b, T_PER, t + 1))
                    return psT[:, t % 3, :]

                pe.wait_ge(s_x, at(b, 16, 16))
                for k in range(KC):
                    for half in range(NHALF):
                        ps = t_slot()
                        for i in range(4):
                            last = nc.tensor.transpose(ps[:, i * P:(i + 1) * P], xn[:, half * 4 + i, k * P:(k + 1) * P], ident[:, :])
                        last.then_inc(s_T, 1)
                        t += 1
                pe.wait_ge(s_Tfree, at(b, T_PER, 3 + 4))
                for wT, rows in ((wkT[:, :, :], KVW), (wqT[:, :, 0:P], P), (wqT[:, :, P:C], P)):
                    ps = s_slot()
                    for half in range(NHALF):
                        for k in range(KC):
                            last = mm(ps[0:rows, half * HALF:(half + 1) * HALF], wT[:, k, :],
                                      xT[:, k, half * HALF:(half + 1) * HALF], start=(k == 0), stop=(k == KC - 1))
                    last.then_inc(s_S, 1)
                    u += 1
                ps = s_slot()
                for i in range(TT):
                    for k in range(KC):
                        last = mm(ps[:, i * KVW:(i + 1) * KVW], xT[:, k, i * P:(i + 1) * P], wvT[:, k, :],
                                  start=(k == 0), stop=(k == KC - 1))
                last.then_inc(s_S, 1)
                u += 1

                def max_unit(g, n):
                    i, heads, cols, dist = UNITS[n]
                    ps = s_slot()
                    for e, h in enumerate(heads):
                        for c in range(0, cols, HALF):
                            w = min(HALF, cols - c)
                            last = mm(ps[:, e * dist + c:e * dist + c + w], QS[0:ROWS, g * G + h, i * P:(i + 1) * P],
                                      KS[0:ROWS, g, c:c + w], start=True, stop=(c + w < cols))
                        d = e * dist + i * P
                        last = mm(ps[:, d:d + P], ident_b[:, :], mask_b[:, :], start=False, stop=True)
                    last.then_inc(s_S, 1)

                def max_rows(g):
                    ps = s_slot()
                    pe.wait_ge(s_m2, at(b, NKV, g + 1))
                    pe.sem_inc(s_gate, 1)
                    nc.tensor.transpose(ps[0:2 * G * TT, 0:P], M2[:, :, :].rearrange("p s r -> p (s r)").bitcast(F32),
                                        ident[:, :]).then_inc(s_S, 1)

                def weigh(g, n):
                    step = g * NST + n
                    q, j, c0, diag = STEPS[n]
                    if j == 0:
                        pe.wait_ge(s_Ofree, at(b, NKV * NHALF, g * NHALF + q + 1))
                    if diag:
                        d = sum(s[3] for s in STEPS[:n + 1])
                        pe.wait_ge(s_sel, at(b, NKV * DIAGS, g * DIAGS + d))
                    else:
                        pe.wait_ge(s_Tfree, at(b, T_PER, 3 + 4 + (step + 1) * G))
                    end = j == 4 * (q + 1) - 1
                    for h in range(G):
                        last = mm(psO[32 * h:32 * h + 32, c0:HALF], V[:, j, g, :], prob[:, step % 2, h, 0:HALF - c0],
                                  start=(j == 0), stop=end)
                    last.then_inc(s_O if end else s_pfree, 1)
                    if end:
                        pe.wait_ge(s_O, at(b, NKV * NHALF, g * NHALF + q + 1))
                        pe.sem_inc(s_pfree, 1)

                pe.wait_ge(s_stack, at(b, 16 * 9, 16 * 9))
                for n in range(NU):
                    max_unit(0, n)
                    u += 1
                max_rows(0)
                u += 1
                pe.wait_ge(s_Sfree, at(b, S_PER, 2 + PROLOG))
                for g in range(NKV):
                    m = 0
                    pe.wait_ge(s_mrow, at(b, 32 * NKV, 32 * (g + 1)))
                    for n, (q, j, c0, diag) in enumerate(STEPS):
                        for h in range(G):
                            ps = t_slot()
                            mm(ps[:, 0:HALF - c0], KS[:, g, j * P:(j + 1) * P],
                               QS[:, g * G + h, q * HALF + c0:(q + 1) * HALF], start=True, stop=True).then_inc(s_T, 1)
                            t += 1
                        if g < NKV - 1:
                            for _ in range(SPREAD[n]):
                                if m < NU:
                                    max_unit(g + 1, m)
                                else:
                                    max_rows(g + 1)
                                m += 1
                                u += 1
                        if g or n:
                            weigh(g if n else g - 1, n - 1 if n else NST - 1)
                weigh(NKV - 1, NST - 1)
                pe.wait_ge(s_Ofree, at(b, NKV * NHALF, 1 + NKV * NHALF))
                for s in range(TT + 5):
                    if s < TT:
                        i = s
                        ps = s_slot()
                        for g in range(NKV):
                            last = nc.tensor.transpose(ps[:, g * P:(g + 1) * P], O[:, g, i * P:(i + 1) * P], ident[:, :])
                        last.then_inc(s_S, 1)
                        u += 1
                    if 0 <= s - 1 < TT:
                        i = s - 1
                        ps = t_slot()
                        pe.wait_ge(s_Sfree, at(b, S_PER, 2 + s_of[("norm", i)] + 1))
                        for k in range(KC):
                            last = nc.tensor.transpose(ps[:, k * P:(k + 1) * P], y[:, i % 2, k * P:(k + 1) * P], ident[:, :])
                        last.then_inc(s_T, 1)
                        assert t == t_of[("y", i)]
                        t += 1
                    if 0 <= s - 2 < TT:
                        i = s - 2
                        ps = s_slot()
                        pe.wait_ge(s_Tfree, at(b, T_PER, 3 + t_of[("y", i)] + 1))
                        for k in range(KC):
                            last = mm(ps[:, 0:C], yT[:, i % 2, k, :], cpT[:, k, :], start=(k == 0), stop=(k == KC - 1))
                        last.then_inc(s_S, 1)
                        u += 1
                    if 0 <= s - 4 < TT:
                        i = s - 4
                        ps = t_slot()
                        pe.wait_ge(s_x1, at(b, TT, i + 1))
                        for k in range(KC):
                            last = nc.tensor.transpose(ps[:, k * P:(k + 1) * P], x1[:, i % 2, k * P:(k + 1) * P], ident[:, :])
                        last.then_inc(s_T, 1)
                        t += 1
                    if 0 <= s - 5 < TT:
                        i = s - 5
                        ps = s_slot()
                        pe.wait_ge(s_Tfree, at(b, T_PER, 3 + t_of[("x1", i)] + 1))
                        for k in range(KC):
                            last = mm(ps[:, 0:NE], x1Tb[:, k, i * P:(i + 1) * P], gwT[:, k, :], start=(k == 0), stop=(k == KC - 1))
                        last.then_inc(s_S, 1)
                        u += 1
                ps = t_slot().bitcast(BF16)
                pe.wait_ge(s_pr3, at(b, 1, 1))
                pe.sem_inc(s_gate, 1)
                for i in range(TT):
                    last = nc.tensor.transpose(ps[0:PROBROWS, i * P:(i + 1) * P], pr3[:, i, :], ident_b[:, :])
                last.then_inc(s_T, 1)
                t += 1
                assert u == S_PER and t == T_PER
            pe.drain().then_inc(s_attdone, 1)
            pe.wait_ge(s_attdone, 5)
            pe.wait_ge(s_selw, 16)
            pe.wait_ge(s_lo, NPC)

            with pe.Fori(0, GROUPS // 2) as gg:
                for par in range(2):
                    pe.wait_ge(s_x1f[par], at(gg, 32, 32))
                    pe.wait_ge(s_xl, at(gg, 2, par + 1))

                    def up(q):
                        n = par * NCH + q
                        rows = LAST if q == NCH - 1 else P
                        cols = slice(q * P, q * P + rows)
                        pe.wait_ge(s_g, at(gg, 2 * NCH, n + 1))
                        for w, (wh, wl) in enumerate(((w1h, w1l), (w3h, w3l))):
                            parts = [(a, x_, k) for k in range(KC) for a, x_ in ((wh, xh), (wh, xl), (wl, xh))]
                            for e, (a, x_, k) in enumerate(parts):
                                last = mm(psH[0:rows, q % 2, w, :], a[:, k, cols], x_[:, par, k, :],
                                          start=(e == 0), stop=(e == len(parts) - 1))
                        last.then_inc(s_h, 1)
                        if q < NCR:
                            if q < 2:
                                pe.wait_ge(s_yo, at(gg, 8, par * 4 + 2 * (q + 1)))
                            mm(psB[:, q % 2, :], sel[:, q, :], pg[:, par, :], start=True, stop=True).then_inc(s_b, 1)

                    def down(q):
                        n = par * NCH + q
                        rows = LAST if q == NCH - 1 else P
                        if q == 0:
                            pe.wait_ge(s_yfree, at(gg, 4, par * 2 + 2))
                        pe.wait_ge(s_gl, at(gg, 2 * NCH, NSL + n + 1))
                        for k in range(KC):
                            for e, (a, g_) in enumerate(((w2h, gh), (w2h, gl), (w2l, gh))):
                                last = mm(psY[:, k, :], a[0:rows, q, k * P:(k + 1) * P], g_[0:rows, q % NSL, :],
                                          start=(q == 0 and e == 0), stop=(q == NCH - 1 and e == 2))
                        last.then_inc(s_gfree, 1)

                    for q in range(NCH + DLAG):
                        if q < NCH:
                            up(q)
                        if q >= DLAG:
                            down(q - DLAG)
                    pe.wait_ge(s_yfree, at(gg, 4, 2 + par * 2 + 2))
                    for m in range(2):
                        pe.wait_ge(s_g, at(gg, 2 * NCH, 2 + par * NCH + NCR - 2 + m + 1))
                        for e in range(2):
                            for k in range(KC):
                                i = 2 * m + e
                                last = nc.tensor.transpose(psB[:, m, e * C + k * P:e * C + (k + 1) * P],
                                                           x1f[:, par, k, i * P:(i + 1) * P], ident[:, :])
                        last.then_inc(s_b, 1)
                        if m == 1:
                            pe.wait_ge(s_b, at(gg, 2 * (NCR + 2), (par + 1) * (NCR + 2)))
                            pe.sem_inc(s_x1free, 1)


_INS = ['L0_attn_x', 'L0_attn_wq_w', 'L0_attn_wq_b', 'L0_attn_wk_w', 'L0_attn_wk_b', 'L0_attn_wv_w', 'L0_attn_wv_b',
        'L0_attn_cp_w', 'L0_attn_cp_b', 'L0_ffn_gate_w', 'L0_ffn_gate_b', 'L0_ffn_w1_shared', 'L0_ffn_w2_shared',
        'L0_ffn_w3_shared', 'L0_ffn_w1_routed', 'L0_ffn_w2_routed', 'L0_ffn_w3_routed']


def shape_constants():
    half = HD // 2
    theta = 1.0 / 10000.0 ** (np.arange(half, dtype=np.float32) * 2.0 / HD)

    def rotation(heads, per, scale):
        out = np.zeros((heads * HD, per * HD), np.float32)
        for h in range(heads):
            for i in range(half):
                c, s = scale * np.cos(h * theta[i]), scale * np.sin(h * theta[i])
                even, odd = h * HD + 2 * i, h * HD + 2 * i + 1
                to_even, to_odd = 2 * i * per + h % per, (2 * i + 1) * per + h % per
                out[even, to_even], out[odd, to_even] = c, -s
                out[odd, to_odd], out[even, to_odd] = c, s
        return out

    owner = (np.arange(NCR * P) // HID)[None, :] == (np.arange(PROBROWS) % NE)[:, None]
    bf16_one = np.where(owner, 0x3F80, 0).astype(np.uint16)
    return [("rot_q", rotation(NH, 8, HD ** -0.5)), ("rot_k", rotation(NKV, NKV, 1.0)),
            ("expert_of", bf16_one), ("iota_e", np.arange(NE, dtype=np.float32))]


def kernel(**inputs):
    import numpy as _np
    import concourse.bacc as _bacc
    from concourse import mybir as _mybir
    from concourse.bass_utils import run_bass_kernel_spmd as _run

    nc = _bacc.Bacc("TRN2", target_bir_lowering=False, num_devices=1)
    arrays, args = {}, []
    for name, a in [(n, _np.ascontiguousarray(inputs[n])) for n in _INS] + shape_constants():
        if name == 'L0_attn_x':
            a = a.reshape(B * T, C)
        arrays[f"in_{name}_dram"] = a
        args.append(nc.dram_tensor(f"in_{name}_dram", a.shape, _mybir.dt.from_np(a.dtype), kind="ExternalInput").ap())
    args.append(nc.dram_tensor("out_0_dram", (B * T, C), _mybir.dt.float32, kind="ExternalOutput").ap())
    attention_moe(nc, *args)
    r = _run(nc, [arrays], core_ids=[0])
    return r.results[0]["out_0_dram"].reshape(B, T, C)
```

```python
from contextlib import ExitStack

import concourse.bass as bass
import numpy as np
from concourse import mybir

F32 = mybir.dt.float32
F32R = mybir.dt.float32r
BF16 = mybir.dt.bfloat16
U16 = mybir.dt.uint16
U32 = mybir.dt.uint32
ALU = mybir.AluOpType
ACT = mybir.ActivationFunctionType
AX_X = mybir.AxisListType.X

P = 128
B, T, C = 2, 1024, 256
NH, G = 16, 4
NKV = NH // G
HD = C // NH
KVW = NKV * HD
KC = C // P
TT = T // P
HALF = 512
NHALF = T // HALF
TH = HALF // P
NE, HID, TOPK = 16, 176, 4
HALL = (NE + 1) * HID
NCH = -(-HALL // P)
NCR = NE * HID // P
LAST = HALL - (NCH - 1) * P
EPS = 1e-5
NEG = -1e30
GROUPS = B * T // HALF
PROBROWS = 3 * NE

PAIRS = ((0, 0), (0, 1), (0, 2), (1, 0), (1, 1), (2, 0))
ROWS = len(PAIRS) * HD
MROWS = 2
QROWS = ROWS + MROWS
NSLOT = 3
NPROB = 3
NSL = 3
DLAG = 2
NSTG = 3
WLOADS, WLOADS2 = 10, 4

HEADGROUPS = [(b, q, g) for b in range(B) for q in range(NHALF) for g in range(NKV)]
NK = len(HEADGROUPS)


def max_units(q):
    if q:
        return [(i, (h,), (i + 1) * P, 2 * HALF) for i in range(TH, TT) for h in range(G)]
    units = [(0, (0, 1, 2, 3), P, P), (1, (0, 1, 2, 3), 2 * P, 2 * P)]
    for i in (2, 3):
        units += [(i, (0, 1), (i + 1) * P, HALF), (i, (2, 3), (i + 1) * P, HALF)]
    return units


def exp_steps(q):
    return [(j, max(0, P * (j - TH * q)), j >= TH * q) for j in range(TH * (q + 1))]


def inputs_items(b):
    items = [("xT", b, k, half) for k in range(KC) for half in range(NHALF)]
    items += [("proj", b, 0), ("proj", b, 1), ("split", b, 0), ("proj", b, 2), ("split", b, 1), ("v", b), ("split", b, 2)]
    return items


def rows_items(b, q):
    items = []
    for s in range(TH + 3):
        for lag, name in ((0, "yT"), (1, "cp"), (2, "ln"), (3, "x1T")):
            if 0 <= s - lag < TH:
                items.append((name, b, q * TH + s - lag))
    return items + [("gate", b, q), ("route", b, q), ("pT", b, q)]


def plan():
    seq, done = [], set()
    clock = {"pe": 0.0, "act": 0.0, "dve": 0.0}
    t_hist = []
    s_hist = []

    def put(item):
        kind = item[0]
        pe = act = dve = 0.0
        if kind == "xT":
            pe, act = 450, 570
        elif kind == "proj":
            pe, act, dve = 3400, 1000, 1200
        elif kind == "split":
            act = 1000
        elif kind == "v":
            pe, dve = 3400, 660
        elif kind == "smax":
            _, q, _ = HEADGROUPS[item[1]]
            i, heads, n, dist = max_units(q)[item[2]]
            pe, dve = len(heads) * (n / 2.4 + 54), (len(heads) * n + 120) / 0.96 + 30
        elif kind == "mrow":
            pe, dve = 60, 700
        elif kind == "st":
            n = HALF - exp_steps(HEADGROUPS[item[1]][1])[item[2]][1]
            pe, act = n / 2.4, (n + 172) / 1.2
        elif kind == "pv":
            n = HALF - exp_steps(HEADGROUPS[item[1]][1])[item[2]][1]
            pe = 4 * n / 2.4 + 60
        elif kind == "evac":
            act = 570
        elif kind == "norm":
            pe, dve = 450, 900
        elif kind == "yT":
            pe, act = 220, 400
        elif kind == "cp":
            pe, dve = 860, 1300
        elif kind == "ln":
            dve = 450
        elif kind == "x1T":
            pe, act = 220, 400
        elif kind == "gate":
            pe, dve = 1700, 250
        elif kind == "route":
            act, dve = 300, 3500
        elif kind == "pT":
            pe, act = 220, 570
        clock["pe"] += pe
        if act:
            clock["act"] = max(clock["act"], clock["pe"]) + act
        if dve:
            clock["dve"] = max(clock["dve"], clock["pe"]) + dve
        if kind in ("xT", "st", "yT", "x1T", "pT"):
            t_hist.append(clock["act"])
            if len(t_hist) > 3:
                clock["pe"] = max(clock["pe"], t_hist[-4])
        if kind in ("proj", "v", "smax", "mrow", "norm", "cp", "gate"):
            s_hist.append(clock["dve"])
            if len(s_hist) > 2:
                clock["pe"] = max(clock["pe"], s_hist[-3])
        seq.append(item)
        done.add(item)

    ahead = []
    for k in range(NK):
        b, q, g = HEADGROUPS[k]
        if k == 6:
            ahead += [(i, None) for i in inputs_items(1)] + [(("kload", 1), None)]
        if k % 2 and (k + 1) // 2 >= NSLOT - 1:
            s = (k + 1) // 2
            if NSLOT <= s < NK // 2:
                last = 2 * (s - NSLOT) + 1
                ahead.append((("qload", s), ("st", last, len(exp_steps(HEADGROUPS[last][1])) - 1, G - 1)))
        ahead += [(("smax", k, n), None) for n in range(len(max_units(q)))]
        ahead.append((("mrow", k), None))
    behind = []

    for item in inputs_items(0):
        put(item)
        if item == ("split", 0, 0):
            put(("kload", 0))
        if item == ("split", 0, 1):
            put(("qload", 0))
    put(("qload", 1))
    put(("qload", 2))

    def filler():
        if behind:
            put(behind.pop(0))
            return True
        if ahead and (ahead[0][1] is None or ahead[0][1] in done):
            put(ahead.pop(0)[0])
            return True
        return False

    def base(item):
        while clock["dve"] - clock["pe"] < 700 and filler():
            pass
        put(item)

    waiting = None
    for k in range(NK):
        b, q, g = HEADGROUPS[k]
        while ("mrow", k) not in done:
            assert ahead[0][1] is None or ahead[0][1] in done
            put(ahead.pop(0)[0])
        for n in range(len(exp_steps(q))):
            for h in range(G):
                base(("st", k, n, h))
            if waiting is not None:
                base(("pv",) + waiting)
                wk, wn = waiting
                wb, wq, wg = HEADGROUPS[wk]
                if wn == len(exp_steps(wq)) - 1:
                    put(("evac", wk))
                    behind.append(("norm", wk))
                    if wg == NKV - 1:
                        behind += rows_items(wb, wq)
            waiting = (k, n)
    put(("pv",) + waiting)
    put(("evac", NK - 1))
    behind.append(("norm", NK - 1))
    behind += rows_items(B - 1, NHALF - 1)
    while behind:
        put(behind.pop(0))
    assert not ahead
    return seq


SEQ = plan()
S_KINDS = ("proj", "v", "smax", "mrow", "norm", "cp", "gate")
T_KINDS = ("xT", "st", "yT", "x1T", "pT")


def count(*kinds):
    return {item: n + 1 for n, item in enumerate(i for i in SEQ if i[0] in kinds)}


S_NO, T_NO = count(*S_KINDS), count(*T_KINDS)
PV_NO, EVAC_NO = count("pv"), count("evac")
SPLIT_NO, CP_NO, LN_NO = count("split"), count("cp"), count("ln")
SEL_NO = {item: n + 1 for n, item in enumerate(
    i for i in SEQ if i[0] == "st" and i[3] == G - 1 and exp_steps(HEADGROUPS[i[1]][1])[i[2]][2])}

WUNITS = sorted(
    [("up", e, max(0, -(-(HID * e - P + 1) // P))) for e in range(NE + 1)]
    + [("down", c, 2 * c + DLAG) for c in range(NCR // 2)]
    + [("down", NCR // 2, NCR + DLAG), ("down", NCR // 2 + 1, NCR + DLAG)], key=lambda u: u[2])


def needs(kind, chunk):
    if kind == "up":
        top = (min(P * (chunk + 1), HALL) - 1) // HID
    else:
        top = chunk // 2 if chunk < NCR else NCR // 2 + chunk - NCR
    return 1 + max(n for n, u in enumerate(WUNITS) if u[0] == kind and u[1] <= top)


def at(turn, per, n):
    return turn * per + n


def attention_moe(nc, x, wq_w, wq_b, wk_w, wk_b, wv_w, wv_b, cp_w, cp_b, gate_w, gate_b,
                  w1_shared, w2_shared, w3_shared, w1_routed, w2_routed, w3_routed,
                  rot_q, rot_k, expert_of, iota_e, out):
    x1t_dram = nc.dram_tensor("x1t_scratch", (C, B * T), F32, kind="Internal").ap()
    x1_dram = nc.dram_tensor("x1_scratch", (B * T, C), F32, kind="Internal").ap()

    ctx = ExitStack()
    with ctx:
        def sem(name):
            return ctx.enter_context(nc.semaphore(name))

        def sb(name, shape, dt=F32, stack=ctx):
            return stack.enter_context(nc.sbuf_tensor(name, shape, dt))

        def pb(name, shape, dt=F32, stack=ctx):
            return stack.enter_context(nc.psum_tensor(name, shape, dt))

        ident = sb("ident", [P, P])
        eps_pow = sb("eps_pow", [P, 1])
        stage = sb("stage", [P, NSTG, 2 * KC * HID])
        probT = sb("probT", [PROBROWS, B * T], BF16)

        att = ExitStack()
        ident_b = sb("ident_b", [P, P], BF16, att)
        mask_b = sb("mask_b", [P, P], BF16, att)
        wq_n = sb("wq_n", [P, KC, C], F32, att)
        wk_n = sb("wk_n", [KVW, C], F32, att)
        wv_n = sb("wv_n", [KVW, C], F32, att)
        cp_n = sb("cp_n", [P, KC, C], F32, att)
        gw_n = sb("gw_n", [NE, C], F32, att)
        rq = sb("rq", [P, KC, P], F32, att)
        rk = sb("rk", [KVW, KVW], F32, att)
        bq_n = sb("bq_n", [P, KC], F32, att)
        bk_n = sb("bk_n", [KVW, 1], F32, att)
        bv_b = sb("bv_b", [P, KVW], F32, att)
        cpb_b = sb("cpb_b", [P, C], F32, att)
        gb_b = sb("gb_b", [P, NE], F32, att)
        iota_b = sb("iota_b", [P, NE], F32, att)
        wqT = sb("wqT", [P, KC, C], F32, att)
        wkT = sb("wkT", [P, KC, KVW], F32, att)
        wvT = sb("wvT", [P, KC, KVW], F32, att)
        cpT = sb("cpT", [P, KC, C], F32, att)
        gwT = sb("gwT", [P, KC, NE], F32, att)
        bq = sb("bq", [P, KC], F32, att)
        bk = sb("bk", [KVW, 1], F32, att)
        xn = sb("xn", [P, B, TT, C], F32, att)
        xT = sb("xT", [P, KC, T], F32, att)
        rest = sb("rest", [P, 2, T], F32, att)
        qp = sb("qp", [P, KC, 3, T], BF16, att)
        kp = sb("kp", [KVW, 3, T], BF16, att)
        QS = sb("QS", [QROWS, NSLOT, 2 * G, HALF], BF16, att)
        KS = sb("KS", [QROWS, B, NKV, T], BF16, att)
        V = sb("V", [P, B, TT, NKV, 2 * HD], F32, att)
        prob = sb("prob", [P, NPROB, G, HALF], F32, att)
        MX = sb("MX", [P, G, TH], F32, att)
        M2 = sb("M2", [P, MROWS, G * TH], BF16, att)
        MT = sb("MT", [MROWS * G * TH, P], BF16, att)
        O = sb("O", [P, 2, HALF], F32, att)
        rc = sb("rc", [P, G * TH], F32, att)
        y = sb("y", [P, 2, TH, C], F32, att)
        yT = sb("yT", [P, 2, KC, P], F32, att)
        r = sb("r", [P, 3, C], F32, att)
        st1 = sb("st1", [P, 6], F32, att)
        mv1 = sb("mv1", [P, 3, 2], F32, att)
        ve1 = sb("ve1", [P, 3, 1], F32, att)
        rs1 = sb("rs1", [P, 3, 1], F32, att)
        x1 = sb("x1", [P, 3, C], F32, att)
        x1T = sb("x1T", [P, 2, KC, HALF], F32, att)
        lg = sb("lg", [P, TH, NE], F32, att)
        th = sb("th", [P, TH, NE], F32, att)
        sc = sb("sc", [P, TH, NE], F32, att)
        top = sb("top", [P, TH, 8], F32, att)
        idx = sb("idx", [P, TH, 8], U32, att)
        idf = sb("idf", [P, TH, 8], F32, att)
        hit = sb("hit", [P, TH, NE, TOPK], F32, att)
        pick = sb("pick", [P, TH, NE], F32, att)
        tsum = sb("tsum", [P, TH, 1], F32, att)
        trec = sb("trec", [P, TH, 1], F32, att)
        prt = sb("prt", [P, TH, NE], F32, att)
        pr3 = sb("pr3", [P, TH, PROBROWS], BF16, att)
        psS = pb("psS", [P, 2, 2 * HALF], F32, att)
        psT = pb("psT", [P, 3, HALF], F32, att)
        psO = pb("psO", [P, HALF], F32, att)
        att.close()

        ffn = ExitStack()
        sel = sb("sel", [PROBROWS, NCR, P], BF16, ffn)
        wuh = sb("wuh", [P, 2, KC, HALL], F32R, ffn)
        wul = sb("wul", [P, 2, KC, HALL], F32R, ffn)
        wdh = sb("wdh", [P, NCH, C], F32R, ffn)
        wdl = sb("wdl", [P, NCH, C], F32R, ffn)
        x1f = sb("x1f", [P, KC, HALF], F32, ffn)
        xh = sb("xh", [P, KC, HALF], F32R, ffn)
        xl = sb("xl", [P, KC, HALF], F32R, ffn)
        za = sb("za", [P, NSL, HALF], F32, ffn)
        ta = sb("ta", [P, NSL, HALF], F32, ffn)
        gh = sb("gh", [P, NSL, HALF], F32R, ffn)
        gl = sb("gl", [P, NSL, HALF], F32R, ffn)
        yS = sb("yS", [P, KC, HALF], F32, ffn)
        x1r = sb("x1r", [P, TH, C], F32, ffn)
        st2 = sb("st2", [P, TH, 6], F32, ffn)
        mv2 = sb("mv2", [P, TH, 2], F32, ffn)
        ve2 = sb("ve2", [P, TH], F32, ffn)
        rs2 = sb("rs2", [P, TH], F32, ffn)
        half_pow = sb("half_pow", [P, TH], F32, ffn)
        psH = pb("psH", [P, 2, 2, HALF], F32, ffn)
        psB = pb("psB", [P, 2, HALF], F32, ffn)
        psY = pb("psY", [P, KC, HALF], F32, ffn)
        ffn.close()

        s_wload = sem("s_wload")
        s_const = sem("s_const")
        s_wload2 = sem("s_wload2")
        s_ones = sem("s_ones")
        s_wt = sem("s_wt")
        s_wtc = sem("s_wtc")
        s_x = [sem(f"s_xload{b}") for b in range(B)]
        s_S = sem("s_S")
        s_Sfree = sem("s_Sfree")
        s_T = sem("s_T")
        s_Tfree = sem("s_Tfree")
        s_part1 = sem("s_part1")
        s_part2 = sem("s_part2")
        s_part3 = sem("s_part3")
        s_kload = [sem(f"s_kload{b}") for b in range(B)]
        s_qload = [sem(f"s_qload{i}") for i in range(NSLOT)]
        s_m2 = sem("s_m2")
        s_mrow = sem("s_mrow")
        s_res = sem("s_res")
        s_sel = sem("s_sel")
        s_pv = sem("s_pv")
        s_evac = sem("s_evac")
        s_var = sem("s_var")
        s_rstd = sem("s_rstd")
        s_x1 = sem("s_x1")
        s_th = sem("s_th")
        s_pr3 = sem("s_pr3")
        s_x1st = [sem(f"s_x1st{i}") for i in range(3)]
        s_x1tst = [sem(f"s_x1tst{i}") for i in range(2)]
        s_attdone = sem("s_attdone")
        s_dve = sem("s_dve")
        s_stage = [sem(f"s_stage{i}") for i in range(NSTG)]
        s_whi = sem("s_whi")
        s_wlo = sem("s_wlo")
        s_selw = sem("s_selw")
        s_x1f = sem("s_x1f")
        s_x1r = sem("s_x1r")
        s_xh = sem("s_xh")
        s_xl = sem("s_xl")
        s_h = sem("s_h")
        s_b = sem("s_b")
        s_copy = sem("s_copy")
        s_z = sem("s_z")
        s_tanh = sem("s_tanh")
        s_w = sem("s_w")
        s_g = sem("s_g")
        s_gh = sem("s_gh")
        s_gl = sem("s_gl")
        s_down = sem("s_down")
        s_yS = sem("s_yS")
        s_back = sem("s_back")
        s_resid = sem("s_resid")
        s_st2 = sem("s_st2")
        s_var2 = sem("s_var2")
        s_rstd2 = sem("s_rstd2")
        s_norm2 = sem("s_norm2")
        s_out = sem("s_out")
        s_pass = sem("s_pass")

        block = ctx.enter_context(nc.Block())

        wd_flat = w2_routed.rearrange("e h d -> (e h) d")

        def wunit(n):
            kind, i, _ = WUNITS[n]
            st = stage[:, n % NSTG, :]
            if kind == "up":
                c = slice(i * HID, (i + 1) * HID)
                return P, st.rearrange("p (w k h) -> p w k h", w=2, k=KC), wuh[:, :, :, c], wul[:, :, :, c]
            if i < NCR // 2:
                c = slice(2 * i, 2 * i + 2)
                return P, st[:, 0:2 * C].rearrange("p (q d) -> p q d", q=2), wdh[:, c, :], wdl[:, c, :]
            c = NCR + i - NCR // 2
            rows = P if c < NCH - 1 else LAST
            return rows, st[0:rows, 0:C], wdh[0:rows, c, :], wdl[0:rows, c, :]

        @block.sync
        def _(sp):
            sp.dma_start(xn[:, 0, :, :], x[0:T, :].rearrange("(i p) c -> p i c", p=P)).then_inc(s_x[0], 16)
            sp.dma_start(wq_n[:, :, :], wq_w.rearrange("(m p) c -> p m c", p=P)).then_inc(s_wload, 16)
            sp.dma_start(rq[:, :, :], rot_q.rearrange("(m p) c -> p m c", p=P)).then_inc(s_wload, 16)
            sp.dma_start(wk_n[:, :], wk_w).then_inc(s_wload, 16)
            sp.dma_start(rk[:, :], rot_k).then_inc(s_wload, 16)
            sp.dma_start(wv_n[:, :], wv_w).then_inc(s_wload, 16)
            for m in range(KC):
                sp.dma_start(bq_n[:, m:m + 1], wq_b[m * P:(m + 1) * P].rearrange("(p a) -> p a", a=1)).then_inc(s_wload, 16)

            def wload(n):
                kind, i, _ = WUNITS[n]
                rows, st, _, _ = wunit(n)
                if n >= NSTG:
                    sp.wait_ge(s_wlo, n - NSTG + 1)
                if kind == "up":
                    for w, (rt, shd) in enumerate(((w1_routed, w1_shared), (w3_routed, w3_shared))):
                        src = rt[i] if i < NE else shd
                        sp.dma_start(st[:, w, :, :], src.rearrange("(k p) h -> p k h", p=P)).then_inc(s_stage[n % NSTG], 16)
                else:
                    if i < NCR // 2:
                        src = wd_flat[2 * i * P:(2 * i + 2) * P, :].rearrange("(q p) d -> p q d", p=P)
                    else:
                        src = w2_shared[(i - NCR // 2) * P:(i - NCR // 2) * P + rows, :]
                    sp.dma_start(st, src).then_inc(s_stage[n % NSTG], 32)

            for item in SEQ:
                kind = item[0]
                if kind == "kload":
                    b = item[1]
                    for a, (_, part) in enumerate(PAIRS):
                        sp.wait_ge((s_part1, s_part2, s_part3)[part], 3 * b + 1)
                        sp.dma_start(KS[a * HD:(a + 1) * HD, b, :, :], kp[:, part, :]).then_inc(s_kload[b], 16)
                elif kind == "qload":
                    s = item[1]
                    b, q, g = HEADGROUPS[2 * s]
                    m = g // 2
                    if s >= NSLOT:
                        last = 2 * (s - NSLOT) + 1
                        sp.wait_ge(s_T, T_NO[("st", last, len(exp_steps(HEADGROUPS[last][1])) - 1, G - 1)])
                    for a, (part, _) in enumerate(PAIRS):
                        sp.wait_ge((s_part1, s_part2, s_part3)[part], 3 * b + 2 + m)
                        sp.dma_start(QS[a * HD:(a + 1) * HD, s % NSLOT, :, :],
                                     qp[:, m, part, q * HALF:(q + 1) * HALF]).then_inc(s_qload[s % NSLOT], 16)
                    if s == 0:
                        sp.dma_start(xn[:, 1, :, :], x[T:2 * T, :].rearrange("(i p) c -> p i c", p=P)).then_inc(s_x[1], 16)
                elif kind == "mrow":
                    k = item[1]
                    sp.wait_ge(s_Sfree, S_NO[item])
                    g = HEADGROUPS[k][2]
                    sp.dma_start(QS[ROWS:QROWS, (k // 2) % NSLOT, g % 2 * G:(g % 2 + 1) * G, :]
                                 .rearrange("s h (i t) -> s (h i) t", t=P), MT[:, :]).then_inc(s_mrow, 16)
                elif kind == "ln":
                    n = LN_NO[item] - 1
                    sp.wait_ge(s_x1, n + 1)
                    _, b, i = item
                    sp.dma_start(x1_dram[b * T + i * P:b * T + (i + 1) * P, :], x1[:, n % 3, :]).then_inc(s_x1st[n % 3], 16)
                elif kind == "gate":
                    _, b, q = item
                    sp.wait_ge(s_Tfree, T_NO[("x1T", b, q * TH + TH - 1)])
                    t0 = b * T + q * HALF
                    sp.dma_start(x1t_dram[:, t0:t0 + HALF].rearrange("(k p) t -> p k t", p=P), x1T[:, q, :, :]).then_inc(s_x1tst[q], 16)
            for n in range(NSTG):
                wload(n)
            tiles = B * TT
            for i in range(3):
                sp.wait_ge(s_x1st[i], 16 * ((tiles - i + 2) // 3))
            for q in range(2):
                sp.wait_ge(s_x1tst[q], 16 * B)
            sp.sem_inc(s_attdone, 1)

            sp.wait_ge(s_attdone, 5)
            sp.dma_start(x1f[:, :, :], x1t_dram[:, 0:HALF].rearrange("(k p) t -> p k t", p=P)).then_inc(s_x1f, 16)
            sp.dma_start(sel[:, :, :].bitcast(U16), expert_of.rearrange("k (q p) -> k q p", p=P)).then_inc(s_selw, 16)
            sp.dma_start(x1r[:, :, :], x1_dram[0:HALF, :].rearrange("(i p) c -> p i c", p=P)).then_inc(s_x1r, 16)
            for n in range(NSTG, len(WUNITS)):
                wload(n)
                if n == len(WUNITS) // 2:
                    sp.wait_ge(s_xl, KC)
                    sp.dma_start(x1f[:, :, :], x1t_dram[:, HALF:2 * HALF].rearrange("(k p) t -> p k t", p=P)).then_inc(s_x1f, 16)

            def rows_turn(n):
                sp.wait_ge(s_norm2, at(n, TH, 0))
                sp.sem_inc(s_pass, 1)
                sp.dma_start(out[bass.ds(n * HALF - HALF, HALF), :].rearrange("(i p) c -> p i c", p=P), x1r[:, :, :]).then_inc(s_out, 16)
                sp.wait_ge(s_out, at(n, 16, 0))
                sp.sem_inc(s_pass, 1)
                sp.dma_start(x1r[:, :, :], x1_dram[bass.ds(n * HALF, HALF), :].rearrange("(i p) c -> p i c", p=P)).then_inc(s_x1r, 16)

            with sp.Fori(1, GROUPS - 1) as n:
                rows_turn(n)
                sp.wait_ge(s_xl, at(n, KC, KC))
                sp.sem_inc(s_pass, 1)
                sp.dma_start(x1f[:, :, :], x1t_dram[:, bass.ds(n * HALF + HALF, HALF)].rearrange("(k p) t -> p k t", p=P)).then_inc(s_x1f, 16)
            rows_turn(GROUPS - 1)
            sp.sem_inc(s_x1f, 16)
            sp.wait_ge(s_norm2, TH * GROUPS)
            sp.dma_start(out[(GROUPS - 1) * HALF:GROUPS * HALF, :].rearrange("(i p) c -> p i c", p=P), x1r[:, :, :]).then_inc(s_out, 16)
            sp.wait_ge(s_out, 16 * GROUPS)

        @block.gpsimd
        def _(pool):
            nc.gpsimd.memset(ident[:, :], 0.0).then_inc(s_const, 1)
            nc.gpsimd.memset(ident_b[:, :], 0.0).then_inc(s_const, 1)
            nc.gpsimd.memset(mask_b[:, :], 0.0).then_inc(s_const, 1)
            pool.wait_ge(s_const, 3)
            for m in (ident, ident_b):
                nc.gpsimd.affine_select(out=m[:, :], in_=m[:, :], compare_op=ALU.not_equal, fill=1.0, base=0,
                                        pattern=[[-1, P]], channel_multiplier=1).then_inc(s_const, 1)
            nc.gpsimd.affine_select(out=mask_b[:, :], in_=mask_b[:, :], compare_op=ALU.is_ge, fill=NEG, base=0,
                                    pattern=[[-1, P]], channel_multiplier=1).then_inc(s_const, 1)
            nc.gpsimd.memset(eps_pow[:, :], -0.5).then_inc(s_const, 1)
            pool.dma_start(cp_n[:, :, :], cp_w.rearrange("(m p) c -> p m c", p=P)).then_inc(s_wload2, 16)
            pool.dma_start(cpb_b[:, :], cp_b.partition_broadcast(P)).then_inc(s_wload2, 16)
            pool.dma_start(gb_b[:, :], gate_b.partition_broadcast(P)).then_inc(s_wload2, 16)
            pool.dma_start(iota_b[:, :], iota_e.partition_broadcast(P)).then_inc(s_wload2, 16)
            for item in SEQ:
                kind = item[0]
                if kind == "split":
                    _, b, m = item
                    n = 3 * b + m
                    rows = KVW if m == 0 else P
                    part = kp if m == 0 else qp[:, m - 1, :, :]
                    pool.wait_ge(s_part2, n + 1)
                    nc.gpsimd.tensor_tensor(part[:, 2, :], rest[0:rows, n % 2, :], part[:, 1, :], ALU.subtract).then_inc(s_part3, 1)
                    if m == KC:
                        pool.wait_ge(s_T, T_NO[("xT", b, KC - 1, NHALF - 1)])
                        if b == 0:
                            pool.wait_ge(s_wload, 16 * WLOADS)
                            pool.wait_ge(s_wload2, 16 * WLOADS2)
                        nc.gpsimd.tensor_tensor(xn[:, b, :, :], xn[:, b, :, :], cpb_b[:, :].unsqueeze(1).to_broadcast([P, TT, C]),
                                                ALU.add).then_inc(s_res, 1)
                elif item in SEL_NO:
                    _, k, n, _ = item
                    pool.wait_ge(s_Tfree, T_NO[item])
                    blk = prob[:, (PV_NO[("pv", k, n)] - 1) % NPROB, :, 0:P]
                    nc.gpsimd.affine_select(out=blk, in_=blk, compare_op=ALU.is_ge, fill=0.0, base=0,
                                            pattern=[[0, G], [1, P]], channel_multiplier=-1).then_inc(s_sel, 1)
                elif kind == "cp":
                    n = CP_NO[item] - 1
                    pool.wait_ge(s_var, n + 1)
                    nc.gpsimd.tensor_tensor(rs1[:, n % 3, :], ve1[:, n % 3, :], eps_pow[:, :], ALU.pow).then_inc(s_rstd, 1)
            pool.drain().then_inc(s_attdone, 1)
            pool.wait_ge(s_attdone, 5)
            nc.gpsimd.memset(half_pow[:, :], -0.5).then_inc(s_const, 1)
            pool.sem_inc(s_gl, NSL)

            def low_weights(n):
                rows, st, hi, lo = wunit(n)
                pool.wait_ge(s_whi, n + 1)
                nc.gpsimd.tensor_tensor(lo, st, hi.bitcast(F32), ALU.subtract).then_inc(s_wlo, 1)

            def turn(n, first):
                for q in range(NCH):
                    if first:
                        for e, u in enumerate(WUNITS):
                            if (u[2] == q + 2) or (q == 0 and u[2] < 2):
                                low_weights(e)
                    rows = LAST if q == NCH - 1 else P
                    pool.wait_ge(s_gh, at(n, NCH, q + 1))
                    nc.gpsimd.tensor_tensor(gl[0:rows, q % NSL, :], za[0:rows, q % NSL, :],
                                            gh[0:rows, q % NSL, :].bitcast(F32), ALU.subtract).then_inc(s_gl, 1)
                    if q == 7 and not first:
                        spread2(at(n, 1, 0))

            def spread2(n):
                pool.wait_ge(s_var2, n)
                nc.gpsimd.tensor_tensor(rs2[:, :], ve2[:, :], half_pow[:, :], ALU.pow).then_inc(s_rstd2, 1)

            pool.wait_ge(s_const, 8)
            turn(0, True)
            with pool.Fori(1, GROUPS) as n:
                turn(n, False)
            spread2(GROUPS)

        @block.scalar
        def _(act):
            act.dma_start(gw_n[:, :], gate_w).then_inc(s_wload, 16)
            act.dma_start(bk_n[:, :], wk_b.rearrange("(p a) -> p a", a=1)).then_inc(s_wload, 16)
            act.dma_start(bv_b[:, :], wv_b.partition_broadcast(P)).then_inc(s_wload, 16)
            act.wait_ge(s_wt, 1)
            nc.scalar.copy(wqT[:, :, :], psT[:, 0, :].rearrange("p (k o) -> p k o", k=KC)).then_inc(s_wtc, 1)
            nc.scalar.copy(cpT[:, :, :], psT[:, 1, :].rearrange("p (k o) -> p k o", k=KC)).then_inc(s_wtc, 1)
            kv = psT[:, 2, 0:2 * KC * KVW].rearrange("p (w k o) -> p w k o", w=2, k=KC)
            nc.scalar.copy(wkT[:, :, :], kv[:, 0, :, :]).then_inc(s_wtc, 1)
            nc.scalar.copy(wvT[:, :, :], kv[:, 1, :, :]).then_inc(s_wtc, 1)
            o = 2 * KC * KVW
            nc.scalar.copy(gwT[:, :, :], psT[:, 2, o:o + KC * NE].rearrange("p (k o) -> p k o", k=KC)).then_inc(s_wtc, 1)
            nc.scalar.copy(bq[:, :], psT[:, 2, o + 32:o + 34]).then_inc(s_wtc, 1)
            nc.scalar.copy(bk[:, :], psT[0:KVW, 2, o + 34:o + 35]).then_inc(s_wtc, 1)
            act.wait_ge(s_wtc, 7)
            for item in SEQ:
                kind = item[0]
                if kind in T_KINDS:
                    ps = psT[:, (T_NO[item] - 1) % 3, :]
                if kind == "st":
                    _, k, n, h = item
                    c0 = exp_steps(HEADGROUPS[k][1])[n][1]
                    step = PV_NO[("pv", k, n)] - 1
                    if h == 0 and step >= NPROB:
                        act.wait_ge(s_pv, step - NPROB + 1)
                    act.wait_ge(s_T, T_NO[item])
                    nc.scalar.activation(prob[:, step % NPROB, h, 0:HALF - c0], ps[:, 0:HALF - c0], ACT.Exp).then_inc(s_Tfree, 1)
                elif kind == "evac":
                    k = item[1]
                    if k >= 2:
                        act.wait_ge(s_S, S_NO[("norm", k - 2)])
                    act.wait_ge(s_pv, PV_NO[("pv", k, len(exp_steps(HEADGROUPS[k][1])) - 1)])
                    nc.scalar.copy(O[:, k % 2, :], psO[:, :]).then_inc(s_evac, 1)
                elif kind == "xT":
                    _, b, k, half = item
                    if b and (k, half) == (0, 0):
                        act.wait_ge(s_S, S_NO[("v", b - 1)])
                    act.wait_ge(s_T, T_NO[item])
                    nc.scalar.copy(xT[:, k, half * HALF:(half + 1) * HALF], ps).then_inc(s_Tfree, 1)
                elif kind == "proj":
                    _, b, m = item
                    rows = KVW if m == 0 else P
                    part = kp if m == 0 else qp[:, m - 1, :, :]
                    bias = bk[:, 0:1] if m == 0 else bq[:, m - 1:m]
                    if b:
                        act.wait_ge(s_kload[b - 1], 16 * len(PAIRS))
                        for s in (2, 3):
                            act.wait_ge(s_qload[s % NSLOT], 16 * len(PAIRS) * (s // NSLOT + 1))
                        act.wait_ge(s_qload[1], 16 * len(PAIRS))
                    act.wait_ge(s_S, S_NO[item])
                    nc.scalar.activation(part[:, 0, :], psS[0:rows, (S_NO[item] - 1) % 2, :], ACT.Identity,
                                         bias=bias).then_inc(s_part1, 1)
                elif kind == "split":
                    _, b, m = item
                    n = 3 * b + m
                    rows = KVW if m == 0 else P
                    part = kp if m == 0 else qp[:, m - 1, :, :]
                    act.wait_ge(s_Sfree, S_NO[("proj", b, m)])
                    nc.scalar.copy(part[:, 1, :], rest[0:rows, n % 2, :]).then_inc(s_part2, 1)
                elif kind == "yT":
                    act.wait_ge(s_T, T_NO[item])
                    nc.scalar.copy(yT[:, item[2] % 2, :, :], ps[:, 0:C].rearrange("p (k t) -> p k t", k=KC)).then_inc(s_Tfree, 1)
                elif kind == "x1T":
                    _, b, i = item
                    if b and i % TH == 0:
                        act.wait_ge(s_x1tst[i // TH], 16 * b)
                    act.wait_ge(s_T, T_NO[item])
                    nc.scalar.copy(x1T[:, i // TH, :, (i % TH) * P:(i % TH + 1) * P],
                                   ps[:, 0:C].rearrange("p (k t) -> p k t", k=KC)).then_inc(s_Tfree, 1)
                elif kind == "route":
                    _, b, q = item
                    act.wait_ge(s_Sfree, S_NO[("gate", b, q)])
                    nc.scalar.activation(th[:, :, :], lg[:, :, :], ACT.Tanh, scale=0.5).then_inc(s_th, 1)
                elif kind == "pT":
                    _, b, q = item
                    t0 = b * T + q * HALF
                    act.wait_ge(s_T, T_NO[item])
                    nc.scalar.copy(probT[:, t0:t0 + HALF], ps[0:PROBROWS, :].bitcast(BF16)[:, 0:HALF]).then_inc(s_Tfree, 1)
            act.drain().then_inc(s_attdone, 1)
            act.wait_ge(s_attdone, 5)

            def high_weights(n):
                rows, st, hi, lo = wunit(n)
                act.wait_ge(s_stage[n % NSTG], 32 * (n // NSTG + 1))
                nc.scalar.copy(hi, st).then_inc(s_whi, 1)

            def high_rows(n, k):
                nc.scalar.copy(xh[:, k, :], x1f[:, k, :]).then_inc(s_xh, 1)

            def high_gated(count_, q):
                rows = LAST if q == NCH - 1 else P
                act.wait_ge(s_g, count_ + 2)
                act.wait_ge(s_down, count_)
                nc.scalar.copy(gh[0:rows, q % NSL, :], za[0:rows, q % NSL, :]).then_inc(s_gh, 1)

            def sums(n):
                act.wait_ge(s_down, n * NCH + NSL)
                for k in range(KC):
                    nc.scalar.copy(yS[:, k, :], psY[:, k, :]).then_inc(s_yS, 1)

            def turn(n, first):
                for q in range(NCH):
                    if first:
                        for e, u in enumerate(WUNITS):
                            if (u[2] == q + 2) or (q == 0 and u[2] < 2):
                                high_weights(e)
                    if q == 2 and not first:
                        sums(n)
                    rows = LAST if q == NCH - 1 else P
                    act.wait_ge(s_h, at(n, NCH, q + 1))
                    act.wait_ge(s_gl, at(n, NCH, q + 1))
                    nc.scalar.copy(za[0:rows, q % NSL, :], psH[0:rows, q % 2, 0, :]).then_inc(s_copy, 1)
                    if q == NCH - 1:
                        act.wait_ge(s_x1f, at(n, 16, 32))
                        for k in range(KC):
                            high_rows(n, k)
                    if q or not first:
                        high_gated(at(n, NCH, q), (q - 1) % NCH)
                    if q < NCR:
                        act.wait_ge(s_z, at(n, NCR, q + 1))
                    else:
                        act.wait_ge(s_copy, at(n, NCH, q + 1))
                    nc.scalar.activation(ta[0:rows, q % NSL, :], za[0:rows, q % NSL, :], ACT.Tanh, scale=0.5).then_inc(s_tanh, 1)

            act.wait_ge(s_x1f, 16)
            for k in range(KC):
                high_rows(0, k)
            turn(0, True)
            with act.Fori(1, GROUPS) as n:
                turn(n, False)
            high_gated(GROUPS * NCH, NCH - 1)
            sums(GROUPS)

        @block.vector
        def _(dve):
            chain = [0]

            def link(ins):
                chain[0] += 1
                ins.then_inc(s_dve, 1)
                dve.wait_ge(s_dve, chain[0])

            nc.vector.memset(KS[:, :, :, :], 1.0).then_inc(s_ones, 1)
            dve.wait_ge(s_wload, 16 * WLOADS)
            dve.wait_ge(s_wload2, 16 * WLOADS2)
            dve.wait_ge(s_wtc, 7)
            link(nc.vector.tensor_scalar(gb_b[:, :], gb_b[:, :], 0.5, None, ALU.add))
            for b in range(B):
                link(nc.vector.memset(V[:, b, :, :, HD:2 * HD], 1.0))
            for item in SEQ:
                kind = item[0]
                if kind in S_KINDS:
                    dve.wait_ge(s_S, S_NO[item])
                    ps = psS[:, (S_NO[item] - 1) % 2, :]
                if kind == "proj":
                    _, b, m = item
                    n = 3 * b + m
                    rows = KVW if m == 0 else P
                    part = kp if m == 0 else qp[:, m - 1, :, :]
                    bias = bk[:, 0:1] if m == 0 else bq[:, m - 1:m]
                    dve.wait_ge(s_part1, n + 1)
                    if n >= 2:
                        dve.wait_ge(s_part3, n - 1)
                    nc.vector.scalar_tensor_tensor(out=rest[0:rows, n % 2, :], in0=ps[0:rows, :], scalar=bias,
                                                   in1=part[:, 0, :], op0=ALU.add, op1=ALU.subtract).then_inc(s_Sfree, 1)
                elif kind == "v":
                    b = item[1]
                    nc.vector.tensor_tensor(V[:, b, :, :, 0:HD], ps[:, 0:HALF].rearrange("p (i v d) -> p i v d", i=TT, v=NKV),
                                            bv_b[:, :].rearrange("p (v d) -> p v d", v=NKV).unsqueeze(1)
                                            .to_broadcast([P, TT, NKV, HD]), ALU.add).then_inc(s_Sfree, 1)
                elif kind == "smax":
                    _, k, n = item
                    q = HEADGROUPS[k][1]
                    i, heads, cols, dist = max_units(q)[n]
                    if n == 0 and k:
                        dve.wait_ge(s_m2, k)
                    src = ps[:, 0:len(heads) * dist].rearrange("p (h n) -> p h n", h=len(heads))[:, :, 0:cols]
                    nc.vector.tensor_reduce(out=MX[:, heads[0]:heads[-1] + 1, i - TH * q], in_=src, op=ALU.max,
                                            axis=AX_X).then_inc(s_Sfree, 1)
                    if n == len(max_units(q)) - 1:
                        dve.wait_ge(s_Sfree, S_NO[item])
                        mx = MX[:, :, :].rearrange("p h i -> p (h i)")
                        link(nc.vector.tensor_scalar(M2[:, 0, :], mx, -1.0, None, ALU.mult))
                        nc.vector.scalar_tensor_tensor(out=M2[:, 1, :], in0=mx, scalar=-1.0, in1=M2[:, 0, :],
                                                       op0=ALU.mult, op1=ALU.subtract).then_inc(s_m2, 1)
                elif kind == "mrow":
                    k = item[1]
                    if k:
                        dve.wait_ge(s_mrow, 16 * k)
                    nc.vector.tensor_copy(MT[:, :], ps[0:MROWS * G * TH, :].bitcast(BF16)[:, 0:P]).then_inc(s_Sfree, 1)
                elif kind == "norm":
                    k = item[1]
                    b, q, g = HEADGROUPS[k]
                    if g == 0 and k >= 2 * NKV:
                        dve.wait_ge(s_T, T_NO[("yT", b - 1, q * TH + TH - 1)])
                    if k:
                        dve.wait_ge(s_Sfree, S_NO[("norm", k - 1)])
                    ps = ps[:, 0:HALF].rearrange("p (i h w) -> p i h w", i=TH, h=G)
                    rc4 = rc[:, :].rearrange("p (i h a) -> p i h a", i=TH, a=1)
                    link(nc.vector.reciprocal(rc4, ps[:, :, :, HD:HD + 1]))
                    nc.vector.tensor_tensor(y[:, q, :, g * KVW:(g + 1) * KVW].rearrange("p i (h d) -> p i h d", h=G),
                                            ps[:, :, :, 0:HD], rc4.to_broadcast([P, TH, G, HD]), ALU.mult).then_inc(s_Sfree, 1)
                elif kind == "cp":
                    _, b, i = item
                    n = CP_NO[item] - 1
                    if n >= 3:
                        dve.wait_ge(s_x1, n - 2)
                    dve.wait_ge(s_res, b + 1)
                    nc.vector.tensor_tensor(r[:, n % 3, :], ps[:, 0:C], xn[:, b, i, :], ALU.add).then_inc(s_Sfree, 1)
                    dve.wait_ge(s_Sfree, S_NO[item])
                    link(nc.vector.bn_stats(st1[:, :], r[:, n % 3, :]))
                    link(nc.vector.bn_aggr(mv1[:, n % 3, :], st1[:, :]))
                    nc.vector.tensor_scalar(ve1[:, n % 3, :], mv1[:, n % 3, 1:2], EPS, None, ALU.add).then_inc(s_var, 1)
                elif kind == "ln":
                    _, b, i = item
                    n = LN_NO[item] - 1
                    dve.wait_ge(s_rstd, n + 1)
                    if n >= 3:
                        prev = [it for it in SEQ if it[0] == "x1T"][n - 3]
                        dve.wait_ge(s_T, T_NO[prev])
                        dve.wait_ge(s_x1st[n % 3], 16 * (n // 3))
                    nc.vector.tensor_scalar(x1[:, n % 3, :], r[:, n % 3, :], mv1[:, n % 3, 0:1], rs1[:, n % 3, 0:1],
                                            ALU.subtract, ALU.mult).then_inc(s_x1, 1)
                elif kind == "gate":
                    nc.vector.tensor_copy(lg[:, :, :], ps[:, 0:TH * NE].rearrange("p (i e) -> p i e", i=TH)).then_inc(s_Sfree, 1)
                elif kind == "route":
                    _, b, q = item
                    h = b * NHALF + q
                    dve.wait_ge(s_th, h + 1)
                    if h:
                        dve.wait_ge(s_pr3, h)
                    link(nc.vector.scalar_tensor_tensor(
                        out=sc[:, :, :], in0=th[:, :, :], scalar=0.5,
                        in1=gb_b[:, :].unsqueeze(1).to_broadcast([P, TH, NE]), op0=ALU.mult, op1=ALU.add))
                    for i in range(TH):
                        last = nc.vector.max(out=top[:, i, :], in_=sc[:, i, :])
                    link(last)
                    for i in range(TH):
                        last = nc.vector.max_index(out=idx[:, i, :], in_max=top[:, i, :], in_values=sc[:, i, :])
                    link(last)
                    link(nc.vector.tensor_copy(idf[:, :, :], idx[:, :, :]))
                    link(nc.vector.tensor_tensor(
                        hit[:, :, :, :], iota_b[:, :].unsqueeze(1).unsqueeze(3).to_broadcast([P, TH, NE, TOPK]),
                        idf[:, :, 0:TOPK].unsqueeze(2).to_broadcast([P, TH, NE, TOPK]), ALU.is_equal))
                    link(nc.vector.tensor_reduce(out=pick[:, :, :], in_=hit[:, :, :, :], op=ALU.add, axis=AX_X))
                    link(nc.vector.tensor_reduce(out=tsum[:, :, 0], in_=top[:, :, 0:TOPK], op=ALU.add, axis=AX_X))
                    link(nc.vector.reciprocal(trec[:, :, :], tsum[:, :, :]))
                    link(nc.vector.tensor_tensor(prt[:, :, :], pick[:, :, :], sc[:, :, :], ALU.mult))
                    link(nc.vector.scalar_tensor_tensor(out=prt[:, :, :], in0=prt[:, :, :], scalar=0.5,
                                                        in1=trec[:, :, :].to_broadcast([P, TH, NE]),
                                                        op0=ALU.mult, op1=ALU.mult))
                    if h:
                        prev = ("pT", b, 0) if q else ("pT", b - 1, 1)
                        dve.wait_ge(s_T, T_NO[prev])
                    for k in range(3):
                        part = pr3[:, :, k * NE:(k + 1) * NE]
                        cp = nc.vector.tensor_copy(part, prt[:, :, :])
                        if k == 2:
                            cp.then_inc(s_pr3, 1)
                            break
                        link(cp)
                        link(nc.vector.tensor_tensor(prt[:, :, :], prt[:, :, :], part, ALU.subtract))
            dve.drain().then_inc(s_attdone, 1)
            dve.wait_ge(s_attdone, 5)
            dve.sem_inc(s_g, 2)

            def low_rows(k, n):
                dve.wait_ge(s_xh, n)
                nc.vector.tensor_tensor(xl[:, k, :], x1f[:, k, :], xh[:, k, :].bitcast(F32), ALU.subtract).then_inc(s_xl, 1)

            def residual(n, m):
                dve.wait_ge(s_x1r, n * 16)
                dve.wait_ge(s_back, n * 2 - 1 + m)
                nc.vector.tensor_tensor(x1r[:, 2 * m:2 * m + 2, :], psB[:, 1 - m, :].rearrange("p (i c) -> p i c", i=2),
                                        x1r[:, 2 * m:2 * m + 2, :], ALU.add).then_inc(s_resid, 1)

            def statistics(n):
                dve.wait_ge(s_resid, n * 2)
                for i in range(TH):
                    nc.vector.bn_stats(st2[:, i, :], x1r[:, i, :]).then_inc(s_st2, 1)

            def variances(n):
                dve.wait_ge(s_st2, n * 2 * TH - TH)
                dve.sem_inc(s_pass, 1)
                for i in range(TH):
                    nc.vector.bn_aggr(mv2[:, i, :], st2[:, i, :]).then_inc(s_st2, 1)
                dve.wait_ge(s_st2, n * 2 * TH)
                nc.vector.tensor_scalar(ve2[:, :], mv2[:, :, 1], EPS, None, ALU.add).then_inc(s_var2, 1)

            def normalise(n):
                dve.wait_ge(s_rstd2, n * 1)
                for i in range(TH):
                    nc.vector.tensor_scalar(x1r[:, i, :], x1r[:, i, :], mv2[:, i, 0:1], rs2[:, i:i + 1],
                                            ALU.subtract, ALU.mult).then_inc(s_norm2, 1)

            def turn(n, first):
                for q in range(NCH):
                    rows = LAST if q == NCH - 1 else P
                    a, t = za[0:rows, q % NSL, :], ta[0:rows, q % NSL, :]
                    h2 = psH[0:rows, q % 2, 1, :]
                    if q < NCR:
                        dve.wait_ge(s_copy, at(n, NCH, q + 1))
                        nc.vector.tensor_tensor(a, a, h2, ALU.mult).then_inc(s_z, 1)
                    if q == NCH - 1:
                        for k in range(KC):
                            low_rows(k, at(n, KC, KC + k + 1))
                    if not first:
                        if q == 5:
                            residual(n, 0)
                        if q == 6:
                            statistics(n)
                        if q == 7:
                            variances(n)
                        if q == 8:
                            normalise(n)
                    dve.wait_ge(s_tanh, at(n, NCH, q + 1))
                    nc.vector.scalar_tensor_tensor(out=t, in0=t, scalar=1.0, in1=a, op0=ALU.add, op1=ALU.mult).then_inc(s_w, 1)
                    if q == 5 and not first:
                        residual(n, 1)
                    dve.wait_ge(s_w, at(n, NCH, q + 1))
                    if q < NCR:
                        dve.wait_ge(s_b, at(n, NCR, q + 1))
                        nc.vector.tensor_tensor(a, t, psB[:, q % 2, :], ALU.mult).then_inc(s_g, 1)
                    else:
                        nc.vector.scalar_tensor_tensor(out=a, in0=h2, scalar=0.5, in1=t, op0=ALU.mult, op1=ALU.mult).then_inc(s_g, 1)

            for k in range(KC):
                low_rows(k, k + 1)
            turn(0, True)
            with dve.Fori(1, GROUPS) as n:
                turn(n, False)
            residual(GROUPS, 0)
            residual(GROUPS, 1)
            statistics(GROUPS)
            variances(GROUPS)
            normalise(GROUPS)

        @block.tensor
        def _(pe):
            mm = nc.tensor.matmul

            pe.wait_ge(s_wload, 16 * WLOADS)
            pe.wait_ge(s_wload2, 16 * WLOADS2)
            pe.wait_ge(s_const, 7)
            pe.wait_ge(s_ones, 1)
            for k in range(KC):
                for m in range(KC):
                    c = k * C + m * P
                    mm(psT[:, 0, c:c + P], wq_n[:, m, k * P:(k + 1) * P], rq[:, m, :], start=True, stop=True)
                    mm(psT[:, 1, c:c + P], cp_n[:, m, k * P:(k + 1) * P], ident[:, :], start=True, stop=True)
                c = k * KVW
                mm(psT[:, 2, c:c + KVW], wk_n[:, k * P:(k + 1) * P], rk[:, :], start=True, stop=True)
                c = (KC + k) * KVW
                mm(psT[:, 2, c:c + KVW], wv_n[:, k * P:(k + 1) * P], ident[0:KVW, 0:KVW], start=True, stop=True)
                c = 2 * KC * KVW + k * NE
                mm(psT[:, 2, c:c + NE], gw_n[:, k * P:(k + 1) * P], ident[0:NE, 0:NE], start=True, stop=True)
            c = 2 * KC * KVW + 32
            for m in range(KC):
                mm(psT[:, 2, c + m:c + m + 1], rq[:, m, :], bq_n[:, m:m + 1], start=True, stop=True)
            mm(psT[0:KVW, 2, c + 2:c + 3], rk[:, :], bk_n[:, :], start=True, stop=True).then_inc(s_wt, 1)
            pe.wait_ge(s_wtc, 7)

            for item in SEQ:
                kind = item[0]
                if kind in S_KINDS:
                    if S_NO[item] > 2:
                        pe.wait_ge(s_Sfree, S_NO[item] - 2)
                    ps = psS[:, (S_NO[item] - 1) % 2, :]
                elif kind in T_KINDS:
                    if T_NO[item] > 3:
                        pe.wait_ge(s_Tfree, T_NO[item] - 3)
                    ps = psT[:, (T_NO[item] - 1) % 3, :]
                if kind == "st":
                    _, k, n, h = item
                    b, q, g = HEADGROUPS[k]
                    j, c0, diag = exp_steps(q)[n]
                    if (n, h) == (0, 0):
                        pe.wait_ge(s_mrow, 16 * (k + 1))
                    mm(ps[:, 0:HALF - c0], KS[:, b, g, j * P:(j + 1) * P],
                       QS[:, (k // 2) % NSLOT, g % 2 * G + h, c0:HALF], start=True, stop=True).then_inc(s_T, 1)
                elif kind == "pv":
                    _, k, n = item
                    b, q, g = HEADGROUPS[k]
                    j, c0, diag = exp_steps(q)[n]
                    if n == 0 and k:
                        pe.wait_ge(s_evac, k)
                    st = ("st", k, n, G - 1)
                    if diag:
                        pe.wait_ge(s_sel, SEL_NO[st])
                    else:
                        pe.wait_ge(s_Tfree, T_NO[st])
                    for h in range(G):
                        last = mm(psO[32 * h:32 * h + 32, c0:HALF], V[:, b, j, g, :],
                                  prob[:, (PV_NO[item] - 1) % NPROB, h, 0:HALF - c0],
                                  start=(n == 0), stop=(n == len(exp_steps(q)) - 1))
                    last.then_inc(s_pv, 1)
                elif kind == "smax":
                    _, k, n = item
                    b, q, g = HEADGROUPS[k]
                    i, heads, cols, dist = max_units(q)[n]
                    if n == 0:
                        s = k // 2
                        pe.wait_ge(s_kload[b], 16 * len(PAIRS))
                        pe.wait_ge(s_qload[s % NSLOT], 16 * len(PAIRS) * (s // NSLOT + 1))
                    for e, h in enumerate(heads):
                        for c in range(0, cols, HALF):
                            w = min(HALF, cols - c)
                            mm(ps[:, e * dist + c:e * dist + c + w],
                               QS[0:ROWS, (k // 2) % NSLOT, g % 2 * G + h, (i - TH * q) * P:(i - TH * q + 1) * P],
                               KS[0:ROWS, b, g, c:c + w], start=True, stop=(c + w < cols))
                        d = e * dist + i * P
                        last = mm(ps[:, d:d + P], ident_b[:, :], mask_b[:, :], start=False, stop=True)
                    last.then_inc(s_S, 1)
                elif kind == "mrow":
                    pe.wait_ge(s_m2, item[1] + 1)
                    nc.tensor.transpose(ps[0:MROWS * G * TH, :].bitcast(BF16)[:, 0:P], M2[:, :, :].rearrange("p s r -> p (s r)"),
                                        ident_b[:, :]).then_inc(s_S, 1)
                elif kind == "norm":
                    k = item[1]
                    pe.wait_ge(s_evac, k + 1)
                    for i in range(TH):
                        last = nc.tensor.transpose(ps[:, i * P:(i + 1) * P], O[:, k % 2, i * P:(i + 1) * P], ident[:, :])
                    last.then_inc(s_S, 1)
                elif kind == "xT":
                    _, b, k, half = item
                    pe.wait_ge(s_x[b], 16)
                    for i in range(TH):
                        last = nc.tensor.transpose(ps[:, i * P:(i + 1) * P], xn[:, b, half * TH + i, k * P:(k + 1) * P], ident[:, :])
                    last.then_inc(s_T, 1)
                elif kind == "proj":
                    _, b, m = item
                    rows = KVW if m == 0 else P
                    wT = wkT if m == 0 else wqT[:, :, (m - 1) * P:m * P]
                    pe.wait_ge(s_Tfree, T_NO[("xT", b, KC - 1, NHALF - 1)])
                    for half in range(NHALF):
                        for k in range(KC):
                            last = mm(ps[0:rows, half * HALF:(half + 1) * HALF], wT[:, k, :],
                                      xT[:, k, half * HALF:(half + 1) * HALF], start=(k == 0), stop=(k == KC - 1))
                    last.then_inc(s_S, 1)
                elif kind == "v":
                    for i in range(TT):
                        for k in range(KC):
                            last = mm(ps[:, i * KVW:(i + 1) * KVW], xT[:, k, i * P:(i + 1) * P], wvT[:, k, :],
                                      start=(k == 0), stop=(k == KC - 1))
                    last.then_inc(s_S, 1)
                elif kind == "yT":
                    _, b, i = item
                    k = (b * NHALF + i // TH) * NKV + NKV - 1
                    pe.wait_ge(s_Sfree, S_NO[("norm", k)])
                    for k in range(KC):
                        last = nc.tensor.transpose(ps[:, k * P:(k + 1) * P], y[:, i // TH, i % TH, k * P:(k + 1) * P], ident[:, :])
                    last.then_inc(s_T, 1)
                elif kind == "cp":
                    _, b, i = item
                    pe.wait_ge(s_Tfree, T_NO[("yT", b, i)])
                    for k in range(KC):
                        last = mm(ps[:, 0:C], yT[:, i % 2, k, :], cpT[:, k, :], start=(k == 0), stop=(k == KC - 1))
                    last.then_inc(s_S, 1)
                elif kind == "x1T":
                    _, b, i = item
                    n = LN_NO[("ln", b, i)] - 1
                    pe.wait_ge(s_x1, n + 1)
                    for k in range(KC):
                        last = nc.tensor.transpose(ps[:, k * P:(k + 1) * P], x1[:, n % 3, k * P:(k + 1) * P], ident[:, :])
                    last.then_inc(s_T, 1)
                elif kind == "gate":
                    _, b, q = item
                    pe.wait_ge(s_Tfree, T_NO[("x1T", b, q * TH + TH - 1)])
                    for i in range(TH):
                        for k in range(KC):
                            last = mm(ps[:, i * NE:(i + 1) * NE], x1T[:, q, k, i * P:(i + 1) * P], gwT[:, k, :],
                                      start=(k == 0), stop=(k == KC - 1))
                    last.then_inc(s_S, 1)
                elif kind == "pT":
                    _, b, q = item
                    pe.wait_ge(s_pr3, b * NHALF + q + 1)
                    for i in range(TH):
                        last = nc.tensor.transpose(ps.bitcast(BF16)[0:PROBROWS, i * P:(i + 1) * P], pr3[:, i, :], ident_b[:, :])
                    last.then_inc(s_T, 1)
            pe.drain().then_inc(s_attdone, 1)
            pe.wait_ge(s_attdone, 5)
            pe.sem_inc(s_down, NSL)
            pe.wait_ge(s_selw, 16)

            def up(n, q, first):
                rows = LAST if q == NCH - 1 else P
                cols = slice(q * P, q * P + rows)
                if first:
                    pe.wait_ge(s_wlo, needs("up", q))
                pe.wait_ge(s_g, at(n, NCH, q + 1))
                for w in range(2):
                    for k in range(KC):
                        if q == 0 and w == 0:
                            pe.wait_ge(s_xl, at(n, KC, k + 1))
                        for e, (a, x_) in enumerate(((wuh, xh), (wuh, xl), (wul, xh))):
                            last = mm(psH[0:rows, q % 2, w, :], a[:, w, k, cols], x_[:, k, :],
                                      start=(k == 0 and e == 0), stop=(k == KC - 1 and e == 2))
                last.then_inc(s_h, 1)

            def down(n, q, first):
                rows = LAST if q == NCH - 1 else P
                if first:
                    pe.wait_ge(s_wlo, needs("down", q))
                pe.wait_ge(s_gl, at(n, NCH, NSL + q + 1))
                for k in range(KC):
                    for e, (a, g_) in enumerate(((wdh, gh), (wdh, gl), (wdl, gh))):
                        last = mm(psY[:, k, :], a[0:rows, q, k * P:(k + 1) * P], g_[0:rows, q % NSL, :],
                                  start=(q == 0 and e == 0), stop=(q == NCH - 1 and e == 2))
                last.then_inc(s_down, 1)

            def back(n, m):
                for e in range(2):
                    for k in range(KC):
                        i = 2 * m + e
                        last = nc.tensor.transpose(psB[:, 1 - m, e * C + k * P:e * C + (k + 1) * P],
                                                   yS[:, k, i * P:(i + 1) * P], ident[:, :])
                last.then_inc(s_back, 1)

            def turn(n, first):
                for q in range(NCH):
                    up(n, q, first)
                    if q == 5 and not first:
                        pe.wait_ge(s_yS, at(n, KC, 0))
                        back(n, 0)
                    if q >= DLAG:
                        if q == DLAG and not first:
                            pe.wait_ge(s_yS, at(n, KC, 0))
                        down(n, q - DLAG, first)
                    elif not first:
                        down(n - 1, NCH - DLAG + q, False)
                    if q == 5 and not first:
                        pe.wait_ge(s_g, at(n, NCH, 2 + q))
                        back(n, 1)
                    if q < NCR:
                        if q in (5, 6) and not first:
                            pe.wait_ge(s_resid, at(n, 2, -2 + q - 4))
                            pe.sem_inc(s_pass, 1)
                        mm(psB[:, q % 2, :], sel[:, q, :], probT[:, bass.ds(n * HALF, HALF)],
                           start=True, stop=True).then_inc(s_b, 1)

            turn(0, True)
            with pe.Fori(1, GROUPS) as n:
                turn(n, False)
            for q in range(NCH - DLAG, NCH):
                down(GROUPS - 1, q, False)
            pe.wait_ge(s_yS, GROUPS * KC)
            for m in range(2):
                back(GROUPS, m)


_INS = ['L0_attn_x', 'L0_attn_wq_w', 'L0_attn_wq_b', 'L0_attn_wk_w', 'L0_attn_wk_b', 'L0_attn_wv_w', 'L0_attn_wv_b',
        'L0_attn_cp_w', 'L0_attn_cp_b', 'L0_ffn_gate_w', 'L0_ffn_gate_b', 'L0_ffn_w1_shared', 'L0_ffn_w2_shared',
        'L0_ffn_w3_shared', 'L0_ffn_w1_routed', 'L0_ffn_w2_routed', 'L0_ffn_w3_routed']


def shape_constants():
    half = HD // 2
    theta = 1.0 / 10000.0 ** (np.arange(half, dtype=np.float32) * 2.0 / HD)

    def rotation(heads, per, scale):
        out = np.zeros((heads * HD, per * HD), np.float32)
        for h in range(heads):
            for i in range(half):
                c, s = scale * np.cos(h * theta[i]), scale * np.sin(h * theta[i])
                even, odd = h * HD + 2 * i, h * HD + 2 * i + 1
                to_even, to_odd = 2 * i * per + h % per, (2 * i + 1) * per + h % per
                out[even, to_even], out[odd, to_even] = c, -s
                out[odd, to_odd], out[even, to_odd] = c, s
        return out

    owner = (np.arange(NCR * P) // HID)[None, :] == (np.arange(PROBROWS) % NE)[:, None]
    bf16_one = np.where(owner, 0x3F80, 0).astype(np.uint16)
    return [("rot_q", rotation(NH, 8, HD ** -0.5)), ("rot_k", rotation(NKV, NKV, 1.0)),
            ("expert_of", bf16_one), ("iota_e", np.arange(NE, dtype=np.float32))]


def kernel(**inputs):
    import numpy as _np
    import concourse.bacc as _bacc
    from concourse import mybir as _mybir
    from concourse.bass_utils import run_bass_kernel_spmd as _run

    nc = _bacc.Bacc("TRN2", target_bir_lowering=False, num_devices=1)
    arrays, args = {}, []
    for name, a in [(n, _np.ascontiguousarray(inputs[n])) for n in _INS] + shape_constants():
        if name == 'L0_attn_x':
            a = a.reshape(B * T, C)
        arrays[f"in_{name}_dram"] = a
        args.append(nc.dram_tensor(f"in_{name}_dram", a.shape, _mybir.dt.from_np(a.dtype), kind="ExternalInput").ap())
    args.append(nc.dram_tensor("out_0_dram", (B * T, C), _mybir.dt.float32, kind="ExternalOutput").ap())
    attention_moe(nc, *args)
    r = _run(nc, [arrays], core_ids=[0])
    return r.results[0]["out_0_dram"].reshape(B, T, C)
```

```python
from contextlib import ExitStack

import concourse.bass as bass
import numpy as np
from concourse import mybir

F32 = mybir.dt.float32
F32R = mybir.dt.float32r
BF16 = mybir.dt.bfloat16
U16 = mybir.dt.uint16
U32 = mybir.dt.uint32
ALU = mybir.AluOpType
ACT = mybir.ActivationFunctionType
AX_X = mybir.AxisListType.X

P = 128
B, T, C = 2, 1024, 256
NH, G = 16, 4
NKV = NH // G
HD = C // NH
KVW = NKV * HD
KC = C // P
TT = T // P
HALF = 512
NHALF = T // HALF
TH = HALF // P
NE, HID, TOPK = 16, 176, 4
HALL = (NE + 1) * HID
NCH = -(-HALL // P)
NCR = NE * HID // P
LAST = HALL - (NCH - 1) * P
EPS = 1e-5
NEG = -1e30
GROUPS = B * T // HALF
PROBROWS = 3 * NE

PAIRS = ((0, 0), (0, 1), (0, 2), (1, 0), (1, 1), (2, 0))
ROWS = len(PAIRS) * HD
MROWS = 2
QROWS = ROWS + MROWS
NSLOT = 3
NPROB = 3
NSL = 3
assert NHALF * NKV == TT
NREST = 4
DLAG = 2
NSTG = 3
WLOADS, WLOADS1, WLOADS2 = 7, 3, 4

HEADGROUPS = [(b, q, g) for b in range(B) for q in range(NHALF) for g in range(NKV)]
NK = len(HEADGROUPS)


def max_units(q):
    if q:
        return [(i, (h,), (i + 1) * P, 2 * HALF) for i in range(TH, TT) for h in range(G)]
    units = [(0, (0, 1, 2, 3), P, P), (1, (0, 1, 2, 3), 2 * P, 2 * P)]
    for i in (2, 3):
        units += [(i, (0, 1), (i + 1) * P, HALF), (i, (2, 3), (i + 1) * P, HALF)]
    return units


def exp_steps(q):
    return [(j, max(0, P * (j - TH * q)), j >= TH * q) for j in range(TH * (q + 1))]


def first_items(b):
    items = [("xT", b, k, 0) for k in range(KC)] + [("proj", b, 0, 0), ("proj", b, 1, 0)]
    items += [("xT", b, k, 1) for k in range(KC)]
    if b == 0:
        items = [("wT", 0), ("wT", 1)] + items + [("wT", 2)]
    return items + [("v", b), ("proj", b, 2, 0)]


def later_items(b):
    return [("proj", b, m, 1) for m in range(KC + 1)] + ([("wT", 3)] if b == 0 else [])


def rows_items(b, q):
    items = []
    for s in range(TH + 3):
        for lag, name in ((0, "yT"), (1, "cp"), (2, "ln"), (3, "x1T")):
            if 0 <= s - lag < TH:
                items.append((name, b, q * TH + s - lag))
    return items + [("gate", b, q), ("route", b, q), ("pT", b, q)]


S_KINDS = ("proj", "v", "smax", "mrow", "norm", "cp", "gate")
T_KINDS = ("wT", "xT", "st", "yT", "x1T", "pT")
STEPS = [(k, n) for k, (_, q, _) in enumerate(HEADGROUPS) for n in range(len(exp_steps(q)))]
STEP_NO = {s: n for n, s in enumerate(STEPS)}

HOP = 0.2
LAND = 2.3


def span(kind, item):
    if kind == "xT":
        return 0.25, 0.5, 0
    if kind == "proj":
        return 1.7, 0.5, 0.65
    if kind == "v":
        return 1.8, 0, 0.6
    if kind == "smax":
        q = HEADGROUPS[item[1]][1]
        i, heads, n, _ = max_units(q)[item[2]]
        extra = 0.55 if item[2] == len(max_units(q)) - 1 else 0
        return len(heads) * (n / 2400 + 0.06), 0, (len(heads) * n + 62) / 960 + extra
    if kind == "mrow":
        return 0.06, 0, 0.15
    if kind in ("st", "pv"):
        n = HALF - exp_steps(HEADGROUPS[item[1]][1])[item[2]][1]
        return (n / 2400, (n + 62) / 1200, 0) if kind == "st" else (4 * n / 2400 + 0.07, 0, 0)
    return {"wT": (2.0, 0.7, 0), "split": (0, 0.5, 0), "evac": (0, 0.5, 0), "norm": (0.45, 0, 0.65), "yT": (0.2, 0.27, 0),
            "cp": (0.9, 0, 1.1), "ln": (0, 0, 0.33), "x1T": (0.2, 0.27, 0), "gate": (0.45, 0, 0.14),
            "route": (0, 0.15, 3.6), "pT": (0.25, 0.48, 0), "kload": (0, 0, 0), "qload": (0, 0, 0)}[kind]


def plan(pace=1.0, lead=4):
    seq, done = [], {}
    clock = {"pe": 8.0, "act": 8.0, "dve": 10.0, "sp": 8.0, "pool": 8.0}
    rings = {"T": [], "S": []}

    def ready(item):
        kind = item[0]
        need = []
        if kind == "proj":
            _, b, m, half = item
            need = [("xT", b, KC - 1, half), ("wT", 1)]
            if b:
                need += [("kload", b - 1, half), ("qload", 2 * half), ("qload", 2 * half + 1)]
        elif kind == "v":
            need = [("xT", item[1], KC - 1, NHALF - 1), ("wT", 2)]
        elif kind == "xT" and item[1]:
            need = [("v", item[1] - 1), ("proj", item[1] - 1, KC, 1)]
        elif kind == "split":
            need = [("proj",) + item[1:]]
        elif kind == "kload":
            need = [("split", item[1], 0, item[2])]
            if item[1:] == (0, 0):
                need.append(("split", 0, 1, 0))
        elif kind == "qload":
            s = item[1]
            b, q, g = HEADGROUPS[2 * s]
            need = [("split", b, 1 + g // 2, q)]
            if s >= NSLOT:
                last = 2 * (s - NSLOT) + 1
                need.append(("st", last, len(exp_steps(HEADGROUPS[last][1])) - 1, G - 1))
        elif kind == "smax":
            b, q, _ = HEADGROUPS[item[1]]
            need = [("kload", b, q), ("qload", item[1] // 2)]
        elif kind == "mrow":
            need = [("smax", item[1], len(max_units(HEADGROUPS[item[1]][1])) - 1)]
            if item[1]:
                need.append(("mrow", item[1] - 1))
        elif kind == "st":
            _, k, n, h = item
            need = [("mrow", k)]
            step = STEP_NO[(k, n)]
            if step >= NPROB:
                need.append(("pv",) + STEPS[step - NPROB])
        elif kind == "pv":
            _, k, n = item
            need = [("st", k, n, G - 1), ("v", HEADGROUPS[k][0])]
            if n == 0 and k:
                need.append(("evac", k - 1))
        elif kind == "evac":
            need = [("pv", item[1], len(exp_steps(HEADGROUPS[item[1]][1])) - 1)]
            if item[1] >= 2:
                need.append(("norm", item[1] - 2))
        elif kind == "norm":
            need = [("evac", item[1])]
        elif kind == "yT":
            _, b, i = item
            need = [("norm", (b * NHALF + i // TH) * NKV + NKV - 1)]
        elif kind == "cp":
            need = [("yT",) + item[1:], ("wT", 3)]
        elif kind == "ln":
            need = [("cp",) + item[1:]]
        elif kind == "x1T":
            need = [("ln",) + item[1:]]
        elif kind == "gate":
            need = [("x1T", item[1], item[2] * TH + TH - 1)]
        elif kind == "route":
            need = [("gate",) + item[1:]]
        elif kind == "pT":
            need = [("route",) + item[1:]]
        if any(n not in done for n in need):
            return None
        at_ = max([done[n] for n in need] + [0.0])
        if kind in S_KINDS and len(rings["S"]) >= 2:
            at_ = max(at_, rings["S"][-2])
        if kind in T_KINDS and len(rings["T"]) >= 3:
            at_ = max(at_, rings["T"][-3])
        return at_

    def start(item):
        t = ready(item)
        if t is None:
            return None
        kind = item[0]
        if kind in ("split", "evac"):
            return max(t, clock["act"])
        if kind == "ln":
            return max(t, clock["dve"])
        if kind == "route":
            return max(t, clock["dve"] - 0.4)
        if kind in ("kload", "qload"):
            return max(t, clock["sp"])
        return max(t, clock["pe"])

    def put(item):
        kind = item[0]
        t = start(item)
        pe, act, dve = span(kind, item)
        end = t
        if pe:
            clock["pe"] = end = t + pe
        if act:
            clock["act"] = end = max(clock["act"], end + HOP) + act
        if dve:
            clock["dve"] = end = max(clock["dve"], end + HOP) + dve
        if kind in T_KINDS:
            rings["T"].append(end + HOP)
        if kind in S_KINDS:
            rings["S"].append(end + HOP)
        end += HOP
        if kind == "split":
            clock["pool"] = end = max(clock["pool"], end) + 1.2
        elif kind == "cp":
            clock["pool"] = end = max(clock["pool"], end) + 0.65
        elif kind == "st" and item[3] == G - 1 and exp_steps(HEADGROUPS[item[1]][1])[item[2]][2]:
            clock["pool"] = end = max(clock["pool"], end) + 0.75
        elif kind in ("kload", "qload"):
            clock["sp"] = end = t if item == ("qload", 0) else t + 0.65 * len(PAIRS)
            end += LAND
        elif kind == "mrow":
            clock["sp"] = max(clock["sp"], end) + 0.65
            end = clock["sp"] + LAND - 0.65
        elif kind in ("ln", "gate"):
            clock["sp"] = max(clock["sp"], end) + 0.65
        done[item] = end
        seq.append(item)

    exps = [("st", k, n, h) for k, n in STEPS for h in range(G)]
    pvs = [("pv", k, n) for k, n in STEPS]
    loads = []
    for s in range(NK // 2):
        b, q, g = HEADGROUPS[2 * s]
        if g == 0:
            loads.append(("kload", b, q))
        loads.append(("qload", s))
    ahead = first_items(0)
    for k in range(NK):
        if k == 2:
            ahead += later_items(0)
        if k == NK // 2 - lead:
            ahead += first_items(1)
        if k == NK // 2 + 1:
            ahead += later_items(1)
        ahead += [("smax", k, n) for n in range(len(max_units(HEADGROUPS[k][1])))] + [("mrow", k)]
    splits = [("split",) + i[1:] for i in ahead if i[0] == "proj"]
    evacs = [("evac", k) for k in range(NK)]
    norms, tiles, lns = [], [], []
    for k, (b, q, g) in enumerate(HEADGROUPS):
        norms.append(("norm", k))
        if g == NKV - 1:
            norms += rows_items(b, q) if k < NK - 1 else []
    streams = [splits, loads, evacs, ahead, pvs, norms, exps]
    while any(streams):
        best = None
        for rank, stream in enumerate(streams):
            if not stream:
                continue
            t = start(stream[0])
            if t is None:
                continue
            wait = max(0.0, t - clock["pe"])
            for engine, kinds in (("act", ("split", "evac")), ("dve", ("ln", "route"))):
                if stream[0][0] in kinds:
                    wait = max(0.0, ready(stream[0]) - max(clock[engine], clock["pe"]))
            if stream is ahead and exps and clock["dve"] - clock["pe"] > pace:
                wait = max(wait, 0.3)
            key = (wait if wait > 0.05 else 0.0, rank)
            if best is None or key < best[0]:
                best = (key, stream)
        item = best[1].pop(0)
        put(item)
        if item == ("evac", NK - 1):
            seq.append(("begin",))
            seq += [("wsplit", n) for n in range(NSTG)]
        if item == ("st", NK - 2, 0, 0):
            assert ("proj", B - 1, KC, 1) in done
            seq.append(("open",))
            seq += [("xsplit", k) for k in range(KC)]
    return seq


def rows_steps():
    steps = []
    for item in rows_items(B - 1, NHALF - 1):
        if item[0] == "pT":
            steps += [[]] * 2
        if item[0] == "ln":
            steps[-1] = steps[-1] + [item]
        else:
            steps.append([item])
    return steps


SEQ = plan()
STEPS_LATE = rows_steps()
LATE = [item for step in STEPS_LATE for item in step]
LASTPT = LATE[-1]


def late(q, second):
    return STEPS_LATE[2 * q + second] if 2 * q + second < len(STEPS_LATE) else []





def count(*kinds):
    return {item: n + 1 for n, item in enumerate(i for i in SEQ + LATE if i[0] in kinds)}


S_NO, T_NO = count(*S_KINDS), count(*T_KINDS)
BEFORE_LATE = {"S": sum(i[0] in S_KINDS for i in SEQ), "T": sum(i[0] in T_KINDS for i in SEQ)}
PV_NO, EVAC_NO = count("pv"), count("evac")
PROJ_NO, CP_NO, LN_NO = count("proj"), count("cp"), count("ln")
SEL_NO = {item: n + 1 for n, item in enumerate(
    i for i in SEQ if i[0] == "st" and i[3] == G - 1 and exp_steps(HEADGROUPS[i[1]][1])[i[2]][2])}

WUNITS = sorted(
    [("up", e, max(0, -(-(HID * e - P + 1) // P))) for e in range(NE + 1)]
    + [("down", c, 2 * c + DLAG) for c in range(NCR // 2)]
    + [("down", NCR // 2, NCR + DLAG), ("down", NCR // 2 + 1, NCR + DLAG)], key=lambda u: u[2])


def needs(kind, chunk):
    if kind == "up":
        top = (min(P * (chunk + 1), HALL) - 1) // HID
    else:
        top = chunk // 2 if chunk < NCR else NCR // 2 + chunk - NCR
    return 1 + max(n for n, u in enumerate(WUNITS) if u[0] == kind and u[1] <= top)


def chunk_units(q):
    return [n for n, u in enumerate(WUNITS) if n >= NSTG and (u[2] == q + 2 or (q == 0 and u[2] < 2))]


def at(turn, per, n):
    return turn * per + n


def attention_moe(nc, x, wq_w, wq_b, wk_w, wk_b, wv_w, wv_b, cp_w, cp_b, gate_w, gate_b,
                  w1_shared, w2_shared, w3_shared, w1_routed, w2_routed, w3_routed,
                  rot_q, rot_k, expert_of, iota_e, out):
    x1t_dram = nc.dram_tensor("x1t_scratch", (C, B * T), F32, kind="Internal").ap()
    x1_dram = nc.dram_tensor("x1_scratch", (B * T, C), F32, kind="Internal").ap()

    ctx = ExitStack()
    with ctx:
        def sem(name):
            return ctx.enter_context(nc.semaphore(name))

        used = {}

        def sb(name, shape, dt=F32, stack=ctx):
            width = 2 if dt is BF16 else 4
            used[stack] = used.get(stack, 0) + -(-int(np.prod(shape[1:])) * width // 32) * 32
            return stack.enter_context(nc.sbuf_tensor(name, shape, dt))

        def pb(name, shape, dt=F32, stack=ctx):
            return stack.enter_context(nc.psum_tensor(name, shape, dt))

        ident = sb("ident", [P, P])
        eps_pow = sb("eps_pow", [P, 1])
        stage = sb("stage", [P, NSTG, 2 * KC * HID])
        probT = sb("probT", [PROBROWS, B * T], BF16)

        ffn = ExitStack()
        x1f = sb("x1f", [P, KC, HALF], F32, ffn)
        xh = sb("xh", [P, KC, HALF], F32R, ffn)
        xl = sb("xl", [P, KC, HALF], F32R, ffn)
        sel = sb("sel", [PROBROWS, NCR, P], BF16, ffn)
        wuh = sb("wuh", [P, 2, KC, HALL], F32R, ffn)
        wul = sb("wul", [P, 2, KC, HALL], F32R, ffn)
        za = sb("za", [P, NSL, HALF], F32, ffn)
        ta = sb("ta", [P, NSL, HALF], F32, ffn)
        gh = sb("gh", [P, NSL, HALF], F32R, ffn)
        gl = sb("gl", [P, NSL, HALF], F32R, ffn)
        st2 = sb("st2", [P, TH, 6], F32, ffn)
        mv2 = sb("mv2", [P, TH, 2], F32, ffn)
        ve2 = sb("ve2", [P, TH], F32, ffn)
        rs2 = sb("rs2", [P, TH], F32, ffn)
        half_pow = sb("half_pow", [P, TH], F32, ffn)
        over_router = used[ffn]
        yS = sb("yS", [P, KC, HALF], F32, ffn)
        x1r = sb("x1r", [P, TH, C], F32, ffn)
        over_rows = used[ffn]
        wd = sb("wd", [P, NCH, 2, C], F32R, ffn)
        psH = pb("psH", [P, 2, 2, HALF], F32, ffn)
        psB = pb("psB", [P, 2, HALF], F32, ffn)
        psY = pb("psY", [P, KC, HALF], F32, ffn)
        ffn.close()

        att = ExitStack()
        wq_n = sb("wq_n", [P, KC, C], F32, att)
        wk_n = sb("wk_n", [KVW, C], F32, att)
        wv_n = sb("wv_n", [KVW, C], F32, att)
        cp_n = sb("cp_n", [P, KC, C], F32, att)
        gw_n = sb("gw_n", [NE, C], F32, att)
        rq = sb("rq", [P, KC, P], F32, att)
        rk = sb("rk", [KVW, KVW], F32, att)
        bq_n = sb("bq_n", [P, KC], F32, att)
        bk_n = sb("bk_n", [KVW, 1], F32, att)
        bv_b = sb("bv_b", [P, KVW], F32, att)
        wqT = sb("wqT", [P, KC, C], F32, att)
        wkT = sb("wkT", [P, KC, KVW], F32, att)
        wvT = sb("wvT", [P, KC, KVW], F32, att)
        bq = sb("bq", [P, KC], F32, att)
        bk = sb("bk", [KVW, 1], F32, att)
        xT = sb("xT", [P, KC, T], F32, att)
        rest = sb("rest", [P, NREST, HALF], F32, att)
        qp = sb("qp", [P, KC, 3, T], BF16, att)
        kp = sb("kp", [KVW, 3, T], BF16, att)
        mask_b = sb("mask_b", [P, P], BF16, att)
        QS = sb("QS", [QROWS, NSLOT, 2 * G, HALF], BF16, att)
        KS = sb("KS", [QROWS, B, NKV, T], BF16, att)
        V = sb("V", [P, B, TT, NKV, 2 * HD], F32, att)
        prob = sb("prob", [P, NPROB, G, HALF], F32, att)
        MX = sb("MX", [P, G, TH], F32, att)
        M2 = sb("M2", [P, MROWS, G * TH], BF16, att)
        MT = sb("MT", [MROWS * G * TH, P], BF16, att)
        sb("spare1", [P, (over_router - used[att]) // 4], F32, att)
        ident_b = sb("ident_b", [P, P], BF16, att)
        cpb_b = sb("cpb_b", [P, C], F32, att)
        gwT = sb("gwT", [P, KC, NE], F32, att)
        gb_b = sb("gb_b", [P, NE], F32, att)
        iota_b = sb("iota_b", [P, NE], F32, att)
        lg = sb("lg", [P, TH, NE], F32, att)
        th = sb("th", [P, TH, NE], F32, att)
        sc = sb("sc", [P, TH, NE], F32, att)
        top = sb("top", [P, TH, 8], F32, att)
        idx = sb("idx", [P, TH, 8], U32, att)
        idf = sb("idf", [P, TH, 8], F32, att)
        hit = sb("hit", [P, TH, NE, TOPK], F32, att)
        pick = sb("pick", [P, TH, NE], F32, att)
        tsum = sb("tsum", [P, TH, 1], F32, att)
        trec = sb("trec", [P, TH, 1], F32, att)
        prt = sb("prt", [P, TH, NE], F32, att)
        pr3 = sb("pr3", [P, TH, PROBROWS], BF16, att)
        sb("spare2", [P, (over_rows - used[att]) // 4], F32, att)
        xn = [sb("xn0", [P, TT, C], F32, att)]
        y = [sb("y0", [P, TH, C], F32, att)]
        x1T = [sb("x1T0", [P, KC, HALF], F32, att)]
        over_late = used[att]
        xn.append(sb("xn1", [P, TT, C], F32, att))
        y.append(sb("y1", [P, TH, C], F32, att))
        x1T.append(sb("x1T1", [P, KC, HALF], F32, att))
        cpT = sb("cpT", [P, KC, C], F32, att)
        O = sb("O", [P, 2, HALF], F32, att)
        rc = sb("rc", [P, G * TH], F32, att)
        yT = sb("yT", [P, 2, KC, P], F32, att)
        r = sb("r", [P, 3, C], F32, att)
        st1 = sb("st1", [P, 6], F32, att)
        mv1 = sb("mv1", [P, 3, 2], F32, att)
        ve1 = sb("ve1", [P, 3, 1], F32, att)
        rs1 = sb("rs1", [P, 3, 1], F32, att)
        x1 = sb("x1", [P, 3, C], F32, att)
        psS = pb("psS", [P, 2, 2 * HALF], F32, att)
        psT = pb("psT", [P, 3, HALF], F32, att)
        psO = pb("psO", [P, HALF], F32, att)
        att.close()

        s_wload = sem("s_wload")
        s_wload1 = sem("s_wload1")
        s_const = sem("s_const")
        s_wload2 = sem("s_wload2")
        s_bias = sem("s_bias")
        s_ones = sem("s_ones")
        s_x = [[sem(f"s_xload{b}_{h}") for h in range(NHALF)] for b in range(B)]
        s_S = sem("s_S")
        s_Sfree = sem("s_Sfree")
        s_T = sem("s_T")
        s_Tfree = sem("s_Tfree")
        s_part1 = sem("s_part1")
        s_part2 = sem("s_part2")
        s_part3 = sem("s_part3")
        s_kload = [[sem(f"s_kload{b}_{h}") for h in range(NHALF)] for b in range(B)]
        s_qload = [sem(f"s_qload{i}") for i in range(NSLOT)]
        s_m2 = sem("s_m2")
        s_mrow = sem("s_mrow")
        s_res = sem("s_res")
        s_sel = sem("s_sel")
        s_pv = sem("s_pv")
        s_evac = sem("s_evac")
        s_var = sem("s_var")
        s_rstd = sem("s_rstd")
        s_x1 = sem("s_x1")
        s_th = sem("s_th")
        s_pr3 = sem("s_pr3")
        s_x1st = [sem(f"s_x1st{i}") for i in range(3)]
        s_x1tst = [sem(f"s_x1tst{i}") for i in range(2)]
        s_dve = sem("s_dve")
        s_stage = [sem(f"s_stage{i}") for i in range(NSTG)]
        s_whi = sem("s_whi")
        s_wlo = sem("s_wlo")
        s_selw = sem("s_selw")
        s_x1f = sem("s_x1f")
        s_x1r = sem("s_x1r")
        s_xh = sem("s_xh")
        s_xl = sem("s_xl")
        s_h = sem("s_h")
        s_b = sem("s_b")
        s_copy = sem("s_copy")
        s_z = sem("s_z")
        s_tanh = sem("s_tanh")
        s_w = sem("s_w")
        s_g = sem("s_g")
        s_gh = sem("s_gh")
        s_gl = sem("s_gl")
        s_down = sem("s_down")
        s_yS = sem("s_yS")
        s_back = sem("s_back")
        s_resid = sem("s_resid")
        s_st2 = sem("s_st2")
        s_var2 = sem("s_var2")
        s_rstd2 = sem("s_rstd2")
        s_norm2 = sem("s_norm2")
        s_out = sem("s_out")
        s_pass = sem("s_pass")

        block = ctx.enter_context(nc.Block())

        wd_flat = w2_routed.rearrange("e h d -> (e h) d")

        def under(n):
            return WUNITS[n][0] == "down" and (min(2 * WUNITS[n][1] + 2, NCH) * 2 * C * 4 > over_late - over_rows)

        def wunit(n):
            kind, i, _ = WUNITS[n]
            st = stage[:, n % NSTG, :]
            if kind == "up":
                c = slice(i * HID, (i + 1) * HID)
                return P, st.rearrange("p (w k h) -> p w k h", w=2, k=KC), wuh[:, :, :, c], wul[:, :, :, c]
            if i < NCR // 2:
                c = slice(2 * i, 2 * i + 2)
                return P, st[:, 0:2 * C].rearrange("p (q d) -> p q d", q=2), wd[:, c, 0, :], wd[:, c, 1, :]
            c = NCR + i - NCR // 2
            rows = P if c < NCH - 1 else LAST
            return rows, st[0:rows, 0:C], wd[0:rows, c, 0, :], wd[0:rows, c, 1, :]

        @block.sync
        def _(sp):
            def xload(b, half):
                t0 = b * T + half * HALF
                sp.dma_start(xn[b][:, half * TH:(half + 1) * TH, :],
                             x[t0:t0 + HALF, :].rearrange("(i p) c -> p i c", p=P)).then_inc(s_x[b][half], 16)

            sp.dma_start(wq_n[:, :, :], wq_w.rearrange("(m p) c -> p m c", p=P)).then_inc(s_wload, 16)
            sp.dma_start(rq[:, :, :], rot_q.rearrange("(m p) c -> p m c", p=P)).then_inc(s_wload, 16)
            xload(0, 0)
            for m in range(KC):
                sp.dma_start(bq_n[:, m:m + 1], wq_b[m * P:(m + 1) * P].rearrange("(p a) -> p a", a=1)).then_inc(s_wload, 16)
            xload(0, 1)
            sp.dma_start(wv_n[:, :], wv_w).then_inc(s_wload1, 16)

            def wload(n):
                kind, i, _ = WUNITS[n]
                rows, st, _, _ = wunit(n)
                if n >= NSTG:
                    sp.wait_ge(s_wlo, n - NSTG + 1)
                if kind == "up":
                    for w, (rt, shd) in enumerate(((w1_routed, w1_shared), (w3_routed, w3_shared))):
                        src = rt[i] if i < NE else shd
                        sp.dma_start(st[:, w, :, :], src.rearrange("(k p) h -> p k h", p=P)).then_inc(s_stage[n % NSTG], 16)
                else:
                    if i < NCR // 2:
                        src = wd_flat[2 * i * P:(2 * i + 2) * P, :].rearrange("(q p) d -> p q d", p=P)
                    else:
                        src = w2_shared[(i - NCR // 2) * P:(i - NCR // 2) * P + rows, :]
                    sp.dma_start(st, src).then_inc(s_stage[n % NSTG], 32)

            def keys_part(b, half, part):
                c = slice(half * HALF, (half + 1) * HALF)
                sp.wait_ge((s_part1, s_part2, s_part3)[part], PROJ_NO[("proj", b, 0, half)])
                if (part, half) == (0, 0):
                    sp.wait_ge(s_ones, b + 1)
                for a, pair in enumerate(PAIRS):
                    if pair[1] == part:
                        sp.dma_start(KS[a * HD:(a + 1) * HD, b, :, c], kp[:, part, c]).then_inc(s_kload[b][half], 16)

            def queries_part(s, part):
                b, q, g = HEADGROUPS[2 * s]
                m = g // 2
                sp.wait_ge((s_part1, s_part2, s_part3)[part], PROJ_NO[("proj", b, 1 + m, q)])
                for a, pair in enumerate(PAIRS):
                    if pair[0] == part:
                        sp.dma_start(QS[a * HD:(a + 1) * HD, s % NSLOT, :, :],
                                     qp[:, m, part, q * HALF:(q + 1) * HALF]).then_inc(s_qload[s % NSLOT], 16)

            def run(item):
                kind = item[0]
                if kind == "kload":
                    _, b, half = item
                    for part in range(3):
                        keys_part(b, half, part)
                        if (b, half) == (0, 0):
                            queries_part(0, part)
                elif kind == "qload":
                    s = item[1]
                    if s >= NSLOT:
                        last = 2 * (s - NSLOT) + 1
                        sp.wait_ge(s_T, T_NO[("st", last, len(exp_steps(HEADGROUPS[last][1])) - 1, G - 1)])
                    if s:
                        for part in range(3):
                            queries_part(s, part)
                    if s == 0:
                        xload(1, 0)
                        xload(1, 1)
                    if s == NK // 4:
                        for n in range(NSTG):
                            wload(n)
                elif kind == "mrow":
                    k = item[1]
                    sp.wait_ge(s_Sfree, S_NO[item])
                    g = HEADGROUPS[k][2]
                    sp.dma_start(QS[ROWS:QROWS, (k // 2) % NSLOT, g % 2 * G:(g % 2 + 1) * G, :]
                                 .rearrange("s h (i t) -> s (h i) t", t=P), MT[:, :]).then_inc(s_mrow, 16)
                elif kind == "ln":
                    n = LN_NO[item] - 1
                    sp.wait_ge(s_x1, n + 1)
                    _, b, i = item
                    sp.dma_start(x1_dram[b * T + i * P:b * T + (i + 1) * P, :], x1[:, n % 3, :]).then_inc(s_x1st[n % 3], 16)
                elif kind == "gate":
                    _, b, q = item
                    sp.wait_ge(s_Tfree, T_NO[("x1T", b, q * TH + TH - 1)])
                    t0 = b * T + q * HALF
                    sp.dma_start(x1t_dram[:, t0:t0 + HALF].rearrange("(k p) t -> p k t", p=P), x1T[q][:, :, :]).then_inc(s_x1tst[q], 16)
                elif kind == "open":
                    last = max(S_NO[("v", B - 1)], S_NO[("proj", B - 1, KC, 1)])
                    sp.wait_ge(s_Sfree, last)
                    sp.wait_ge(s_x1tst[0], 16)
                    sp.dma_start(x1f[:, :, :], x1t_dram[:, 0:HALF].rearrange("(k p) t -> p k t", p=P)).then_inc(s_x1f, 16)
                    sp.dma_start(sel[:, :, :].bitcast(U16), expert_of.rearrange("k (q p) -> k q p", p=P)).then_inc(s_selw, 16)

            for item in SEQ:
                run(item)
            nload = NSTG
            for q in range(NCH):
                for item in late(q, 0) + late(q, 1):
                    run(item)
                ahead = NSTG + sum(len(chunk_units(p)) for p in range(q + 1)) + NSTG
                while nload < min(ahead, len(WUNITS)):
                    wload(nload)
                    nload += 1
                if q == NCH // 2 + 1:
                    sp.wait_ge(s_xl, KC)
                    for q in range(2):
                        sp.wait_ge(s_x1tst[q], 16 * B)
                    for i in range(3):
                        sp.wait_ge(s_x1st[i], 16 * ((B * TT - i + 2) // 3))
                    sp.dma_start(x1f[:, :, :], x1t_dram[:, HALF:2 * HALF].rearrange("(k p) t -> p k t", p=P)).then_inc(s_x1f, 16)
                    sp.wait_ge(s_T, T_NO[LASTPT])
                    sp.dma_start(x1r[:, :, :], x1_dram[0:HALF, :].rearrange("(i p) c -> p i c", p=P)).then_inc(s_x1r, 16)

            def rows_turn(n):
                sp.wait_ge(s_norm2, at(n, TH, 0))
                sp.sem_inc(s_pass, 1)
                sp.dma_start(out[bass.ds(n * HALF - HALF, HALF), :].rearrange("(i p) c -> p i c", p=P), x1r[:, :, :]).then_inc(s_out, 16)
                sp.wait_ge(s_out, at(n, 16, 0))
                sp.sem_inc(s_pass, 1)
                sp.dma_start(x1r[:, :, :], x1_dram[bass.ds(n * HALF, HALF), :].rearrange("(i p) c -> p i c", p=P)).then_inc(s_x1r, 16)

            with sp.Fori(1, GROUPS - 1) as n:
                rows_turn(n)
                sp.wait_ge(s_xl, at(n, KC, KC))
                sp.sem_inc(s_pass, 1)
                sp.dma_start(x1f[:, :, :], x1t_dram[:, bass.ds(n * HALF + HALF, HALF)].rearrange("(k p) t -> p k t", p=P)).then_inc(s_x1f, 16)
            rows_turn(GROUPS - 1)
            sp.sem_inc(s_x1f, 16)
            for m in range(2):
                sp.wait_ge(s_norm2, TH * (GROUPS - 1) + 2 * m + 2)
                t0 = (GROUPS - 1) * HALF + m * HALF // 2
                sp.dma_start(out[t0:t0 + HALF // 2, :].rearrange("(i p) c -> p i c", p=P),
                             x1r[:, 2 * m:2 * m + 2, :]).then_inc(s_out, 16)
            sp.wait_ge(s_out, 16 * (GROUPS + 1))

        @block.gpsimd
        def _(pool):
            def low_weights(n):
                rows, st, hi, lo = wunit(n)
                pool.wait_ge(s_whi, n + 1)
                nc.gpsimd.tensor_tensor(lo, st, hi.bitcast(F32), ALU.subtract).then_inc(s_wlo, 1)

            nc.gpsimd.memset(ident[:, :], 0.0).then_inc(s_const, 1)
            nc.gpsimd.memset(ident_b[:, :], 0.0).then_inc(s_const, 1)
            nc.gpsimd.memset(mask_b[:, :], 0.0).then_inc(s_const, 1)
            pool.wait_ge(s_const, 3)
            for m in (ident, ident_b):
                nc.gpsimd.affine_select(out=m[:, :], in_=m[:, :], compare_op=ALU.not_equal, fill=1.0, base=0,
                                        pattern=[[-1, P]], channel_multiplier=1).then_inc(s_const, 1)
            nc.gpsimd.affine_select(out=mask_b[:, :], in_=mask_b[:, :], compare_op=ALU.is_ge, fill=NEG, base=0,
                                    pattern=[[-1, P]], channel_multiplier=1).then_inc(s_const, 1)
            nc.gpsimd.memset(eps_pow[:, :], -0.5).then_inc(s_const, 1)
            pool.dma_start(cp_n[:, :, :], cp_w.rearrange("(m p) c -> p m c", p=P)).then_inc(s_wload2, 16)
            pool.dma_start(cpb_b[:, :], cp_b.partition_broadcast(P)).then_inc(s_wload2, 16)
            pool.dma_start(gb_b[:, :], gate_b.partition_broadcast(P)).then_inc(s_wload2, 16)
            pool.dma_start(iota_b[:, :], iota_e.partition_broadcast(P)).then_inc(s_wload2, 16)
            def run(item):
                kind = item[0]
                if kind == "split":
                    _, b, m, half = item
                    n = PROJ_NO[("proj", b, m, half)] - 1
                    rows = KVW if m == 0 else P
                    part = (kp if m == 0 else qp[:, m - 1, :, :])[:, :, half * HALF:(half + 1) * HALF]
                    pool.wait_ge(s_part2, n + 1)
                    nc.gpsimd.tensor_tensor(part[:, 2, :], rest[0:rows, n % NREST, :], part[:, 1, :], ALU.subtract).then_inc(s_part3, 1)
                elif kind == "norm":
                    b, i = divmod(item[1], NHALF * NKV)
                    if item[1] == 0:
                        pool.wait_ge(s_wload2, 16 * WLOADS2)
                    if i == 0:
                        pool.wait_ge(s_T, T_NO[("xT", b, KC - 1, NHALF - 1)])
                    nc.gpsimd.tensor_tensor(xn[b][:, i, :], xn[b][:, i, :], cpb_b[:, :], ALU.add).then_inc(s_res, 1)
                elif item in SEL_NO:
                    _, k, n, _ = item
                    pool.wait_ge(s_Tfree, T_NO[item])
                    blk = prob[:, (PV_NO[("pv", k, n)] - 1) % NPROB, :, 0:P]
                    nc.gpsimd.affine_select(out=blk, in_=blk, compare_op=ALU.is_ge, fill=0.0, base=0,
                                            pattern=[[0, G], [1, P]], channel_multiplier=-1).then_inc(s_sel, 1)
                elif kind == "cp":
                    n = CP_NO[item] - 1
                    pool.wait_ge(s_var, n + 1)
                    nc.gpsimd.tensor_tensor(rs1[:, n % 3, :], ve1[:, n % 3, :], eps_pow[:, :], ALU.pow).then_inc(s_rstd, 1)
                elif kind == "begin":
                    pool.wait_ge(s_pv, len(PV_NO))
                    nc.gpsimd.memset(half_pow[:, :], -0.5).then_inc(s_const, 1)
                elif kind == "wsplit":
                    low_weights(item[1])

            for item in SEQ:
                run(item)
            pool.sem_inc(s_gl, NSL)

            def turn(n, first):
                for q in range(NCH):
                    if first:
                        for e in chunk_units(q):
                            low_weights(e)
                        for item in late(q, 0) + late(q, 1):
                            run(item)
                    rows = LAST if q == NCH - 1 else P
                    pool.wait_ge(s_gh, at(n, NCH, q + 1))
                    nc.gpsimd.tensor_tensor(gl[0:rows, q % NSL, :], za[0:rows, q % NSL, :],
                                            gh[0:rows, q % NSL, :].bitcast(F32), ALU.subtract).then_inc(s_gl, 1)
                    if q == 7 and not first:
                        spread2(at(n, 1, 0))

            def spread2(n):
                pool.wait_ge(s_var2, n)
                nc.gpsimd.tensor_tensor(rs2[:, :], ve2[:, :], half_pow[:, :], ALU.pow).then_inc(s_rstd2, 1)

            pool.wait_ge(s_const, 8)
            turn(0, True)
            with pool.Fori(1, GROUPS) as n:
                turn(n, False)
            for m in range(2):
                pool.wait_ge(s_var2, GROUPS + m)
                t = slice(2 * m, 2 * m + 2)
                nc.gpsimd.tensor_tensor(rs2[:, t], ve2[:, t], half_pow[:, t], ALU.pow).then_inc(s_rstd2, 1)

        @block.scalar
        def _(act):
            def high_weights(n):
                rows, st, hi, lo = wunit(n)
                act.wait_ge(s_stage[n % NSTG], 32 * (n // NSTG + 1))
                nc.scalar.copy(hi, st).then_inc(s_whi, 1)

            def high_rows(n, k):
                nc.scalar.copy(xh[:, k, :], x1f[:, k, :]).then_inc(s_xh, 1)

            act.dma_start(wk_n[:, :], wk_w).then_inc(s_wload, 16)
            act.dma_start(rk[:, :], rot_k).then_inc(s_wload, 16)
            act.dma_start(bk_n[:, :], wk_b.rearrange("(p a) -> p a", a=1)).then_inc(s_wload, 16)
            act.dma_start(gw_n[:, :], gate_w).then_inc(s_wload1, 16)
            act.dma_start(bv_b[:, :], wv_b.partition_broadcast(P)).then_inc(s_wload1, 16)
            def run(item):
                kind = item[0]
                if kind in T_KINDS:
                    ps = psB[:, 1, :] if item in LATE else psT[:, (T_NO[item] - 1) % 3, :]
                if kind == "st":
                    _, k, n, h = item
                    c0 = exp_steps(HEADGROUPS[k][1])[n][1]
                    step = PV_NO[("pv", k, n)] - 1
                    if h == 0 and step >= NPROB:
                        act.wait_ge(s_pv, step - NPROB + 1)
                    act.wait_ge(s_T, T_NO[item])
                    nc.scalar.activation(prob[:, step % NPROB, h, 0:HALF - c0], ps[:, 0:HALF - c0], ACT.Exp).then_inc(s_Tfree, 1)
                elif kind == "evac":
                    k = item[1]
                    if k >= 2:
                        act.wait_ge(s_S, S_NO[("norm", k - 2)])
                    act.wait_ge(s_pv, PV_NO[("pv", k, len(exp_steps(HEADGROUPS[k][1])) - 1)])
                    nc.scalar.copy(O[:, k % 2, :], psO[:, :]).then_inc(s_evac, 1)
                elif kind == "wT":
                    act.wait_ge(s_T, T_NO[item])
                    if item[1] == 0:
                        nc.scalar.copy(wqT[:, :, :], ps.rearrange("p (k o) -> p k o", k=KC)).then_inc(s_Tfree, 1)
                    elif item[1] == 1:
                        o = KC * KVW
                        nc.scalar.copy(wkT[:, :, :], ps[:, 0:o].rearrange("p (k o) -> p k o", k=KC)).then_inc(s_bias, 1)
                        nc.scalar.copy(bq[:, :], ps[:, o:o + KC]).then_inc(s_bias, 1)
                        nc.scalar.copy(bk[:, :], ps[0:KVW, o + KC:o + KC + 1]).then_inc(s_Tfree, 1)
                        act.wait_ge(s_Tfree, T_NO[item])
                    elif item[1] == 2:
                        o = KC * KVW
                        nc.scalar.copy(wvT[:, :, :], ps[:, 0:o].rearrange("p (k o) -> p k o", k=KC)).then_inc(s_bias, 1)
                        nc.scalar.copy(gwT[:, :, :], ps[:, o:o + KC * NE].rearrange("p (k o) -> p k o", k=KC)).then_inc(s_Tfree, 1)
                    else:
                        nc.scalar.copy(cpT[:, :, :], ps.rearrange("p (k o) -> p k o", k=KC)).then_inc(s_Tfree, 1)
                elif kind == "xT":
                    _, b, k, half = item
                    if b and (k, half) == (0, 0):
                        act.wait_ge(s_S, max(S_NO[("v", b - 1)], S_NO[("proj", b - 1, KC, 1)]))
                    act.wait_ge(s_T, T_NO[item])
                    nc.scalar.copy(xT[:, k, half * HALF:(half + 1) * HALF], ps).then_inc(s_Tfree, 1)
                elif kind == "proj":
                    _, b, m, half = item
                    rows = KVW if m == 0 else P
                    part = (kp if m == 0 else qp[:, m - 1, :, :])[:, :, half * HALF:(half + 1) * HALF]
                    bias = bk[:, 0:1] if m == 0 else bq[:, m - 1:m]
                    if PROJ_NO[item] == 1:
                        act.wait_ge(s_bias, 2)
                    if b:
                        act.wait_ge(s_kload[b - 1][half], 16 * len(PAIRS))
                        for s in (2 * half, 2 * half + 1):
                            act.wait_ge(s_qload[s % NSLOT], 16 * len(PAIRS) * (s // NSLOT + 1))
                    act.wait_ge(s_S, S_NO[item])
                    nc.scalar.activation(part[:, 0, :], psS[0:rows, (S_NO[item] - 1) % 2, 0:HALF], ACT.Identity,
                                         bias=bias).then_inc(s_part1, 1)
                elif kind == "split":
                    _, b, m, half = item
                    n = PROJ_NO[("proj", b, m, half)] - 1
                    rows = KVW if m == 0 else P
                    part = (kp if m == 0 else qp[:, m - 1, :, :])[:, :, half * HALF:(half + 1) * HALF]
                    act.wait_ge(s_Sfree, S_NO[("proj", b, m, half)])
                    nc.scalar.copy(part[:, 1, :], rest[0:rows, n % NREST, :]).then_inc(s_part2, 1)
                elif kind == "yT":
                    act.wait_ge(s_T, T_NO[item])
                    nc.scalar.copy(yT[:, item[2] % 2, :, :], ps[:, 0:C].rearrange("p (k t) -> p k t", k=KC)).then_inc(s_Tfree, 1)
                elif kind == "x1T":
                    _, b, i = item
                    if b and i % TH == 0:
                        act.wait_ge(s_x1tst[i // TH], 16 * b)
                    act.wait_ge(s_T, T_NO[item])
                    nc.scalar.copy(x1T[i // TH][:, :, (i % TH) * P:(i % TH + 1) * P],
                                   ps[:, 0:C].rearrange("p (k t) -> p k t", k=KC)).then_inc(s_Tfree, 1)
                elif kind == "route":
                    _, b, q = item
                    act.wait_ge(s_Sfree, S_NO[("gate", b, q)])
                    nc.scalar.activation(th[:, :, :], lg[:, :, :], ACT.Tanh, scale=0.5).then_inc(s_th, 1)
                elif kind == "pT":
                    _, b, q = item
                    t0 = b * T + q * HALF
                    act.wait_ge(s_T, T_NO[item])
                    nc.scalar.copy(probT[:, t0:t0 + HALF], ps[0:PROBROWS, :].bitcast(BF16)[:, 0:HALF]).then_inc(s_Tfree, 1)
                elif kind == "begin":
                    act.wait_ge(s_pv, len(PV_NO))
                elif kind == "wsplit":
                    high_weights(item[1])
                elif kind == "xsplit":
                    act.wait_ge(s_x1f, 16)
                    high_rows(0, item[1])


            for item in SEQ:
                run(item)
            def high_gated(count_, q):
                rows = LAST if q == NCH - 1 else P
                act.wait_ge(s_g, count_ + 2)
                act.wait_ge(s_down, count_)
                nc.scalar.copy(gh[0:rows, q % NSL, :], za[0:rows, q % NSL, :]).then_inc(s_gh, 1)

            def sums(n):
                act.wait_ge(s_down, n * NCH + NSL)
                for k in range(KC):
                    nc.scalar.copy(yS[:, k, :], psY[:, k, :]).then_inc(s_yS, 1)

            opened = []

            def turn(n, first):
                for q in range(NCH):
                    if first:
                        for e in chunk_units(q):
                            if WUNITS[e][0] == "down" and WUNITS[e][1] == 0:
                                act.wait_ge(s_x1tst[0], 16 * B)
                            if under(e) and not opened:
                                opened.append(e)
                                act.wait_ge(s_Sfree, len(S_NO))
                                act.wait_ge(s_x1tst[1], 16 * B)
                                for i in range(3):
                                    act.wait_ge(s_x1st[i], 16 * ((B * TT - i + 2) // 3))
                            high_weights(e)
                    if q == 2 and not first:
                        sums(n)
                    rows = LAST if q == NCH - 1 else P
                    act.wait_ge(s_h, at(n, NCH, q + 1))
                    act.wait_ge(s_gl, at(n, NCH, q + 1))
                    nc.scalar.copy(za[0:rows, q % NSL, :], psH[0:rows, q % 2, 0, :]).then_inc(s_copy, 1)
                    if first:
                        for item in late(q, 0):
                            run(item)
                    if q == NCH - 1:
                        act.wait_ge(s_x1f, at(n, 16, 32))
                        for k in range(KC):
                            high_rows(n, k)
                    if q or not first:
                        high_gated(at(n, NCH, q), (q - 1) % NCH)
                    if q < NCR:
                        act.wait_ge(s_z, at(n, NCR, q + 1))
                    else:
                        act.wait_ge(s_copy, at(n, NCH, q + 1))
                    nc.scalar.activation(ta[0:rows, q % NSL, :], za[0:rows, q % NSL, :], ACT.Tanh, scale=0.5).then_inc(s_tanh, 1)
                    if first:
                        for item in late(q, 1):
                            run(item)

            turn(0, True)
            with act.Fori(1, GROUPS) as n:
                turn(n, False)
            high_gated(GROUPS * NCH, NCH - 1)
            act.wait_ge(s_down, GROUPS * NCH + NSL)
            for m in range(2):
                for k in range(KC):
                    t = slice(m * HALF // 2, (m + 1) * HALF // 2)
                    nc.scalar.copy(yS[:, k, t], psY[:, k, t]).then_inc(s_yS, 1)

        @block.vector
        def _(dve):
            chain = [0]

            def link(ins):
                chain[0] += 1
                ins.then_inc(s_dve, 1)
                dve.wait_ge(s_dve, chain[0])

            def low_rows(k, n):
                dve.wait_ge(s_xh, n)
                nc.vector.tensor_tensor(xl[:, k, :], x1f[:, k, :], xh[:, k, :].bitcast(F32), ALU.subtract).then_inc(s_xl, 1)

            for b in range(B):
                nc.vector.memset(KS[:, b, :, :], 1.0).then_inc(s_ones, 1)
                link(nc.vector.memset(V[:, b, :, :, HD:2 * HD], 1.0))
            dve.wait_ge(s_wload2, 16 * WLOADS2)
            link(nc.vector.tensor_scalar(gb_b[:, :], gb_b[:, :], 0.5, None, ALU.add))
            def run(item):
                kind = item[0]
                if kind in S_KINDS:
                    dve.wait_ge(s_S, S_NO[item])
                    ps = psB[:, 1, :] if item in LATE else psS[:, (S_NO[item] - 1) % 2, :]
                if item == ("v", 0):
                    dve.wait_ge(s_wload1, 16 * WLOADS1)
                if kind == "proj":
                    _, b, m, half = item
                    n = PROJ_NO[item] - 1
                    rows = KVW if m == 0 else P
                    part = (kp if m == 0 else qp[:, m - 1, :, :])[:, :, half * HALF:(half + 1) * HALF]
                    bias = bk[:, 0:1] if m == 0 else bq[:, m - 1:m]
                    dve.wait_ge(s_part1, n + 1)
                    if n >= NREST:
                        dve.wait_ge(s_part3, n - NREST + 1)
                    nc.vector.scalar_tensor_tensor(out=rest[0:rows, n % NREST, :], in0=ps[0:rows, 0:HALF], scalar=bias,
                                                   in1=part[:, 0, :], op0=ALU.add, op1=ALU.subtract).then_inc(s_Sfree, 1)
                elif kind == "v":
                    b = item[1]
                    nc.vector.tensor_tensor(V[:, b, :, :, 0:HD], ps[:, 0:HALF].rearrange("p (i v d) -> p i v d", i=TT, v=NKV),
                                            bv_b[:, :].rearrange("p (v d) -> p v d", v=NKV).unsqueeze(1)
                                            .to_broadcast([P, TT, NKV, HD]), ALU.add).then_inc(s_Sfree, 1)
                elif kind == "smax":
                    _, k, n = item
                    q = HEADGROUPS[k][1]
                    i, heads, cols, dist = max_units(q)[n]
                    if n == 0 and k:
                        dve.wait_ge(s_m2, k)
                    src = ps[:, 0:len(heads) * dist].rearrange("p (h n) -> p h n", h=len(heads))[:, :, 0:cols]
                    nc.vector.tensor_reduce(out=MX[:, heads[0]:heads[-1] + 1, i - TH * q], in_=src, op=ALU.max,
                                            axis=AX_X).then_inc(s_Sfree, 1)
                    if n == len(max_units(q)) - 1:
                        dve.wait_ge(s_Sfree, S_NO[item])
                        mx = MX[:, :, :].rearrange("p h i -> p (h i)")
                        link(nc.vector.tensor_scalar(M2[:, 0, :], mx, -1.0, None, ALU.mult))
                        nc.vector.scalar_tensor_tensor(out=M2[:, 1, :], in0=mx, scalar=-1.0, in1=M2[:, 0, :],
                                                       op0=ALU.mult, op1=ALU.subtract).then_inc(s_m2, 1)
                elif kind == "mrow":
                    k = item[1]
                    if k:
                        dve.wait_ge(s_mrow, 16 * k)
                    nc.vector.tensor_copy(MT[:, :], ps[0:MROWS * G * TH, :].bitcast(BF16)[:, 0:P]).then_inc(s_Sfree, 1)
                elif kind == "norm":
                    k = item[1]
                    b, q, g = HEADGROUPS[k]
                    if g == 0 and k >= 2 * NKV:
                        dve.wait_ge(s_T, T_NO[("yT", b - 1, q * TH + TH - 1)])
                    if k:
                        dve.wait_ge(s_Sfree, S_NO[("norm", k - 1)])
                    ps = ps[:, 0:HALF].rearrange("p (i h w) -> p i h w", i=TH, h=G)
                    rc4 = rc[:, :].rearrange("p (i h a) -> p i h a", i=TH, a=1)
                    link(nc.vector.reciprocal(rc4, ps[:, :, :, HD:HD + 1]))
                    nc.vector.tensor_tensor(y[q][:, :, g * KVW:(g + 1) * KVW].rearrange("p i (h d) -> p i h d", h=G),
                                            ps[:, :, :, 0:HD], rc4.to_broadcast([P, TH, G, HD]), ALU.mult).then_inc(s_Sfree, 1)
                elif kind == "cp":
                    _, b, i = item
                    n = CP_NO[item] - 1
                    if n >= 3:
                        dve.wait_ge(s_x1, n - 2)
                    dve.wait_ge(s_res, b * TT + i + 1)
                    nc.vector.tensor_tensor(r[:, n % 3, :], ps[:, 0:C], xn[b][:, i, :], ALU.add).then_inc(s_Sfree, 1)
                    dve.wait_ge(s_Sfree, S_NO[item])
                    link(nc.vector.bn_stats(st1[:, :], r[:, n % 3, :]))
                    link(nc.vector.bn_aggr(mv1[:, n % 3, :], st1[:, :]))
                    nc.vector.tensor_scalar(ve1[:, n % 3, :], mv1[:, n % 3, 1:2], EPS, None, ALU.add).then_inc(s_var, 1)
                elif kind == "ln":
                    _, b, i = item
                    n = LN_NO[item] - 1
                    dve.wait_ge(s_rstd, n + 1)
                    if n >= 3:
                        prev = [it for it in SEQ + LATE if it[0] == "x1T"][n - 3]
                        dve.wait_ge(s_T, T_NO[prev])
                        dve.wait_ge(s_x1st[n % 3], 16 * (n // 3))
                    nc.vector.tensor_scalar(x1[:, n % 3, :], r[:, n % 3, :], mv1[:, n % 3, 0:1], rs1[:, n % 3, 0:1],
                                            ALU.subtract, ALU.mult).then_inc(s_x1, 1)
                elif kind == "gate":
                    nc.vector.tensor_copy(lg[:, :, :], ps[:, 0:TH * NE].rearrange("p (i e) -> p i e", i=TH)).then_inc(s_Sfree, 1)
                elif kind == "route":
                    _, b, q = item
                    h = b * NHALF + q
                    dve.wait_ge(s_th, h + 1)
                    if h:
                        dve.wait_ge(s_pr3, h)
                    link(nc.vector.scalar_tensor_tensor(
                        out=sc[:, :, :], in0=th[:, :, :], scalar=0.5,
                        in1=gb_b[:, :].unsqueeze(1).to_broadcast([P, TH, NE]), op0=ALU.mult, op1=ALU.add))
                    for i in range(TH):
                        last = nc.vector.max(out=top[:, i, :], in_=sc[:, i, :])
                    link(last)
                    for i in range(TH):
                        last = nc.vector.max_index(out=idx[:, i, :], in_max=top[:, i, :], in_values=sc[:, i, :])
                    link(last)
                    link(nc.vector.tensor_copy(idf[:, :, :], idx[:, :, :]))
                    link(nc.vector.tensor_tensor(
                        hit[:, :, :, :], iota_b[:, :].unsqueeze(1).unsqueeze(3).to_broadcast([P, TH, NE, TOPK]),
                        idf[:, :, 0:TOPK].unsqueeze(2).to_broadcast([P, TH, NE, TOPK]), ALU.is_equal))
                    link(nc.vector.tensor_reduce(out=pick[:, :, :], in_=hit[:, :, :, :], op=ALU.add, axis=AX_X))
                    link(nc.vector.tensor_reduce(out=tsum[:, :, 0], in_=top[:, :, 0:TOPK], op=ALU.add, axis=AX_X))
                    link(nc.vector.reciprocal(trec[:, :, :], tsum[:, :, :]))
                    link(nc.vector.tensor_tensor(prt[:, :, :], pick[:, :, :], sc[:, :, :], ALU.mult))
                    link(nc.vector.scalar_tensor_tensor(out=prt[:, :, :], in0=prt[:, :, :], scalar=0.5,
                                                        in1=trec[:, :, :].to_broadcast([P, TH, NE]),
                                                        op0=ALU.mult, op1=ALU.mult))
                    if h:
                        prev = ("pT", b, 0) if q else ("pT", b - 1, 1)
                        dve.wait_ge(s_T, T_NO[prev])
                    for k in range(3):
                        part = pr3[:, :, k * NE:(k + 1) * NE]
                        cp = nc.vector.tensor_copy(part, prt[:, :, :])
                        if k == 2:
                            cp.then_inc(s_pr3, 1)
                            break
                        link(cp)
                        link(nc.vector.tensor_tensor(prt[:, :, :], prt[:, :, :], part, ALU.subtract))
                elif kind == "begin":
                    dve.sem_inc(s_g, 2)
                elif kind == "xsplit":
                    low_rows(item[1], item[1] + 1)


            for item in SEQ:
                run(item)
            def residual(n, m):
                dve.wait_ge(s_x1r, n * 16)
                dve.wait_ge(s_back, n * 2 - 1 + m)
                nc.vector.tensor_tensor(x1r[:, 2 * m:2 * m + 2, :], psB[:, 1 - m, :].rearrange("p (i c) -> p i c", i=2),
                                        x1r[:, 2 * m:2 * m + 2, :], ALU.add).then_inc(s_resid, 1)

            def statistics(n):
                dve.wait_ge(s_resid, n * 2)
                for i in range(TH):
                    nc.vector.bn_stats(st2[:, i, :], x1r[:, i, :]).then_inc(s_st2, 1)

            def variances(n):
                dve.wait_ge(s_st2, n * 2 * TH - TH)
                dve.sem_inc(s_pass, 1)
                for i in range(TH):
                    nc.vector.bn_aggr(mv2[:, i, :], st2[:, i, :]).then_inc(s_st2, 1)
                dve.wait_ge(s_st2, n * 2 * TH)
                nc.vector.tensor_scalar(ve2[:, :], mv2[:, :, 1], EPS, None, ALU.add).then_inc(s_var2, 1)

            def normalise(n):
                dve.wait_ge(s_rstd2, n * 1)
                for i in range(TH):
                    nc.vector.tensor_scalar(x1r[:, i, :], x1r[:, i, :], mv2[:, i, 0:1], rs2[:, i:i + 1],
                                            ALU.subtract, ALU.mult).then_inc(s_norm2, 1)

            def turn(n, first):
                for q in range(NCH):
                    rows = LAST if q == NCH - 1 else P
                    a, t = za[0:rows, q % NSL, :], ta[0:rows, q % NSL, :]
                    h2 = psH[0:rows, q % 2, 1, :]
                    if q < NCR:
                        dve.wait_ge(s_copy, at(n, NCH, q + 1))
                        nc.vector.tensor_tensor(a, a, h2, ALU.mult).then_inc(s_z, 1)
                    if first:
                        for item in late(q, 0):
                            run(item)
                    if q == NCH - 1:
                        for k in range(KC):
                            low_rows(k, at(n, KC, KC + k + 1))
                    if not first:
                        if q == 5:
                            residual(n, 0)
                        if q == 6:
                            statistics(n)
                        if q == 7:
                            variances(n)
                        if q == 8:
                            normalise(n)
                    dve.wait_ge(s_tanh, at(n, NCH, q + 1))
                    nc.vector.scalar_tensor_tensor(out=t, in0=t, scalar=1.0, in1=a, op0=ALU.add, op1=ALU.mult).then_inc(s_w, 1)
                    if q == 5 and not first:
                        residual(n, 1)
                    dve.wait_ge(s_w, at(n, NCH, q + 1))
                    if q < NCR:
                        dve.wait_ge(s_b, at(n, NCR, q + 1))
                        nc.vector.tensor_tensor(a, t, psB[:, 0 if first else q % 2, :], ALU.mult).then_inc(s_g, 1)
                    else:
                        nc.vector.scalar_tensor_tensor(out=a, in0=h2, scalar=0.5, in1=t, op0=ALU.mult, op1=ALU.mult).then_inc(s_g, 1)
                    if first:
                        for item in late(q, 1):
                            run(item)

            turn(0, True)
            with dve.Fori(1, GROUPS) as n:
                turn(n, False)
            base = (GROUPS - 1) * 2 * TH
            for m in range(2):
                residual(GROUPS, m)
                dve.wait_ge(s_resid, 2 * GROUPS - 1 + m)
                tiles = range(2 * m, 2 * m + 2)
                for i in tiles:
                    nc.vector.bn_stats(st2[:, i, :], x1r[:, i, :]).then_inc(s_st2, 1)
                dve.wait_ge(s_st2, base + 4 * m + 2)
                for i in tiles:
                    nc.vector.bn_aggr(mv2[:, i, :], st2[:, i, :]).then_inc(s_st2, 1)
                dve.wait_ge(s_st2, base + 4 * m + 4)
                nc.vector.tensor_scalar(ve2[:, 2 * m:2 * m + 2], mv2[:, 2 * m:2 * m + 2, 1], EPS, None, ALU.add).then_inc(s_var2, 1)
            for m in range(2):
                dve.wait_ge(s_rstd2, GROUPS + m)
                for i in range(2 * m, 2 * m + 2):
                    nc.vector.tensor_scalar(x1r[:, i, :], x1r[:, i, :], mv2[:, i, 0:1], rs2[:, i:i + 1],
                                            ALU.subtract, ALU.mult).then_inc(s_norm2, 1)

        @block.tensor
        def _(pe):
            mm = nc.tensor.matmul

            def weights_back(ps):
                for i in range(TH):
                    last = nc.tensor.transpose(ps.bitcast(BF16)[0:PROBROWS, i * P:(i + 1) * P], pr3[:, i, :], ident_b[:, :])
                last.then_inc(s_T, 1)

            pe.wait_ge(s_const, 7)
            def run(item):
                kind = item[0]
                if item in LATE and kind in S_KINDS + T_KINDS:
                    ps = psB[:, 1, :]
                    units = [i for i in LATE if i[0] in S_KINDS + T_KINDS]
                    if item != units[0]:
                        prev = units[units.index(item) - 1]
                        if prev[0] in S_KINDS:
                            pe.wait_ge(s_Sfree, S_NO[prev])
                        else:
                            pe.wait_ge(s_Tfree, T_NO[prev])
                elif kind in S_KINDS:
                    if S_NO[item] > 2:
                        pe.wait_ge(s_Sfree, S_NO[item] - 2)
                    ps = psS[:, (S_NO[item] - 1) % 2, :]
                elif kind in T_KINDS:
                    if T_NO[item] > 3:
                        pe.wait_ge(s_Tfree, T_NO[item] - 3)
                    ps = psT[:, (T_NO[item] - 1) % 3, :]
                if kind == "st":
                    _, k, n, h = item
                    b, q, g = HEADGROUPS[k]
                    j, c0, diag = exp_steps(q)[n]
                    if (n, h) == (0, 0):
                        pe.wait_ge(s_mrow, 16 * (k + 1))
                    mm(ps[:, 0:HALF - c0], KS[:, b, g, j * P:(j + 1) * P],
                       QS[:, (k // 2) % NSLOT, g % 2 * G + h, c0:HALF], start=True, stop=True).then_inc(s_T, 1)
                elif kind == "pv":
                    _, k, n = item
                    b, q, g = HEADGROUPS[k]
                    j, c0, diag = exp_steps(q)[n]
                    if n == 0 and k:
                        pe.wait_ge(s_evac, k)
                    st = ("st", k, n, G - 1)
                    if diag:
                        pe.wait_ge(s_sel, SEL_NO[st])
                    else:
                        pe.wait_ge(s_Tfree, T_NO[st])
                    for h in range(G):
                        last = mm(psO[32 * h:32 * h + 32, c0:HALF], V[:, b, j, g, :],
                                  prob[:, (PV_NO[item] - 1) % NPROB, h, 0:HALF - c0],
                                  start=(n == 0), stop=(n == len(exp_steps(q)) - 1))
                    last.then_inc(s_pv, 1)
                elif kind == "smax":
                    _, k, n = item
                    b, q, g = HEADGROUPS[k]
                    i, heads, cols, dist = max_units(q)[n]
                    if n == 0:
                        s = k // 2
                        pe.wait_ge(s_kload[b][q], 16 * len(PAIRS))
                        pe.wait_ge(s_qload[s % NSLOT], 16 * len(PAIRS) * (s // NSLOT + 1))
                    for e, h in enumerate(heads):
                        for c in range(0, cols, HALF):
                            w = min(HALF, cols - c)
                            mm(ps[:, e * dist + c:e * dist + c + w],
                               QS[0:ROWS, (k // 2) % NSLOT, g % 2 * G + h, (i - TH * q) * P:(i - TH * q + 1) * P],
                               KS[0:ROWS, b, g, c:c + w], start=True, stop=(c + w < cols))
                        d = e * dist + i * P
                        last = mm(ps[:, d:d + P], ident_b[:, :], mask_b[:, :], start=False, stop=True)
                    last.then_inc(s_S, 1)
                elif kind == "mrow":
                    pe.wait_ge(s_m2, item[1] + 1)
                    nc.tensor.transpose(ps[0:MROWS * G * TH, :].bitcast(BF16)[:, 0:P], M2[:, :, :].rearrange("p s r -> p (s r)"),
                                        ident_b[:, :]).then_inc(s_S, 1)
                elif kind == "norm":
                    k = item[1]
                    pe.wait_ge(s_evac, k + 1)
                    for i in range(TH):
                        last = nc.tensor.transpose(ps[:, i * P:(i + 1) * P], O[:, k % 2, i * P:(i + 1) * P], ident[:, :])
                    last.then_inc(s_S, 1)
                elif kind == "wT":
                    o = KC * KVW
                    if item[1] == 0:
                        pe.wait_ge(s_wload, 16 * WLOADS)
                        for k in range(KC):
                            for m in range(KC):
                                last = mm(ps[:, k * C + m * P:k * C + (m + 1) * P], wq_n[:, m, k * P:(k + 1) * P],
                                          rq[:, m, :], start=True, stop=True)
                    elif item[1] == 1:
                        for k in range(KC):
                            mm(ps[:, k * KVW:(k + 1) * KVW], wk_n[:, k * P:(k + 1) * P], rk[:, :], start=True, stop=True)
                        for m in range(KC):
                            mm(ps[:, o + m:o + m + 1], rq[:, m, :], bq_n[:, m:m + 1], start=True, stop=True)
                        last = mm(ps[0:KVW, o + KC:o + KC + 1], rk[:, :], bk_n[:, :], start=True, stop=True)
                    elif item[1] == 2:
                        pe.wait_ge(s_wload1, 16 * WLOADS1)
                        for k in range(KC):
                            nc.tensor.transpose(ps[:, k * KVW:(k + 1) * KVW], wv_n[:, k * P:(k + 1) * P], ident[0:KVW, 0:KVW])
                            last = nc.tensor.transpose(ps[:, o + k * NE:o + (k + 1) * NE], gw_n[:, k * P:(k + 1) * P],
                                                       ident[0:NE, 0:NE])
                    else:
                        pe.wait_ge(s_wload2, 16 * WLOADS2)
                        for k in range(KC):
                            for m in range(KC):
                                last = nc.tensor.transpose(ps[:, k * C + m * P:k * C + (m + 1) * P],
                                                           cp_n[:, m, k * P:(k + 1) * P], ident[:, :])
                    last.then_inc(s_T, 1)
                elif kind == "xT":
                    _, b, k, half = item
                    pe.wait_ge(s_x[b][half], 16)
                    for i in range(TH):
                        last = nc.tensor.transpose(ps[:, i * P:(i + 1) * P], xn[b][:, half * TH + i, k * P:(k + 1) * P], ident[:, :])
                    last.then_inc(s_T, 1)
                elif kind == "proj":
                    _, b, m, half = item
                    rows = KVW if m == 0 else P
                    wT = wkT if m == 0 else wqT[:, :, (m - 1) * P:m * P]
                    pe.wait_ge(s_Tfree, T_NO[("xT", b, KC - 1, half)])
                    for k in range(KC):
                        last = mm(ps[0:rows, 0:HALF], wT[:, k, :],
                                  xT[:, k, half * HALF:(half + 1) * HALF], start=(k == 0), stop=(k == KC - 1))
                    last.then_inc(s_S, 1)
                elif kind == "v":
                    pe.wait_ge(s_Tfree, T_NO[("xT", item[1], KC - 1, NHALF - 1)])
                    if item[1] == 0:
                        pe.wait_ge(s_Tfree, T_NO[("wT", 2)])
                    for i in range(TT):
                        for k in range(KC):
                            last = mm(ps[:, i * KVW:(i + 1) * KVW], xT[:, k, i * P:(i + 1) * P], wvT[:, k, :],
                                      start=(k == 0), stop=(k == KC - 1))
                    last.then_inc(s_S, 1)
                elif kind == "yT":
                    _, b, i = item
                    k = (b * NHALF + i // TH) * NKV + NKV - 1
                    pe.wait_ge(s_Sfree, S_NO[("norm", k)])
                    for k in range(KC):
                        last = nc.tensor.transpose(ps[:, k * P:(k + 1) * P], y[i // TH][:, i % TH, k * P:(k + 1) * P], ident[:, :])
                    last.then_inc(s_T, 1)
                elif kind == "cp":
                    _, b, i = item
                    pe.wait_ge(s_Tfree, max(T_NO[("yT", b, i)], T_NO[("wT", 3)]))
                    for k in range(KC):
                        last = mm(ps[:, 0:C], yT[:, i % 2, k, :], cpT[:, k, :], start=(k == 0), stop=(k == KC - 1))
                    last.then_inc(s_S, 1)
                elif kind == "x1T":
                    _, b, i = item
                    n = LN_NO[("ln", b, i)] - 1
                    pe.wait_ge(s_x1, n + 1)
                    for k in range(KC):
                        last = nc.tensor.transpose(ps[:, k * P:(k + 1) * P], x1[:, n % 3, k * P:(k + 1) * P], ident[:, :])
                    last.then_inc(s_T, 1)
                elif kind == "gate":
                    _, b, q = item
                    pe.wait_ge(s_Tfree, T_NO[("x1T", b, q * TH + TH - 1)])
                    for i in range(TH):
                        for k in range(KC):
                            last = mm(ps[:, i * NE:(i + 1) * NE], x1T[q][:, k, i * P:(i + 1) * P], gwT[:, k, :],
                                      start=(k == 0), stop=(k == KC - 1))
                    last.then_inc(s_S, 1)
                elif kind == "pT":
                    _, b, q = item
                    pe.wait_ge(s_pr3, b * NHALF + q + 1)
                    weights_back(ps)

            for item in SEQ:
                run(item)
            pe.wait_ge(s_Sfree, BEFORE_LATE["S"])
            pe.wait_ge(s_Tfree, BEFORE_LATE["T"])
            pe.sem_inc(s_down, NSL)
            pe.wait_ge(s_selw, 16)

            def up(n, q, first):
                rows = LAST if q == NCH - 1 else P
                cols = slice(q * P, q * P + rows)
                if first:
                    pe.wait_ge(s_wlo, needs("up", q))
                pe.wait_ge(s_g, at(n, NCH, q + 1))
                for w in range(2):
                    for k in range(KC):
                        if q == 0 and w == 0:
                            pe.wait_ge(s_xl, at(n, KC, k + 1))
                        for e, (a, x_) in enumerate(((wuh, xh), (wuh, xl), (wul, xh))):
                            last = mm(psH[0:rows, q % 2, w, :], a[:, w, k, cols], x_[:, k, :],
                                      start=(k == 0 and e == 0), stop=(k == KC - 1 and e == 2))
                last.then_inc(s_h, 1)

            def down(n, q, first):
                rows = LAST if q == NCH - 1 else P
                if first:
                    pe.wait_ge(s_wlo, needs("down", q))
                pe.wait_ge(s_gl, at(n, NCH, NSL + q + 1))
                for k in range(KC):
                    for e, (a, g_) in enumerate(((0, gh), (0, gl), (1, gh))):
                        last = mm(psY[:, k, :], wd[0:rows, q, a, k * P:(k + 1) * P], g_[0:rows, q % NSL, :],
                                  start=(q == 0 and e == 0), stop=(q == NCH - 1 and e == 2))
                last.then_inc(s_down, 1)

            def back(n, m):
                for e in range(2):
                    for k in range(KC):
                        i = 2 * m + e
                        last = nc.tensor.transpose(psB[:, 1 - m, e * C + k * P:e * C + (k + 1) * P],
                                                   yS[:, k, i * P:(i + 1) * P], ident[:, :])
                last.then_inc(s_back, 1)

            def turn(n, first):
                for q in range(NCH):
                    up(n, q, first)
                    if first:
                        for item in late(q, 0):
                            run(item)
                    if q == 5 and not first:
                        pe.wait_ge(s_yS, at(n, KC, 0))
                        back(n, 0)
                    if q >= DLAG:
                        if q == DLAG and not first:
                            pe.wait_ge(s_yS, at(n, KC, 0))
                        down(n, q - DLAG, first)
                    elif not first:
                        down(n - 1, NCH - DLAG + q, False)
                    if q == 5 and not first:
                        pe.wait_ge(s_g, at(n, NCH, 2 + q))
                        back(n, 1)
                    if first:
                        for item in late(q, 1):
                            run(item)
                        if 0 < q < NCR:
                            pe.wait_ge(s_g, 2 + q)
                    if q < NCR:
                        if q in (5, 6) and not first:
                            pe.wait_ge(s_resid, at(n, 2, -2 + q - 4))
                            pe.sem_inc(s_pass, 1)
                        mm(psB[:, 0 if first else q % 2, :], sel[:, q, :], probT[:, bass.ds(n * HALF, HALF)],
                           start=True, stop=True).then_inc(s_b, 1)

            turn(0, True)
            with pe.Fori(1, GROUPS) as n:
                turn(n, False)
            for q in range(NCH - DLAG, NCH):
                down(GROUPS - 1, q, False)
            for m in range(2):
                pe.wait_ge(s_yS, (GROUPS - 1 + m) * KC + KC)
                back(GROUPS, m)


_INS = ['L0_attn_x', 'L0_attn_wq_w', 'L0_attn_wq_b', 'L0_attn_wk_w', 'L0_attn_wk_b', 'L0_attn_wv_w', 'L0_attn_wv_b',
        'L0_attn_cp_w', 'L0_attn_cp_b', 'L0_ffn_gate_w', 'L0_ffn_gate_b', 'L0_ffn_w1_shared', 'L0_ffn_w2_shared',
        'L0_ffn_w3_shared', 'L0_ffn_w1_routed', 'L0_ffn_w2_routed', 'L0_ffn_w3_routed']


def shape_constants():
    half = HD // 2
    theta = 1.0 / 10000.0 ** (np.arange(half, dtype=np.float32) * 2.0 / HD)

    def rotation(heads, per, scale):
        out = np.zeros((heads * HD, per * HD), np.float32)
        for h in range(heads):
            for i in range(half):
                c, s = scale * np.cos(h * theta[i]), scale * np.sin(h * theta[i])
                even, odd = h * HD + 2 * i, h * HD + 2 * i + 1
                to_even, to_odd = 2 * i * per + h % per, (2 * i + 1) * per + h % per
                out[even, to_even], out[odd, to_even] = c, -s
                out[odd, to_odd], out[even, to_odd] = c, s
        return out

    owner = (np.arange(NCR * P) // HID)[None, :] == (np.arange(PROBROWS) % NE)[:, None]
    bf16_one = np.where(owner, 0x3F80, 0).astype(np.uint16)
    return [("rot_q", rotation(NH, 8, HD ** -0.5)), ("rot_k", rotation(NKV, NKV, 1.0)),
            ("expert_of", bf16_one), ("iota_e", np.arange(NE, dtype=np.float32))]


def kernel(**inputs):
    import numpy as _np
    import concourse.bacc as _bacc
    from concourse import mybir as _mybir
    from concourse.bass_utils import run_bass_kernel_spmd as _run

    nc = _bacc.Bacc("TRN2", target_bir_lowering=False, num_devices=1)
    arrays, args = {}, []
    for name, a in [(n, _np.ascontiguousarray(inputs[n])) for n in _INS] + shape_constants():
        if name == 'L0_attn_x':
            a = a.reshape(B * T, C)
        arrays[f"in_{name}_dram"] = a
        args.append(nc.dram_tensor(f"in_{name}_dram", a.shape, _mybir.dt.from_np(a.dtype), kind="ExternalInput").ap())
    args.append(nc.dram_tensor("out_0_dram", (B * T, C), _mybir.dt.float32, kind="ExternalOutput").ap())
    attention_moe(nc, *args)
    r = _run(nc, [arrays], core_ids=[0])
    return r.results[0]["out_0_dram"].reshape(B, T, C)
```
